# Optimizing a Trainium2 kernel written in Bass

```python
import numpy as np
import jax
import jax.numpy as jnp

def _softmax(x, axis=-1):
    return jax.nn.softmax(x, axis=axis)

def _gelu(x):
    return jax.nn.gelu(x, approximate=True)

def _silu(x):
    return jax.nn.silu(x)

def _sigmoid(x):
    return jax.nn.sigmoid(x)

def _layernorm(x, axis=-1, eps=1e-05):
    m = jnp.mean(x, axis=axis, keepdims=True)
    v = jnp.var(x, axis=axis, keepdims=True)
    return (x - m) / jnp.sqrt(v + eps)

def _scatter_add(tgt, idx, src, axis=0):
    return tgt.at[idx].add(src)

def _segment_sum(src, seg, n):
    return jax.ops.segment_sum(src, seg, n)
kernel_name = 'mk_gps_d1_gnn_r16_dc8996'

def setup_inputs(seed: int=0):
    np.random.seed(seed)
    _w = jnp.asarray

    def _rec_inputs():
        import jax
        import jax.numpy as jnp
        _gk = jax.random.key(seed)
        x = -0.0002117 + 1 * jax.random.normal(jax.random.fold_in(_gk, 1), (6250, 256), jnp.float32)
        src = jax.random.randint(jax.random.fold_in(_gk, 2), (100000,), 0, 6250, jnp.int32)
        dst = jax.random.randint(jax.random.fold_in(_gk, 3), (100000,), 0, 6250, jnp.int32)
        _o = jnp.argsort(dst, stable=True)
        src = src[_o]
        dst = dst[_o]
        edge_weight = jax.random.uniform(jax.random.fold_in(_gk, 12), (100000,), jnp.float32, 0.0, 1)
        return (x, src, dst, edge_weight)
    x, src, dst, edge_weight = _rec_inputs()

    def _L0_gnn_setup():
        import jax, jax.numpy as jnp
        import numpy as np
        N_NODES = 6250
        N_EDGES = 200000
        D_IN = 256
        D_OUT = 256
        key = jax.random.key(seed)
        k1, k2, k3, k4, k5, k6 = jax.random.split(key, 6)
        x = jax.random.normal(k1, (N_NODES, D_IN), dtype=jnp.float32)
        edge_row = jax.random.randint(k2, (N_EDGES,), 0, N_NODES, dtype=jnp.int32)
        edge_col = jax.random.randint(k3, (N_EDGES,), 0, N_NODES, dtype=jnp.int32)
        edge_val = jax.random.uniform(k4, (N_EDGES,), dtype=jnp.float32)
        bound = 1.0 / np.sqrt(D_IN)
        W = jax.random.uniform(k5, (D_OUT, D_IN), minval=-bound, maxval=bound, dtype=jnp.float32)
        b = jax.random.uniform(k6, (D_OUT,), minval=-bound, maxval=bound, dtype=jnp.float32)
        return {'x': x, 'edge_row': edge_row, 'edge_col': edge_col, 'edge_val': edge_val, 'W': W, 'b': b}
    _L0_gnn_all = _L0_gnn_setup()
    _L0_gnn_in = {k: v for k, v in _L0_gnn_all.items() if k in ('W', 'b')}
    del _L0_gnn_all

    def _L0_mix_setup():
        import jax, jax.numpy as jnp
        import numpy as np
        NUM_HEADS = 8
        key = jax.random.key(seed)
        ks = jax.random.split(key, 5)
        B, N, C = (8, 1024, 256)
        x = jax.random.normal(ks[0], (B, N, C), dtype=jnp.float32)
        Wq = jax.random.normal(ks[1], (C, C), dtype=jnp.float32) * 0.02
        Wkv = jax.random.normal(ks[2], (2 * C, C), dtype=jnp.float32) * 0.02
        Wproj = jax.random.normal(ks[3], (C, C), dtype=jnp.float32) * 0.02
        bproj = jnp.zeros((C,), dtype=jnp.float32)
        return {'x': x, 'Wq': Wq, 'Wkv': Wkv, 'Wproj': Wproj, 'bproj': bproj}
    _L0_mix_all = _L0_mix_setup()
    _L0_mix_in = {k: v for k, v in _L0_mix_all.items() if k in ('Wq', 'Wkv', 'Wproj', 'bproj')}
    del _L0_mix_all

    def _L0_ffn_setup():
        import jax, jax.numpy as jnp
        import numpy as np
        B, S, D, H, E, K = (8, 512, 256, 1024, 8, 2)
        key = jax.random.key(seed)
        ks = jax.random.split(key, 7)
        s_in = 1.0 / np.sqrt(D)
        s_hid = 1.0 / np.sqrt(H)
        return {'x': jax.random.normal(ks[0], (B, S, D), dtype=jnp.float32), 'Wg': jax.random.uniform(ks[1], (E, D), jnp.float32, -s_in, s_in), 'bg': jax.random.uniform(ks[2], (E,), jnp.float32, -s_in, s_in), 'W1': jax.random.uniform(ks[3], (E, H, D), jnp.float32, -s_in, s_in), 'b1': jax.random.uniform(ks[4], (E, H), jnp.float32, -s_in, s_in), 'W2': jax.random.uniform(ks[5], (E, D, H), jnp.float32, -s_hid, s_hid), 'b2': jax.random.uniform(ks[6], (E, D), jnp.float32, -s_hid, s_hid)}
    _L0_ffn_all = _L0_ffn_setup()
    _L0_ffn_in = {k: v for k, v in _L0_ffn_all.items() if k in ('Wg', 'bg', 'W1', 'b1', 'W2', 'b2')}
    del _L0_ffn_all
    return {'x': x, 'src': src, 'dst': dst, 'edge_weight': edge_weight, 'L0_gnn_W': _L0_gnn_in['W'], 'L0_gnn_b': _L0_gnn_in['b'], 'L0_mix_Wq': _L0_mix_in['Wq'], 'L0_mix_Wkv': _L0_mix_in['Wkv'], 'L0_mix_Wproj': _L0_mix_in['Wproj'], 'L0_mix_bproj': _L0_mix_in['bproj'], 'L0_ffn_Wg': _L0_ffn_in['Wg'], 'L0_ffn_bg': _L0_ffn_in['bg'], 'L0_ffn_W1': _L0_ffn_in['W1'], 'L0_ffn_b1': _L0_ffn_in['b1'], 'L0_ffn_W2': _L0_ffn_in['W2'], 'L0_ffn_b2': _L0_ffn_in['b2']}

def reference(x, src, dst, edge_weight, L0_gnn_W, L0_gnn_b, L0_mix_Wq, L0_mix_Wkv, L0_mix_Wproj, L0_mix_bproj, L0_ffn_Wg, L0_ffn_bg, L0_ffn_W1, L0_ffn_b1, L0_ffn_W2, L0_ffn_b2):
    import jax
    import jax.numpy as jnp

    def _L0_gnn_ref(x, edge_row, edge_col, edge_val, W, b):
        import jax, jax.numpy as jnp
        import numpy as np
        N_NODES = 6250
        N_EDGES = 200000
        D_IN = 256
        D_OUT = 256
        gathered = edge_val[:, None] * x[edge_col]
        agg = jax.ops.segment_sum(gathered, edge_row, num_segments=N_NODES)
        return jnp.einsum('nd,od->no', agg, W) + b

    def _L0_mix_ref(x, Wq, Wkv, Wproj, bproj):
        import jax, jax.numpy as jnp
        import numpy as np
        NUM_HEADS = 8
        B, N, C = x.shape
        h = NUM_HEADS
        d = C // h
        q = jnp.einsum('bnc,oc->bno', x, Wq).reshape(B, N, h, d).transpose(0, 2, 1, 3)
        kv = jnp.einsum('bnc,oc->bno', x, Wkv).reshape(B, N, 2, h, d)
        k = kv[:, :, 0].transpose(0, 2, 1, 3)
        v = kv[:, :, 1].transpose(0, 2, 1, 3)
        q = jax.nn.elu(q) + 1.0
        k = jax.nn.elu(k) + 1.0
        k_sum = k.sum(axis=2)
        D_inv = 1.0 / jnp.maximum(jnp.einsum('bhnd,bhd->bhn', q, k_sum), 1e-06)
        context = jnp.einsum('bhnd,bhne->bhde', k, v)
        attn = jnp.einsum('bhnd,bhde->bhne', q, context) * D_inv[..., None]
        out = attn.transpose(0, 2, 1, 3).reshape(B, N, C)
        out = jnp.einsum('bnc,oc->bno', out, Wproj) + bproj
        return out

    def _L0_ffn_ref(x, Wg, bg, W1, b1, W2, b2):
        import jax, jax.numpy as jnp
        import numpy as np
        B, S, D, H, E, K = (8, 512, 256, 1024, 8, 2)
        gate_scores = jnp.einsum('bsd,ed->bse', x, Wg) + bg
        topk_scores, topk_idx = jax.lax.top_k(gate_scores, K)
        topk_probs = jax.nn.softmax(topk_scores, axis=-1)
        combine = jnp.sum(topk_probs[..., None] * jax.nn.one_hot(topk_idx, E, dtype=x.dtype), axis=-2)
        out = jnp.zeros_like(x)
        for e in range(E):
            h = jax.nn.relu(jnp.einsum('bsd,hd->bsh', x, W1[e]) + b1[e])
            y = jnp.einsum('bsh,dh->bsd', h, W2[e]) + b2[e]
            out = out + combine[..., e:e + 1] * y
        return out
    xn = _layernorm(x, axis=-1)
    x = x + _L0_gnn_ref(xn, src, dst, edge_weight, L0_gnn_W, L0_gnn_b) + _L0_mix_ref(xn[None], L0_mix_Wq, L0_mix_Wkv, L0_mix_Wproj, L0_mix_bproj)[0]
    x = x + _L0_ffn_ref(_layernorm(x, axis=-1)[None], L0_ffn_Wg, L0_ffn_bg, L0_ffn_W1, L0_ffn_b1, L0_ffn_W2, L0_ffn_b2)[0]
    return x

_drawn_inputs = setup_inputs


def setup_inputs(seed=0):
    import zlib

    import numpy as np

    out = dict(_drawn_inputs(seed))
    spreads = {'L0_mix_bproj': (0.0, 0.1)}
    factors = {'L0_mix_Wq': 8.0,
     'L0_mix_Wkv': 8.0,
     'L0_mix_Wproj': 8.0,
     'L0_ffn_bg': 2.765,
     'L0_ffn_b1': 8.0,
     'L0_ffn_b2': 7.214}
    for name, (base, spread) in spreads.items():
        noise = np.random.default_rng([zlib.crc32(name.encode()), seed]).standard_normal(out[name].shape)
        drawn = base * np.exp(spread * noise) if base else spread * noise
        out[name] = jnp.asarray(drawn.astype(out[name].dtype))
    for name, factor in factors.items():
        out[name] = (out[name] * factor).astype(out[name].dtype)
    return out
```

```python
import numpy as np
import concourse.bass as bass
from concourse import mybir
from contextlib import ExitStack

F32, F16, I32, U32, U16 = (mybir.dt.float32, mybir.dt.float16, mybir.dt.int32, mybir.dt.uint32, mybir.dt.uint16)
ALU = mybir.AluOpType
ACT = mybir.ActivationFunctionType
AX = mybir.AxisListType

P = 128
N, D = 6250, 256
NT = -(-N // P)
TAIL = N - (NT - 1) * P
NP = NT * P
E = 100000
EF = E // P
EC = EF + 1
ER = E - EF * P
ETM = (E + NT * (P - 1)) // P
UG = 8
ET = -(-ETM // (2 * UG)) * 2 * UG
W = 4
US = 17
assert EC % (2 * US) == 0
NE, H, TOP = 8, 1024, 2
MT = (TOP * N + NE * (P - 1)) // P
HB = H // P
DH = D // P
HEAD = 32
EPS = 1e-5
DEN_MIN = 1e-6
CH = DH * NE * H // 1024


class Arena:

    def __init__(self, t, cols):
        self.t, self.at, self.cols = t, 0, cols

    def take(self, n, dt=F32):
        words = n if dt in (F32, I32, U32) else -(-n // 2)
        words += words % 2
        a = self.t[:, self.at:self.at + words]
        self.at += words
        assert self.at <= self.cols, (self.at, self.cols)
        return (a if dt == F32 else a.bitcast(dt))[:, 0:n]


class Core:
    pass


def matrix(a, n, m):
    return a.rearrange("p (n m) -> p n m", n=n, m=m)


class Chain:

    def __init__(self, e, sem):
        self.e, self.sem, self.n, self.k = e, sem, 0, 0

    def enter(self, i, per):
        self.before = self.n + self.k
        self.n, self.k, self.per = self.before + i * per, 0, per

    def leave(self, trips):
        assert self.k == self.per, (self.k, self.per)
        self.n, self.k = self.before + trips * self.per, 0

    def add(self, ins):
        self.k += 1
        ins.then_inc(self.sem, 1)

    def sync(self):
        self.e.wait_ge(self.sem, self.n + self.k)

    def link(self, ins):
        self.add(ins)
        self.sync()


def build(nc, A, out, stage=9):
    ctx = ExitStack()
    with ctx:
        c = Core()
        c.sem = lambda name: ctx.enter_context(nc.semaphore(name))
        sb = lambda name, n, dt=F32: ctx.enter_context(nc.sbuf_tensor(name, [P, n], dt))
        c.acc = sb("acc", NT * D)
        c.big = sb("big", 4 * 8192)
        c.rec = sb("rec", ET * W, I32)
        c.pos = sb("pos", ET, I32)
        c.misc = sb("misc", 3100)
        k = Arena(sb("consts", 560), 560)
        c.ident = k.take(P)
        c.ident16 = k.take(P, F16)
        c.before = k.take(P, F16)
        c.column = k.take(P)
        c.idx = [k.take(UG, I32) for _ in range(2)]
        c.spare = k.take(8)
        c.valid = k.take(1)
        c.scale = k.take(2)
        c.descale = k.take(2)
        ps = ctx.enter_context(nc.psum_tensor("ps", [P, 8 * 512], F32))
        c.bank = [ps[:, 512 * i:512 * i + 512] for i in range(8)]
        c.wide = [ps[:, 1024 * i:1024 * i + 1024] for i in range(4)]
        wide16 = c.big[:, :].bitcast(F16)
        c.w = [[wide16[:, (2 * layer + part) * 16384:(2 * layer + part + 1) * 16384] for part in range(2)] for layer in range(2)]
        c.acc3 = matrix(c.acc[:, :], NT, D)
        dram = lambda name, shape, dt=F32: nc.dram_tensor(name, shape, dt).ap()
        c.rec_d = dram("rec_d", (P * ET, W), I32)
        c.blk_d = dram("blk_d", (1, ET), I32)
        c.z_d = dram("z_d", (NP, D))
        c.tok_d = dram("tok_d", (NP, 2 * D), F16)
        c.slot_d = dram("slot_d", (MT * P, 2 * D), F16)
        c.y_d = dram("y_d", (MT * P, D))
        rank(nc, c, A)
        if stage >= 2:
            mix(nc, c, A)
        if stage >= 3:
            graph(nc, c)
        if stage >= 4:
            route(nc, c, A)
            experts(nc, c, A)
            combine(nc, c, out)
        else:
            dump(nc, c, out, stage)


def dump(nc, c, out, stage):
    s = c.sem("dump")
    with nc.Block() as block:
        @block.sync
        def _(e):
            if stage == 1:
                e.dma_start(out[0:512, :].rearrange("(p a) d -> p (a d)", p=P)[:, 0:782], c.pos[:, 0:782].bitcast(F32)).then_inc(s, 16)
                e.wait_ge(s, 16)
            else:
                e.dma_start(out[0:(NT - 1) * P, :].rearrange("(t p) d -> p t d", p=P), c.acc3[:, 0:NT - 1, :]).then_inc(s, 16)
                e.wait_ge(s, 16)
                e.dma_start(out[(NT - 1) * P:N, :], c.acc3[0:TAIL, NT - 1, :]).then_inc(s, 16)
                e.wait_ge(s, 32)


def rank(nc, c, A):
    big, acc = Arena(c.big, 32768), Arena(c.acc, NT * D)
    onehot = matrix(big.take(NT * EC, F16), NT, EC)
    pick1 = matrix(big.take(NT * P, F16), NT, P)
    pick256 = matrix(big.take(NT * P, F16), NT, P)
    band = big.take(5 * P, F16)
    blanks = matrix(acc.take(ET * W, I32), ET, W)
    src, dst, wgt, blk_i = (acc.take(EC, I32) for _ in range(4))
    blk16 = acc.take(EC, F16)
    ones, upto, base = (acc.take(EC) for _ in range(3))
    base_i, part_i = (acc.take(EC, I32) for _ in range(2))
    lo16, hi16 = (acc.take(EC, F16) for _ in range(2))
    place = big.take(EC)
    number = big.take(64)
    tile_no = big.take(ET)
    tiles_f, start128, end = (big.take(2) for _ in range(3))
    tiles_i = big.take(2, I32)
    started = big.take(ET, F16)
    few = big.take(2, F16)
    before_f = big.take(P)
    blk_row = big.take(ET, I32)
    rec = matrix(c.rec[:, 0:EC * W], EC, W)
    counts, starts, row = c.wide[0], c.bank[2], c.wide[3]
    s_load, s_tail, s_out = (c.sem("rank_" + n) for n in ("load", "tail", "out"))
    s_preset, s_blank, s_k, s_cast, s_hot, s_cnt, s_til, s_sta, s_end, s_row, s_base, s_pre, s_pos, s_rec, s_c, s_g, s_p, s_blkrow = (
        c.sem("rank_" + n) for n in ("preset", "blank", "consts", "cast", "hot", "counts", "tiles", "starts",
                                     "end", "row", "base", "prefix", "pos", "rec", "vector", "gpsimd", "tensor", "blkrow"))
    cols = [(0, 512), (512, EC)]
    inputs = ((src, A["src"]), (dst, A["dst"]), (wgt, A["edge_weight"].bitcast(I32)))
    one = lambda a: a.rearrange("p (a t) -> p a t", a=1)
    def choose(e, b, u):
        e.wait_ge(s_pre, b + 1)
        e.copy_predicated(place, onehot[:, b, :].bitcast(U16), c.wide[u + 1][:, 0:EC]).then_inc(s_pos, 1)
        e.wait_ge(s_pos, b + 1)

    def places(e, b, u, free):
        if free:
            e.wait_ge(s_pos, b - 1)
        for x, y in cols:
            e.matmul(c.wide[u + 1][:, x:y], c.before, onehot[:, bass.ds(b, 1), x:y], start=True, stop=False)
            e.matmul(c.wide[u + 1][:, x:y], pick1[:, bass.ds(b, 1), :], lo16[:, x:y], start=False, stop=False)
            l = e.matmul(c.wide[u + 1][:, x:y], pick256[:, bass.ds(b, 1), :], hi16[:, x:y], start=False, stop=True)
        l.then_inc(s_pre, 1)

    with nc.Block() as block:
        @block.sync
        def _(e):
            for t, a in inputs:
                e.dma_start(t[:, 0:EF], a[0:EF * P].rearrange("(p t) -> p t", p=P)).then_inc(s_load, 16)
            e.wait_ge(s_preset, 3)
            for t, a in inputs:
                e.dma_start(t[0:ER, EF:EC], a[EF * P:E].rearrange("(p t) -> p t", t=1)).then_inc(s_tail, 16)
            e.wait_ge(s_blank, 2)
            e.dma_start(c.rec_d.rearrange("(p t) w -> p (t w)", p=P), blanks.rearrange("p t w -> p (t w)")).then_inc(s_out, 16)
            e.wait_ge(s_blkrow, 1)
            e.dma_start(c.blk_d, blk_row[0:1, :]).then_inc(s_out, 16)
            e.wait_ge(s_out, 32)

        @block.gpsimd
        def _(e):
            g = Chain(e, s_g)
            iota = lambda t, n: g.add(e.iota(t, pattern=[[1, n]], base=0, channel_multiplier=0,
                                             allow_small_or_imprecise_dtypes=True))
            select = lambda t, op, base, pattern, by: e.affine_select(
                out=t, in_=t, compare_op=op, fill=0.0, base=base, pattern=pattern, channel_multiplier=by).then_inc(s_k, 1)
            iota(number, 64)
            iota(tile_no, ET)
            iota(c.column, P)
            g.add(e.memset(pick1, 1.0))
            g.add(e.memset(c.ident, 1.0))
            g.add(e.memset(before_f, 1.0))
            g.add(e.memset(few, 1.0))
            g.add(e.memset(band, 0.0))
            g.sync()
            e.memset(band[:, P - 1:P], 1.0).then_inc(s_k, 1)
            select(pick1, ALU.is_equal, 0, [[-1, NT], [0, P]], 1)
            select(c.ident, ALU.is_equal, 0, [[-1, P]], 1)
            select(before_f, ALU.is_gt, 0, [[1, P]], -1)
            select(few, ALU.is_gt, NT - 1, [[0, 2]], -1)
            e.memset(rec[:, :, 3], 0).then_inc(s_rec, 1)
            e.wait_ge(s_load, 48)
            e.wait_ge(s_tail, 48)
            e.tensor_copy(rec[:, :, 0], dst).then_inc(s_rec, 1)
            e.tensor_copy(rec[:, :, 2], wgt).then_inc(s_rec, 1)

        @block.vector
        def _(e):
            v = Chain(e, s_c)
            e.memset(src[:, EF:EC], NP + P).then_inc(s_preset, 1)
            e.memset(dst[:, EF:EC], 0).then_inc(s_preset, 1)
            e.memset(wgt[:, EF:EC], 0).then_inc(s_preset, 1)
            e.memset(blanks, 0).then_inc(s_blank, 1)
            v.add(e.memset(place, 0.0))
            v.add(e.memset(ones, 1.0))
            e.wait_ge(s_blank, 1)
            e.memset(blanks.bitcast(F32)[:, :, 1], -1.0).then_inc(s_blank, 1)
            e.wait_ge(s_k, 5)
            e.tensor_copy(c.ident16, c.ident).then_inc(s_cast, 1)
            e.tensor_copy(c.before, before_f).then_inc(s_cast, 1)
            e.tensor_scalar(pick256, pick1, 256.0, None, ALU.mult).then_inc(s_cast, 1)
            e.wait_ge(s_load, 48)
            e.wait_ge(s_tail, 48)
            v.link(e.tensor_scalar(blk_i, src, 7, None, ALU.logical_shift_right))
            v.link(e.tensor_copy(blk16, blk_i))
            with e.Fori(0, NT // 7) as i:
                for u in range(7):
                    b = i * 7 + u
                    e.tensor_scalar(onehot[:, bass.ds(b, 1), :], one(blk16), number[:, bass.ds(b, 1)], None,
                                    ALU.is_equal).then_inc(s_hot, 1)
            v.link(e.tensor_scalar(part_i, src, P - 1, None, ALU.bitwise_and))
            e.tensor_copy(rec.bitcast(F32)[:, :, 1], part_i).then_inc(s_rec, 1)
            e.wait_ge(s_cnt, 1)
            v.link(e.tensor_tensor_scan(upto, ones, counts[:, 0:EC], 0.0, ALU.mult, ALU.add))
            v.link(e.tensor_scalar(tiles_i[:, 0:1], upto[:, EC - 1:EC], P - 1.0, None, ALU.add))
            v.link(e.tensor_scalar(tiles_i[:, 1:2], tiles_i[:, 0:1], 7, None, ALU.logical_shift_right))
            e.tensor_copy(tiles_f[:, 0:1], tiles_i[:, 1:2]).then_inc(s_til, 1)
            e.wait_ge(s_til, 1)
            e.wait_ge(s_sta, 1)
            v.add(e.tensor_scalar(start128[:, 0:1], starts[:, 0:1], float(P), None, ALU.mult))
            v.link(e.tensor_tensor(end[:, 0:1], starts[:, 0:1], tiles_f[:, 0:1], ALU.add))
            e.tensor_scalar(started, tile_no, end[:, 0:1], None, ALU.is_ge).then_inc(s_end, 1)
            v.link(e.scalar_tensor_tensor(out=base, in0=upto, scalar=start128[:, 0:1], in1=counts[:, 0:EC],
                                          op0=ALU.add, op1=ALU.subtract))
            v.link(e.tensor_copy(base_i, base))
            v.link(e.tensor_scalar(part_i, base_i, 8, None, ALU.logical_shift_right))
            v.link(e.tensor_copy(hi16, part_i))
            v.link(e.tensor_scalar(part_i, base_i, 255, None, ALU.bitwise_and))
            e.tensor_copy(lo16, part_i).then_inc(s_base, 1)
            e.wait_ge(s_row, 1)
            e.tensor_copy(blk_row[0:1, :], row[0:1, 0:ET]).then_inc(s_blkrow, 1)
            for b in range(NT):
                choose(e, b, b % 2)
            v.link(e.tensor_copy(base_i, place))
            v.add(e.tensor_scalar(part_i, base_i, 7, None, ALU.logical_shift_right))
            v.link(e.tensor_scalar(src, base_i, P - 1, None, ALU.bitwise_and))
            v.link(e.scalar_tensor_tensor(out=c.pos[:, 0:EC], in0=src, scalar=float(ET), in1=part_i,
                                          op0=ALU.mult, op1=ALU.add))

        @block.tensor
        def _(e):
            e.wait_ge(s_k, 5)
            e.wait_ge(s_cast, 3)
            for x, y in cols:
                e.matmul(counts[:, x:y], band[:, P:2 * P], band[:, P:P + y - x], start=True, stop=False)
            with e.Fori(0, NT) as b:
                e.wait_ge(s_hot, b + 1)
                for x, y in cols:
                    e.matmul(counts[:, x:y], band[:, bass.ds(P - 1 - b, P)], onehot[:, bass.ds(b, 1), x:y],
                             start=False, stop=False)
            for x, y in cols:
                l = e.matmul(counts[:, x:y], band[:, P:2 * P], band[:, P:P + y - x], start=False, stop=True)
            l.then_inc(s_cnt, 1)
            e.wait_ge(s_til, 1)
            e.matmul(starts[:, 0:1], before_f, tiles_f[:, 0:1], start=True, stop=True).then_inc(s_sta, 1)
            e.wait_ge(s_end, 1)
            e.matmul(row[0:1, 0:512], few[:, 0:1], started[:, 0:512], start=True, stop=True)
            e.matmul(row[0:1, 512:ET], few[:, 0:1], started[:, 512:ET], start=True, stop=True).then_inc(s_row, 1)
            e.wait_ge(s_base, 1)
            places(e, 0, 0, False)
            places(e, 1, 1, False)
            with e.Fori(1, (NT - 1) // 2) as i:
                for u in range(2):
                    places(e, i * 2 + u, u, True)
            places(e, NT - 1, 0, True)


class Step:

    def __init__(self, j, u, more=True):
        self.j, self.u, self.more, self.i = j, u, more, j * 2 + u
        self.zero = isinstance(j, int) and j == u == 0
        self.fresh = isinstance(j, int) and j == 0
        self.first2 = self.fresh

    def next(self):
        return Step(self.j + self.u, 1 - self.u)

    def prev(self):
        return Step(self.j - 1 + self.u, 1 - self.u)


def paired(e, steps, body, chain=None, per=0):
    assert steps % 2
    body(Step(0, 0))
    body(Step(0, 1))
    with e.Fori(1, steps // 2) as j:
        if chain:
            chain.enter(j - 1, 2 * per)
        for u in range(2):
            body(Step(j, u))
    if chain:
        chain.leave(steps // 2 - 1)
    body(Step(steps // 2, 0, False))


def carry(e, g, spare):
    g.sync()
    g.add(e.tensor_tensor(spare[:, 4:6], spare[:, 0:2], spare[:, 2:4], ALU.add))


def stats(e, v, c, st, mean, var, s_var):
    with e.Fori(0, NT // 7) as i:
        v.enter(i, 7)
        for u in range(7):
            v.add(e.bn_stats(st[:, bass.ds(i * 7 + u, 1), :], c.acc3[:, bass.ds(i * 7 + u, 1), :]))
    v.leave(NT // 7)
    v.sync()
    v.add(e.tensor_tensor(mean, st[:, :, 1], st[:, :, 4], ALU.add))
    v.link(e.tensor_tensor(var, st[:, :, 1], st[:, :, 4], ALU.subtract))
    v.link(e.tensor_tensor(var, var, var, ALU.mult))
    v.add(e.tensor_scalar(var, var, 0.25, EPS, ALU.mult, ALU.add))
    v.link(e.tensor_tensor(st[:, :, 0], st[:, :, 2], st[:, :, 5], ALU.add))
    v.add(e.tensor_scalar(mean, mean, 0.5, None, ALU.mult))
    e.scalar_tensor_tensor(out=var, in0=st[:, :, 0], scalar=1.0 / D, in1=var, op0=ALU.mult, op1=ALU.add).then_inc(s_var, 1)


def mix(nc, c, A):
    big, misc = Arena(c.big, 32768), Arena(c.misc, 3100)
    qT = matrix(big.take(DH * NP), DH, NP)
    wq, wk, wp = (matrix(big.take(DH * D), DH, D) for _ in range(3))
    wvz = matrix(big.take(DH * 2 * D), DH, 2 * D)
    context, ksum = (matrix(big.take(DH * P), DH, P) for _ in range(2))
    heads = big.take(P)
    st = matrix(big.take(NT * 6), NT, 6)
    mean, var, std, rstd = (big.take(NT) for _ in range(4))
    xn = [big.take(D) for _ in range(2)]
    xT = [matrix(big.take(D), DH, P) for _ in range(2)]
    low, ex = big.take(2 * D), big.take(2 * D)
    kf = [big.take(D) for _ in range(2)]
    vo = [matrix(big.take(DH * (P + 1)), DH, P + 1) for _ in range(2)]
    zo = [big.take(D) for _ in range(2)]
    den = [big.take(D) for _ in range(2)]
    aT = [matrix(big.take(D), DH, P) for _ in range(2)]
    bias, ones, zeros = big.take(D), big.take(P), big.take(D + 4)
    valid = c.valid
    most = big.take(6)
    most2, clamp, s_f, both = (big.take(4) for _ in range(4))
    most2 = most2[:, 0:2]
    bits = big.take(2, I32)
    biases = big.take(H)
    assert big.at <= 24576
    big.at = 24576
    raw = big.take(8192)
    to = [misc.take(US, I32) for _ in range(2)]
    what = [misc.take(US * W, I32) for _ in range(2)]
    spare = c.spare
    part = [misc.take(1024) for _ in range(2)]
    S = lambda name: c.sem("mix_" + name)
    s_x, s_x0, s_w, s_raw, s_red, s_zero0, s_zero, s_v, s_g, s_std = map(S, (
        "x", "x0", "weights", "raw", "reduced", "zero0", "zero", "vector", "gpsimd", "std"))
    s_stage, s_sc = S("stage"), [S("scatter0"), S("scatter1")]
    s_xn, s_tr, s_xt, s_qk, s_vz, s_low, s_ex, s_kf, s_vo, s_zo, s_ctx = map(S, (
        "xn", "tr", "xt", "qk", "vz", "low", "ex", "kf", "vo", "zo", "ctx"))
    s_zs = [S("zstore0"), S("zstore1")]
    s_bd, s_nd, s_at, s_pj, s_add = map(S, ("bd", "nd", "at", "pj", "add"))
    s_mt, s_mr, s_mb, s_scale = map(S, ("most_t", "most_r", "most_b", "scale"))
    s_k, s_ones, s_var, s_b1, s_b10, s_bmax, s_hi, s_lo = map(S, ("consts", "ones", "var", "b1", "b1_0", "most", "hi", "lo"))
    s_part = [S("part0"), S("part1")]
    qk_ps = [c.bank[0], c.bank[1]]
    vz_ps = [c.bank[2], c.bank[3]]
    tr_ps = [c.bank[4], c.bank[5]]
    ctx_ps = matrix(c.bank[6][:, 0:DH * (P + 1)], DH, P + 1)
    RAW = [("w1T", 0), ("w1T", 1), ("w2T", 0), ("w2T", 1)]
    flat = {k: A[k].rearrange("p a b -> p (a b)") for k in ("w1T", "w2T")}
    last = NT - 1

    def norm(e, s):
        if not s.fresh:
            e.wait_ge(s_tr, s.i - 1)
        e.tensor_scalar(xn[s.u], c.acc3[:, bass.ds(s.i, 1), :], mean[:, bass.ds(s.i, 1)], rstd[:, bass.ds(s.i, 1)],
                        ALU.subtract, ALU.mult).then_inc(s_xn, 1)

    def features(e, s):
        if s.more:
            norm(e, s.next())
        e.wait_ge(s_qk, s.i + 1)
        e.tensor_scalar(low, qk_ps[s.u], 0.0, None, ALU.min).then_inc(s_low, 1)
        if not s.fresh:
            e.wait_ge(s_ctx, s.i - 1)
        e.wait_ge(s_ex, s.i + 1)
        e.scalar_tensor_tensor(out=kf[s.u], in0=qk_ps[s.u][:, D:2 * D], scalar=0.0, in1=ex[:, D:2 * D],
                               op0=ALU.max, op1=ALU.add)
        e.scalar_tensor_tensor(out=qT[:, :, bass.ds(s.i * P, P)], in0=matrix(qk_ps[s.u][:, 0:D], DH, P), scalar=0.0,
                               in1=matrix(ex[:, 0:D], DH, P), op0=ALU.max, op1=ALU.add).then_inc(s_kf, 1)

    def add_to(e, s):
        e.wait_ge(s_pj, s.i + 1)
        e.tensor_tensor(c.acc3[:, bass.ds(s.i, 1), :], c.acc3[:, bass.ds(s.i, 1), :],
                        vz_ps[s.u][:, 0:D].rearrange("p (a d) -> p a d", a=1), ALU.add).then_inc(s_add, 1)

    def xt_copy(e, s):
        e.wait_ge(s_tr, s.i + 1)
        if not s.fresh:
            e.wait_ge(s_vz, s.i - 1)
        e.copy(xT[s.u], matrix(tr_ps[s.u][:, 0:D], DH, P)).then_inc(s_xt, 1)

    def copies(e, s):
        if s.more:
            xt_copy(e, s.next())
        e.wait_ge(s_low, s.i + 1)
        if not s.zero:
            e.wait_ge(s_kf, s.i)
        e.activation(ex, low, ACT.Exp).then_inc(s_ex, 1)
        e.wait_ge(s_vz, s.i + 1)
        if not s.fresh:
            e.wait_ge(s_ctx, s.i - 1)
        if not s.more:
            for h in range(DH):
                e.copy(vo[s.u][:, h, P:P + 1], valid)
        e.copy(vo[s.u][:, :, 0:P], matrix(vz_ps[s.u][:, 0:D], DH, P)).then_inc(s_vo, 1)
        if not s.fresh:
            e.wait_ge(s_zs[s.u], 16 * s.j)
        e.copy(zo[s.u], vz_ps[s.u][:, D:2 * D]).then_inc(s_zo, 1)

    def turn(e, s):
        e.wait_ge(s_xn, s.i + 1)
        if not s.fresh:
            e.wait_ge(s_xt, s.i - 1)
        for h in range(DH):
            l = e.transpose(tr_ps[s.u][:, h * P:h * P + P], xn[s.u][:, h * P:h * P + P], c.ident)
        l.then_inc(s_tr, 1)

    def project(e, s):
        if s.more:
            turn(e, s.next())
        e.wait_ge(s_xt, s.i + 1)
        if not s.fresh:
            e.wait_ge(s_kf, s.i - 1)
        for m in range(DH):
            for h in range(DH):
                e.matmul(qk_ps[s.u][:, m * P:m * P + P], wq[:, h, m * P:m * P + P], xT[s.u][:, h, :], start=h == 0, stop=h == 1)
        for h in range(DH):
            l = e.matmul(qk_ps[s.u][:, D:2 * D], xT[s.u][:, h, :], wk[:, h, :], start=h == 0, stop=h == 1)
        l.then_inc(s_qk, 1)
        if not s.fresh:
            e.wait_ge(s_zo, s.i - 1)
        for h in range(DH):
            l = e.matmul(vz_ps[s.u], xT[s.u][:, h, :], wvz[:, h, :], start=h == 0, stop=h == 1)
        l.then_inc(s_vz, 1)
        if not s.zero:
            context_sum(e, s.prev())

    def context_sum(e, s):
        e.wait_ge(s_kf, s.i + 1)
        e.wait_ge(s_vo, s.i + 1)
        for h in range(DH):
            l = e.matmul(ctx_ps[:, h, :], kf[s.u][:, h * P:h * P + P], vo[s.u][:, h, :], start=False, stop=False)
        l.then_inc(s_ctx, 1)

    def attend(e, s):
        if not s.fresh:
            e.wait_ge(s_at, s.i - 1)
        for h in range(DH):
            e.matmul(qk_ps[s.u][:, h * P:h * P + P], context[:, h, :], qT[:, h, bass.ds(s.i * P, P)], start=True, stop=True)
            l = e.matmul(qk_ps[s.u][:, D + h * P:D + h * P + P], ksum[:, h, :], qT[:, h, bass.ds(s.i * P, P)], start=True, stop=True)
        l.then_inc(s_nd, 1)

    def out_proj(e, s):
        if s.more:
            attend(e, s.next())
        e.wait_ge(s_at, s.i + 1)
        if not s.fresh:
            e.wait_ge(s_add, s.i - 1)
        for h in range(DH):
            e.matmul(vz_ps[s.u][:, 0:D], aT[s.u][:, h, :], wp[:, h, :], start=h == 0, stop=False)
        e.matmul(vz_ps[s.u][:, 0:D], ones[0:2, :], bias[0:2, :], start=False, stop=True).then_inc(s_pj, 1)

    with nc.Block() as block:
        @block.sync
        def _(e):
            e.wait_ge(s_x0, 1)
            e.dma_start(c.acc3[:, 0:last, :], A["x"][0:last * P, :].rearrange("(t p) d -> p t d", p=P)).then_inc(s_x, 16)
            e.dma_start(c.acc3[0:TAIL, last, :], A["x"][last * P:N, :]).then_inc(s_x, 16)
            e.dma_start(wq, A["q_wT"]).then_inc(s_w, 16)
            e.dma_start(wk, A["kv_wT"][:, :, 0:D]).then_inc(s_w, 16)
            e.dma_start(wvz[:, :, 0:D], A["kv_wT"][:, :, D:2 * D]).then_inc(s_w, 16)
            e.dma_start(wvz[:, :, D:2 * D], A["gnn_wT"]).then_inc(s_w, 16)
            e.dma_start(wp, A["proj_wT"]).then_inc(s_w, 16)
            e.dma_start(bias[0:1, :], A["proj_b"]).then_inc(s_w, 16)
            e.dma_start(bias[1:2, :], A["gnn_b"]).then_inc(s_w, 16)
            e.dma_start(raw, flat["w1T"][:, 0:8192]).then_inc(s_raw, 16)
            e.wait_ge(s_b10, 1)
            e.dma_start(biases[0:NE, :], A["b1"]).then_inc(s_b1, 16)
            e.wait_ge(s_zero0, 1)
            e.dma_start(c.slot_d.rearrange("(p t) w -> p t w", p=P),
                        zeros[:, 0:D].bitcast(F16).rearrange("p (a w) -> p a w", a=1).to_broadcast([P, MT, 2 * D])).then_inc(s_zero, 16)
            e.wait_ge(s_red, 1)
            e.dma_start(raw, flat["w1T"][:, 8192:16384]).then_inc(s_raw, 16)

            def store(s):
                e.wait_ge(s_zo, s.i + 1)
                e.dma_start(c.z_d[bass.ds(s.i * P, P), :], zo[s.u]).then_inc(s_zs[s.u], 16)
            paired(e, NT, store)
            for r in (2, 3):
                e.wait_ge(s_red, r)
                e.dma_start(raw, flat["w2T"][:, (r - 2) * 8192:(r - 1) * 8192]).then_inc(s_raw, 16)
            for layer, name in enumerate(("w1T", "w2T")):
                def load(k, u):
                    e.dma_start(part[u], flat[name][:, bass.ds(k * 1024, 1024)]).then_inc(s_part[u], 16)
                if layer == 0:
                    load(0, 0)
                    load(1, 1)
                with e.Fori(1 - layer, CH // 2) as j:
                    for u in range(2):
                        e.wait_ge(s_lo, CH * layer + j * 2 + u - 1)
                        load(j * 2 + u, u)
            e.wait_ge(s_zero, 16)
            e.wait_ge(s_zs[0], 16 * (NT // 2 + 1))
            e.wait_ge(s_zs[1], 16 * (NT // 2))

        @block.gpsimd
        def _(e):
            g = Chain(e, s_g)
            g.add(e.memset(spare, 0.0))
            g.add(e.memset(valid, 1.0))
            g.sync()
            e.affine_select(out=valid, in_=valid, compare_op=ALU.is_gt, fill=0.0, base=TAIL,
                            pattern=[[0, 1]], channel_multiplier=-1).then_inc(s_k, 1)
            rec = matrix(c.rec[:, 0:EC * W], EC, W)

            def scatter(j, first, tail=False):
                for u in range(2):
                    if not first:
                        e.wait_ge(s_sc[u], 16 * US * j)
                    at = (j * 2 + u) * US
                    g.add(e.tensor_copy(to[u], c.pos[:, bass.ds(at, US)]))
                    g.add(e.tensor_copy(matrix(what[u], US, W), rec[:, bass.ds(at, US), :]))
                    carry(e, g, spare)
                    for n in range(US):
                        k = ER if tail and u == 1 and n == US - 1 else P
                        e.indirect_dma_start(out=c.rec_d, out_offset=bass.IndirectOffsetOnAxis(ap=to[u][0:k, n:n + 1], axis=0),
                                             in_=what[u][0:k, n * W:n * W + W], in_offset=None).then_inc(s_sc[u], 16)
            trips = EC // (2 * US)
            scatter(0, True)
            with e.Fori(1, trips - 1) as j:
                g.enter(j - 1, 6)
                scatter(j, False)
            g.leave(trips - 2)
            scatter(trips - 1, False, True)
            for u in range(2):
                e.wait_ge(s_sc[u], 16 * US * trips)

        @block.vector
        def _(e):
            v = Chain(e, s_v)
            e.memset(c.acc3[:, last, :], 0.0).then_inc(s_x0, 1)
            e.memset(zeros, 0.0).then_inc(s_zero0, 1)
            e.memset(biases, 0.0).then_inc(s_b10, 1)
            v.link(e.memset(heads, 0.0))
            for a in range(0, P, HEAD):
                v.add(e.memset(heads[a:a + HEAD, a:a + HEAD], 1.0))
            for t in (ones, vo[0], vo[1]):
                e.memset(t, 1.0).then_inc(s_ones, 1)
            e.wait_ge(s_x, 32)
            stats(e, v, c, st, mean, var, s_var)
            e.wait_ge(s_std, 1)
            v.link(e.reciprocal(rstd, std))
            e.wait_ge(s_raw, 16)
            e.tensor_reduce(most[:, 0:1], raw, AX.X, ALU.max, apply_absolute_value=True).then_inc(s_red, 1)
            norm(e, Step(0, 0))
            paired(e, NT, lambda s: features(e, s))
            e.wait_ge(s_ctx, NT + 1)
            for h in range(DH):
                v.add(e.tensor_tensor(context[:, h, :], ctx_ps[:, h, 0:P], heads, ALU.mult))
                l = e.tensor_scalar(ksum[:, h, :], heads, ctx_ps[:, h, P:P + 1], None, ALU.mult)
            l.then_inc(s_bd, 1)
            e.wait_ge(s_raw, 32)
            e.tensor_reduce(most[:, 1:2], raw, AX.X, ALU.max, apply_absolute_value=True).then_inc(s_red, 1)

            def attention(s):
                e.wait_ge(s_nd, s.i + 1)
                if not s.fresh:
                    e.wait_ge(s_pj, s.i - 1)
                v.link(e.tensor_scalar(den[s.u], qk_ps[s.u][:, D:2 * D], DEN_MIN, None, ALU.max))
                v.link(e.reciprocal(den[s.u], den[s.u]))
                e.tensor_tensor(aT[s.u], matrix(qk_ps[s.u][:, 0:D], DH, P), matrix(den[s.u], DH, P), ALU.mult).then_inc(s_at, 1)
                if not s.zero:
                    add_to(e, s.prev())
            paired(e, NT, attention, v, 2)
            add_to(e, Step(NT // 2, 0))
            for r in (2, 3):
                e.wait_ge(s_raw, 16 * (r + 1))
                e.tensor_reduce(most[:, r:r + 1], raw, AX.X, ALU.max, apply_absolute_value=True).then_inc(s_red, 1)
            e.wait_ge(s_b1, 16)
            v.link(e.tensor_reduce(most[:, 4:5], biases, AX.X, ALU.max, apply_absolute_value=True))
            e.wait_ge(s_red, 4)
            v.link(e.tensor_tensor(most2, most[:, 0:4:2], most[:, 1:4:2], ALU.max))
            e.tensor_tensor(most2[:, 0:1], most2[:, 0:1], most[:, 4:5], ALU.max).then_inc(s_bmax, 1)
            e.wait_ge(s_mt, 1)
            v.link(e.tensor_reduce(clamp[0:2, 0:1], c.bank[7][0:2, 0:P], AX.X, ALU.max))
            v.link(e.tensor_scalar(clamp[0:2, 0:1], clamp[0:2, 0:1], 2.0 ** -60, 2.0 ** 60, ALU.max, ALU.min))
            v.link(e.tensor_scalar(bits[0:2, 0:1], clamp[0:2, 0:1].bitcast(I32), 0x7F800000, None, ALU.bitwise_and))
            v.add(e.tensor_scalar(s_f[0:2, 0:1].bitcast(I32), bits[0:2, 0:1], -1.0, 257.0 * 2 ** 23, ALU.mult, ALU.add))
            v.link(e.tensor_scalar(s_f[0:2, 1:2].bitcast(I32), bits[0:2, 0:1], 3.0 * 2 ** 23, None, ALU.subtract))
            v.add(e.tensor_scalar(both[0:2, 0:2], c.ident[0:2, 0:2], s_f[0:2, 0:1], None, ALU.mult))
            e.tensor_scalar(both[0:2, 2:4], c.ident[0:2, 0:2], s_f[0:2, 1:2], None, ALU.mult).then_inc(s_mr, 1)
            e.wait_ge(s_mb, 1)
            v.link(e.tensor_copy(c.scale, c.bank[7][:, 256:258]))
            v.link(e.tensor_copy(c.descale, c.bank[7][:, 258:260]))
            v.add(e.tensor_tensor(c.descale[:, 1:2], c.descale[:, 0:1], c.descale[:, 1:2], ALU.mult))
            v.sync()
            e.nop().then_inc(s_scale, 1)

            def low_part(layer, j, u):
                k = j * 2 + u
                e.wait_ge(s_hi, CH * layer + k + 1)
                e.scalar_tensor_tensor(out=c.w[layer][1][:, bass.ds(k * 1024, 1024)], in0=part[u], scalar=c.scale[:, layer:layer + 1],
                                       in1=c.w[layer][0][:, bass.ds(k * 1024, 1024)], op0=ALU.mult, op1=ALU.subtract).then_inc(s_lo, 1)
            for layer in range(2):
                with e.Fori(0, CH // 2) as j:
                    for u in range(2):
                        low_part(layer, j, u)

        @block.scalar
        def _(e):
            e.wait_ge(s_var, 1)
            e.activation(std, var, ACT.Sqrt).then_inc(s_std, 1)
            xt_copy(e, Step(0, 0))
            e.wait_ge(s_k, 1)
            e.wait_ge(s_ones, 3)
            paired(e, NT, lambda s: copies(e, s))
            e.wait_ge(s_scale, 1)
            for layer in range(2):
                with e.Fori(0, CH // 2) as j:
                    for u in range(2):
                        k = j * 2 + u
                        e.wait_ge(s_part[u], 16 * (CH // 2 * layer + j + 1))
                        e.activation(c.w[layer][0][:, bass.ds(k * 1024, 1024)], part[u], ACT.Copy,
                                     scale=c.scale[:, layer:layer + 1]).then_inc(s_hi, 1)

        @block.tensor
        def _(e):
            e.wait_ge(s_w, 16 * 7)
            e.wait_ge(s_zero0, 1)
            e.wait_ge(s_ones, 3)
            e.matmul(ctx_ps, zeros[:, 0:P], matrix(zeros[:, 0:DH * (P + 1)], DH, P + 1), start=True, stop=False)
            turn(e, Step(0, 0))
            paired(e, NT, lambda s: project(e, s))
            context_sum(e, Step(NT // 2, 0))
            e.matmul(ctx_ps, zeros[:, 0:P], matrix(zeros[:, 0:DH * (P + 1)], DH, P + 1), start=False, stop=True).then_inc(s_ctx, 1)
            e.wait_ge(s_bd, 1)
            e.wait_ge(s_zo, NT)
            attend(e, Step(0, 0))
            paired(e, NT, lambda s: out_proj(e, s))
            e.wait_ge(s_bmax, 1)
            e.transpose(c.bank[7][0:2, 0:P], most2, c.ident).then_inc(s_mt, 1)
            e.wait_ge(s_mr, 1)
            e.matmul(c.bank[7][:, 256:260], ones[0:2, :], both[0:2, :], start=True, stop=True).then_inc(s_mb, 1)


def graph(nc, c):
    misc = Arena(c.misc, 3100)
    rows = [misc.take(D) for _ in range(UG)]
    hot = [misc.take(P) for _ in range(UG)]
    rec, rec_f = matrix(c.rec[:, :], ET, W), matrix(c.rec[:, :].bitcast(F32), ET, W)
    groups, LEAD = ET // UG, UG // 2
    s_rec, s_idx, s_hot, s_mm, s_add, s_blk, s_g = (c.sem("graph_" + n) for n in ("rec", "idx", "hot", "mm", "add", "blk", "gpsimd"))
    s_row = [c.sem(f"graph_row{k}") for k in range(UG)]
    idx, spare = c.idx, c.spare
    with nc.Block() as block:
        @block.sync
        def _(e):
            e.dma_start(c.rec[:, :], c.rec_d.rearrange("(p t) w -> p (t w)", p=P)).then_inc(s_rec, 16)
            e.dma_start(c.pos[0:1, :], c.blk_d).then_inc(s_blk, 16)

        @block.scalar
        def _(e):
            e.wait_ge(s_rec, 16)
            e.copy(idx[0], rec[:, 0:UG, 0]).then_inc(s_idx, 1)
            e.copy(idx[1], rec[:, UG:2 * UG, 0]).then_inc(s_idx, 1)
            with e.Fori(1, groups // 2) as j:
                for u in range(2):
                    q = j * 2 + u
                    e.wait_ge(s_mm, (q - 1) * UG)
                    e.copy(idx[u], rec[:, bass.ds(q * UG, UG), 0]).then_inc(s_idx, 1)

        def gather(e, g, q, u, h, first=False):
            e.wait_ge(s_idx, q + 1)
            if not first:
                e.wait_ge(s_mm, q * UG + (h - 1) * LEAD)
            carry(e, g, spare)
            for k in range(h * LEAD, (h + 1) * LEAD):
                e.indirect_dma_start(out=rows[k], out_offset=None, in_=c.z_d,
                                     in_offset=bass.IndirectOffsetOnAxis(ap=idx[u][:, k:k + 1], axis=0)).then_inc(s_row[k], 16)

        @block.gpsimd
        def _(e):
            g = Chain(e, s_g)
            gather(e, g, 0, 0, 0, True)
            gather(e, g, 0, 0, 1, True)
            gather(e, g, 1, 1, 0)
            gather(e, g, 1, 1, 1)
            with e.Fori(1, groups // 2) as j:
                g.enter(j - 1, 4)
                for u in range(2):
                    for h in range(2):
                        gather(e, g, j * 2 + u, u, h)
            g.leave(groups // 2 - 1)

        def one_hot(e, t, k):
            e.tensor_scalar(hot[k], c.column, rec_f[:, bass.ds(t, 1), 1], rec_f[:, bass.ds(t, 1), 2],
                            ALU.is_equal, ALU.mult).then_inc(s_hot, 1)

        @block.vector
        def _(e):
            e.wait_ge(s_rec, 16)
            e.wait_ge(s_blk, 16)
            for k in range(LEAD):
                one_hot(e, k, k)

            def group(q, more=True):
                _, blocks = nc.values_load_multi_w_load_instructions(
                    c.pos[0:1, bass.ds(q * UG, UG)], engines=[mybir.EngineType.DVE], min_val=0, max_val=NT - 1)
                for k in range(UG):
                    if more or k < UG - LEAD:
                        one_hot(e, q * UG + k + LEAD, (k + LEAD) % UG)
                    rows_of = c.acc3[:, bass.ds(blocks[k], 1), :]
                    e.wait_ge(s_mm, q * UG + k + 1)
                    e.tensor_tensor(rows_of, rows_of, c.bank[k][:, 0:D].rearrange("p (a d) -> p a d", a=1), ALU.add).then_inc(s_add, 1)
                    e.wait_ge(s_add, q * UG + k + 1)
            with e.Fori(0, groups - 1) as q:
                group(q)
            group(groups - 1, False)

        @block.tensor
        def _(e):
            with e.Fori(0, groups) as q:
                for k in range(UG):
                    e.wait_ge(s_hot, q * UG + k + 1)
                    e.wait_ge(s_row[k], 16 * (q + 1))
                    e.matmul(c.bank[k][:, 0:D], hot[k], rows[k], start=True, stop=True).then_inc(s_mm, 1)


def route(nc, c, A):
    misc, more, pos = Arena(c.misc, 3100), Arena(c.rec, ET * W), Arena(c.pos, ET)
    more.t = c.rec[:, :].bitcast(F32)
    pos.t = c.pos[:, :].bitcast(F32)
    c.prob = [pos.take(NT) for _ in range(TOP)]
    c.slot = [pos.take(NT, I32) for _ in range(TOP)]
    c.expert = pos.take(MT, I32)
    st = matrix(more.take(NT * 6), NT, 6)
    mean, var, std, rstd = (more.take(NT) for _ in range(4))
    scores = matrix(more.take(NT * NE), NT, NE)
    shared = more.at
    wg = matrix(more.take(DH * NE), DH, NE)
    bg, ones = more.take(NE), more.take(P)
    xn = [misc.take(D) for _ in range(2)]
    xT = [matrix(misc.take(D), DH, P) for _ in range(2)]
    tok = [misc.take(2 * D, F16) for _ in range(2)]
    S = lambda name: c.sem("route_" + name)
    s_w, s_v, s_var, s_std, s_ones, s_xn, s_tr, s_xt, s_gate, s_hi, s_lo = map(S, (
        "weights", "vector", "var", "std", "ones", "xn", "tr", "xt", "gate", "hi", "lo"))
    s_st = [S("store0"), S("store1")]
    tr_ps, g_ps = [c.bank[4], c.bank[5]], [c.bank[0], c.bank[1]]

    def norm(e, s):
        if not s.fresh:
            e.wait_ge(s_tr, s.i - 1)
            e.wait_ge(s_lo, s.i - 1)
        e.tensor_scalar(xn[s.u], c.acc3[:, bass.ds(s.i, 1), :], mean[:, bass.ds(s.i, 1)], rstd[:, bass.ds(s.i, 1)],
                        ALU.subtract, ALU.mult).then_inc(s_xn, 1)

    def turn(e, s):
        e.wait_ge(s_xn, s.i + 1)
        if not s.fresh:
            e.wait_ge(s_xt, s.i - 1)
        for h in range(DH):
            l = e.transpose(tr_ps[s.u][:, h * P:h * P + P], xn[s.u][:, h * P:h * P + P], c.ident)
        l.then_inc(s_tr, 1)

    def gate(e, s):
        if s.more:
            turn(e, s.next())
        e.wait_ge(s_xt, s.i + 1)
        if not s.fresh:
            e.wait_ge(s_lo, s.i - 1)
        for h in range(DH):
            e.matmul(g_ps[s.u][:, 0:NE], xT[s.u][:, h, :], wg[:, h, :], start=h == 0, stop=False)
        e.matmul(g_ps[s.u][:, 0:NE], ones[0:1, :], bg[0:1, :], start=False, stop=True).then_inc(s_gate, 1)

    with nc.Block() as block:
        @block.sync
        def _(e):
            e.dma_start(wg, A["gate_wT"]).then_inc(s_w, 16)
            e.dma_start(bg[0:1, :], A["gate_b"]).then_inc(s_w, 16)

            def store(s):
                e.wait_ge(s_lo, s.i + 1)
                e.dma_start(c.tok_d[bass.ds(s.i * P, P), :], tok[s.u]).then_inc(s_st[s.u], 16)
            paired(e, NT, store)
            e.wait_ge(s_st[0], 16 * (NT // 2 + 1))
            e.wait_ge(s_st[1], 16 * (NT // 2))

        @block.vector
        def _(e):
            v = Chain(e, s_v)
            e.memset(ones, 1.0).then_inc(s_ones, 1)
            stats(e, v, c, st, mean, var, s_var)
            e.wait_ge(s_std, 1)
            v.link(e.reciprocal(rstd, std))
            norm(e, Step(0, 0))

            def pick(s):
                if s.more:
                    norm(e, s.next())
                e.wait_ge(s_gate, s.i + 1)
                v.add(e.tensor_copy(scores[:, bass.ds(s.i, 1), :], g_ps[s.u][:, 0:NE].rearrange("p (a t) -> p a t", a=1)))
                e.wait_ge(s_hi, s.i + 1)
                e.tensor_tensor(tok[s.u][:, D:2 * D], xn[s.u], tok[s.u][:, 0:D], ALU.subtract).then_inc(s_lo, 1)
            paired(e, NT, pick, v, 1)

        @block.scalar
        def _(e):
            e.wait_ge(s_var, 1)
            e.activation(std, var, ACT.Sqrt).then_inc(s_std, 1)

            def copies(s):
                e.wait_ge(s_tr, s.i + 1)
                if not s.fresh:
                    e.wait_ge(s_gate, s.i - 1)
                e.copy(xT[s.u], matrix(tr_ps[s.u][:, 0:D], DH, P)).then_inc(s_xt, 1)
                if not s.fresh:
                    e.wait_ge(s_st[s.u], 16 * s.j)
                e.copy(tok[s.u][:, 0:D], xn[s.u]).then_inc(s_hi, 1)
            paired(e, NT, copies)

        @block.tensor
        def _(e):
            e.wait_ge(s_w, 32)
            e.wait_ge(s_ones, 1)
            turn(e, Step(0, 0))
            paired(e, NT, lambda s: gate(e, s))

    misc.at = 0
    more.at = shared
    share = matrix(more.take(NT * NE), NT, NE)
    hot = [matrix(more.take(NT * NE), NT, NE) for _ in range(TOP)]
    mask16 = matrix(more.take(NE * NT, F16), NE, NT)
    ones16 = more.take(P, F16)
    slots, after = matrix(misc.take(NE * NT), NE, NT), matrix(misc.take(NE * NT), NE, NT)
    by_token = matrix(misc.take(NT * NE), NT, NE)
    ones_row = misc.take(NE * NT)
    slot_f = [misc.take(NT) for _ in range(TOP)]
    last_e, past, tiles, ends, shift = (misc.take(NE) for _ in range(5))
    tiles_i = misc.take(2 * NE, I32)
    begun = matrix(misc.take(MT * (NE - 1)), MT, NE - 1)
    order = misc.take(MT)
    gap, ex, total = (more.take(NT) for _ in range(3))
    best = [more.take(NT) for _ in range(TOP)]
    rank_of = more.take(NE)
    lead = more.take(NT)
    above, sums = matrix(c.bank[0][:, 0:NE * NT], NE, NT), matrix(c.bank[1][:, 0:NE * NT], NE, NT)
    flat = lambda a: a.rearrange("p a b -> p (a b)")
    turned = lambda a: a.rearrange("p a b -> p b a")
    col = lambda a: a.rearrange("p (t a) -> p t a", a=1)
    s_c, s_mask, s_cnt, s_gap, s_ex = map(S, ("chain2", "mask", "counts", "gap", "ex"))
    with nc.Block() as block:
        @block.vector
        def _(e):
            v = Chain(e, s_c)
            v.add(e.memset(ones16, 1.0))
            v.add(e.memset(ones_row, 1.0))
            v.add(e.memset(past, 0.0))
            v.link(e.tensor_scalar(rank_of, c.column[:, 0:NE], -1.0, float(NE), ALU.mult, ALU.add))
            wide = [P, NT, NE]
            for k in range(TOP):
                v.link(e.tensor_reduce(best[k], scores, AX.X, ALU.max))
                v.link(e.tensor_tensor(hot[k], scores, col(best[k]).to_broadcast(wide), ALU.is_equal))
                v.link(e.tensor_tensor(by_token, hot[k], rank_of.rearrange("p (a e) -> p a e", a=1).to_broadcast(wide), ALU.mult))
                v.link(e.tensor_reduce(lead, by_token, AX.X, ALU.max))
                v.link(e.tensor_tensor(hot[k], by_token, col(lead).to_broadcast(wide), ALU.is_equal))
                if k == 0:
                    v.link(e.scalar_tensor_tensor(out=scores, in0=hot[0], scalar=-3e38, in1=scores, op0=ALU.mult, op1=ALU.add))
            e.tensor_tensor(gap, best[1], best[0], ALU.subtract).then_inc(s_gap, 1)
            for k in range(TOP):
                v.add(e.tensor_scalar(hot[k][:, NT - 1, :], hot[k][:, NT - 1, :], c.valid, None, ALU.mult))
            v.sync()
            e.tensor_tensor(turned(mask16), hot[0], hot[1], ALU.add).then_inc(s_mask, 1)
            e.wait_ge(s_ex, 1)
            v.link(e.tensor_scalar(total, ex, 1.0, None, ALU.add))
            v.link(e.reciprocal(c.prob[0], total))
            v.link(e.tensor_tensor(c.prob[1], ex, c.prob[0], ALU.mult))
            v.add(e.tensor_tensor(share, hot[0], col(c.prob[0]).to_broadcast([P, NT, NE]), ALU.mult))
            v.link(e.tensor_tensor(by_token, hot[1], col(c.prob[1]).to_broadcast([P, NT, NE]), ALU.mult))
            v.link(e.tensor_tensor(share, share, by_token, ALU.add))
            e.wait_ge(s_cnt, 1)
            v.link(e.tensor_tensor_scan(flat(after), ones_row, flat(sums), 0.0, ALU.mult, ALU.add))
            v.add(e.tensor_copy(last_e, after[:, :, NT - 1]))
            v.link(e.tensor_copy(past[:, 1:NE], after[:, 0:NE - 1, NT - 1]))
            v.add(e.tensor_tensor(slots, after, sums, ALU.subtract))
            v.link(e.tensor_tensor(tiles, last_e, past, ALU.subtract))
            v.link(e.tensor_tensor(slots, slots, above, ALU.add))
            v.link(e.tensor_scalar(tiles_i[:, 0:NE], tiles, P - 1.0, None, ALU.add))
            v.link(e.tensor_scalar(tiles_i[:, NE:2 * NE], tiles_i[:, 0:NE], 7, None, ALU.logical_shift_right))
            v.link(e.tensor_copy(tiles, tiles_i[:, NE:2 * NE]))
            v.link(e.tensor_tensor_scan(ends, ones_row[:, 0:NE], tiles, 0.0, ALU.mult, ALU.add))
            v.link(e.tensor_tensor(shift, ends, tiles, ALU.subtract))
            v.link(e.scalar_tensor_tensor(out=shift, in0=shift, scalar=float(P), in1=past, op0=ALU.mult, op1=ALU.subtract))
            v.link(e.tensor_tensor(slots, slots, col(shift).to_broadcast([P, NE, NT]), ALU.add))
            for k in range(TOP):
                v.link(e.tensor_tensor(by_token, hot[k], turned(slots), ALU.mult))
                v.link(e.tensor_reduce(slot_f[k], by_token, AX.X, ALU.add))
                v.link(e.tensor_copy(c.slot[k], slot_f[k]))
            v.link(e.tensor_tensor(begun, col(c.column[:, 0:MT]).to_broadcast([P, MT, NE - 1]),
                                   ends[:, 0:NE - 1].rearrange("p (a e) -> p a e", a=1).to_broadcast([P, MT, NE - 1]), ALU.is_ge))
            v.link(e.tensor_reduce(order, begun, AX.X, ALU.add))
            v.link(e.tensor_copy(c.expert, order))

        @block.scalar
        def _(e):
            e.wait_ge(s_gap, 1)
            e.activation(ex, gap, ACT.Exp).then_inc(s_ex, 1)

        @block.tensor
        def _(e):
            e.wait_ge(s_mask, 1)
            e.wait_ge(s_c, 1)
            e.matmul(flat(above), c.before, flat(mask16), start=True, stop=True)
            e.matmul(flat(sums), ones16, flat(mask16), start=True, stop=True).then_inc(s_cnt, 1)

    misc.at = 0
    tok = [misc.take(2 * D, F16) for _ in range(2)]
    b2 = misc.take(D)
    cb = [misc.take(NE) for _ in range(2)]
    cbT = [misc.take(P) for _ in range(2)]
    to = [misc.take(TOP, I32) for _ in range(2)]
    s_b2, s_g, s_cb, s_ct, s_cbT, s_b, s_acc = map(S, ("b2", "gpsimd", "cb", "ct", "cbT", "b", "acc"))
    s_tok, s_sc = [S("tok0"), S("tok1")], [S("scatter0"), S("scatter1")]
    ct_ps, b_ps = [c.bank[2], c.bank[3]], [c.bank[6], c.bank[7]]
    with nc.Block() as block:
        @block.sync
        def _(e):
            e.dma_start(b2[0:NE, :], A["b2"]).then_inc(s_b2, 16)

            def load(s):
                if not s.fresh:
                    e.wait_ge(s_sc[s.u], 16 * TOP * s.j)
                e.dma_start(tok[s.u], c.tok_d[bass.ds(s.i * P, P), :]).then_inc(s_tok[s.u], 16)
            paired(e, NT, load)

        @block.gpsimd
        def _(e):
            g = Chain(e, s_g)

            def scatter(s):
                if not s.fresh:
                    e.wait_ge(s_sc[s.u], 16 * TOP * s.j)
                for k in range(TOP):
                    g.add(e.tensor_copy(to[s.u][:, k:k + 1], c.slot[k][:, bass.ds(s.i, 1)]))
                e.wait_ge(s_tok[s.u], 16 * (s.j + 1))
                carry(e, g, c.spare)
                rows = P if s.more else TAIL
                for k in range(TOP):
                    e.indirect_dma_start(out=c.slot_d, out_offset=bass.IndirectOffsetOnAxis(ap=to[s.u][0:rows, k:k + 1], axis=0),
                                         in_=tok[s.u][0:rows, :], in_offset=None).then_inc(s_sc[s.u], 16)
            paired(e, NT, scatter, g, 3)
            e.wait_ge(s_sc[0], 16 * TOP * (NT // 2 + 1))
            e.wait_ge(s_sc[1], 16 * TOP * (NT // 2))

        @block.scalar
        def _(e):
            def copies(s):
                if not s.fresh:
                    e.wait_ge(s_ct, s.i - 1)
                e.copy(cb[s.u].rearrange("p (a n) -> p a n", a=1), share[:, bass.ds(s.i, 1), :]).then_inc(s_cb, 1)
                if not s.fresh:
                    e.wait_ge(s_b, s.i - 1)
                e.wait_ge(s_ct, s.i + 1)
                e.copy(cbT[s.u][0:NE, :], ct_ps[s.u][0:NE, 0:P]).then_inc(s_cbT, 1)
            paired(e, NT, copies)

        @block.tensor
        def _(e):
            e.wait_ge(s_b2, 16)

            def bias(s):
                e.wait_ge(s_cb, s.i + 1)
                if not s.fresh:
                    e.wait_ge(s_cbT, s.i - 1)
                e.transpose(ct_ps[s.u][0:NE, 0:P], cb[s.u], c.ident).then_inc(s_ct, 1)
                e.wait_ge(s_cbT, s.i + 1)
                if not s.fresh:
                    e.wait_ge(s_acc, s.i - 1)
                e.matmul(b_ps[s.u][:, 0:D], cbT[s.u][0:NE, :], b2[0:NE, :], start=True, stop=True).then_inc(s_b, 1)
            paired(e, NT, bias)

        @block.vector
        def _(e):
            def add(s):
                e.wait_ge(s_b, s.i + 1)
                tile = c.acc3[:, bass.ds(s.i, 1), :]
                e.tensor_tensor(tile, tile, b_ps[s.u][:, 0:D].rearrange("p (a d) -> p a d", a=1), ALU.add).then_inc(s_acc, 1)
            paired(e, NT, add)


def experts(nc, c, A):
    misc, more = Arena(c.misc, 3100), Arena(c.rec, ET * W)
    more.t = c.rec[:, :].bitcast(F32)
    xs = [misc.take(2 * D, F16) for _ in range(2)]
    xT = [matrix(misc.take(2 * D, F16), 2 * DH, P) for _ in range(2)]
    y = [misc.take(D) for _ in range(2)]
    bias = misc.take(H, F16)
    select = misc.take(NE * P, F16)
    high, low = ([matrix(more.take(H, F16), HB, P) for _ in range(2)] for _ in range(2))
    bias_f = more.take(H)
    S = lambda name: c.sem("experts_" + name)
    s_b, s_b0, s_bh, s_bias, s_sel, s_tr, s_xt, s_h, s_high, s_low, s_y, s_out = map(S, (
        "b1", "b1_0", "b1_high", "bias", "select", "tr", "xt", "h", "high", "low", "y", "out"))
    s_xs, s_ys = [S("xs0"), S("xs1")], [S("ystore0"), S("ystore1")]
    tr_ps = [matrix(c.bank[u][:, 0:D].bitcast(F16), 2 * DH, P) for u in range(2)]
    h_ps = [matrix(c.wide[1 + u], HB, P) for u in range(2)]
    y_ps = [c.bank[6], c.bank[7]]
    half = HB // 2
    (w1h, w1l), (w2h, w2l) = c.w

    def turn(e, s):
        e.wait_ge(s_xs[s.u], 16 * (s.j + 1))
        if not s.fresh:
            e.wait_ge(s_xt, s.i - 1)
        for n in range(2 * DH):
            l = e.transpose(tr_ps[s.u][:, n, :], xs[s.u][:, n * P:n * P + P], c.ident16)
        l.then_inc(s_tr, 1)

    def expert(s):
        return nc.values_load(c.expert[0:1, bass.ds(s.i, 1)], engines=[mybir.EngineType.PE], min_val=0, max_val=NE - 1)

    def first(e, s):
        x = expert(s)
        e.wait_ge(s_xt, s.i + 1)
        for m in range(HB):
            if not s.fresh and m % half == 0:
                e.wait_ge(s_low, 2 * s.i - 3 + m // half)
            o = h_ps[s.u][:, m, :]
            e.matmul(o, bias[:, m * P:m * P + P], select[:, bass.ds(x * P, P)], start=True, stop=False)
            for h in range(DH):
                at = bass.ds(x * H + (h * NE * H + m * P), P)
                e.matmul(o, w1h[:, at], xT[s.u][:, h, :], start=False, stop=False)
                e.matmul(o, w1h[:, at], xT[s.u][:, DH + h, :], start=False, stop=False)
                l = e.matmul(o, w1l[:, at], xT[s.u][:, h, :], start=False, stop=h == DH - 1)
            if m % half == half - 1:
                l.then_inc(s_h, 1)

    def second(e, s):
        x = expert(s)
        e.wait_ge(s_low, 2 * s.i + 2)
        if not s.fresh:
            e.wait_ge(s_y, s.i - 1)
        for m in range(HB):
            at = bass.ds(x * D + m * NE * D, D)
            o = y_ps[s.u][:, 0:D]
            e.matmul(o, high[s.u][:, m, :], w2h[:, at], start=m == 0, stop=False)
            e.matmul(o, high[s.u][:, m, :], w2l[:, at], start=False, stop=False)
            l = e.matmul(o, low[s.u][:, m, :], w2h[:, at], start=False, stop=m == HB - 1)
        l.then_inc(s_out, 1)

    def relu(e, s):
        for n in range(2):
            e.wait_ge(s_h, 2 * s.i + 1 + n)
            if not s.fresh and n == 0:
                e.wait_ge(s_out, s.i - 1)
            part = slice(n * half, (n + 1) * half)
            e.activation(high[s.u][:, part, :], h_ps[s.u][:, part, :], ACT.Relu).then_inc(s_high, 1)

    def result(e, s):
        e.wait_ge(s_out, s.i + 1)
        if not s.fresh:
            e.wait_ge(s_ys[s.u], 16 * s.j)
        e.activation(y[s.u], y_ps[s.u][:, 0:D], ACT.Copy, scale=c.descale[:, 1:2]).then_inc(s_y, 1)

    with nc.Block() as block:
        @block.sync
        def _(e):
            e.wait_ge(s_b0, 1)
            e.dma_start(bias_f[0:NE, :], A["b1"]).then_inc(s_b, 16)
            e.dma_start(bias_f[32:32 + NE, :], A["b1"]).then_inc(s_b, 16)

            def load(s):
                if not s.fresh:
                    e.wait_ge(s_tr, s.i - 1)
                e.dma_start(xs[s.u], c.slot_d[bass.ds(s.i * P, P), :]).then_inc(s_xs[s.u], 16)
            paired(e, MT, load)

        @block.gpsimd
        def _(e):
            e.memset(select, 0.0).then_inc(s_sel, 1)
            e.wait_ge(s_sel, 1)
            for n, base in enumerate((0, -32)):
                e.affine_select(out=matrix(select, NE, P), in_=matrix(select, NE, P), compare_op=ALU.not_equal, fill=1.0,
                                base=base, pattern=[[-1, NE], [0, P]], channel_multiplier=1).then_inc(s_sel, 1)
                e.wait_ge(s_sel, n + 2)

            def store(s):
                e.wait_ge(s_y, s.i + 1)
                e.dma_start(c.y_d[bass.ds(s.i * P, P), :], y[s.u]).then_inc(s_ys[s.u], 16)
            paired(e, MT, store)
            e.wait_ge(s_ys[0], 16 * (MT // 2 + 1))
            e.wait_ge(s_ys[1], 16 * (MT // 2))

        @block.scalar
        def _(e):
            e.wait_ge(s_b, 32)
            e.wait_ge(s_b0, 2)
            e.activation(bias[0:NE, :], bias_f[0:NE, :], ACT.Copy, scale=c.scale[0:NE, 0:1]).then_inc(s_bh, 1)
            e.activation(bias[32:32 + NE, :], bias_f[32:32 + NE, :], ACT.Copy, scale=c.scale[32:32 + NE, 0:1]).then_inc(s_bh, 1)

            def step(s):
                e.wait_ge(s_tr, s.i + 1)
                if not s.fresh:
                    e.wait_ge(s_h, 2 * s.i - 2)
                e.copy(xT[s.u], tr_ps[s.u]).then_inc(s_xt, 1)
                if not s.zero:
                    relu(e, s.prev())
                    if not s.first2:
                        result(e, s.prev().prev())
            paired(e, MT, step)
            relu(e, Step(MT // 2, 0))
            result(e, Step(MT // 2 - 1, 1))
            result(e, Step(MT // 2, 0))

        @block.vector
        def _(e):
            e.memset(bias_f, 0.0).then_inc(s_b0, 1)
            e.memset(bias, 0.0).then_inc(s_b0, 1)
            e.wait_ge(s_bh, 2)
            e.scalar_tensor_tensor(out=bias[32:32 + NE, :], in0=bias_f[32:32 + NE, :], scalar=c.scale[32:32 + NE, 0:1],
                                   in1=bias[32:32 + NE, :], op0=ALU.mult, op1=ALU.subtract).then_inc(s_bias, 1)

            def rest(s):
                for n in range(2):
                    e.wait_ge(s_high, 2 * s.i + 1 + n)
                    if not s.fresh and n == 0:
                        e.wait_ge(s_out, s.i - 1)
                    part = slice(n * half, (n + 1) * half)
                    e.scalar_tensor_tensor(out=low[s.u][:, part, :], in0=h_ps[s.u][:, part, :], scalar=0.0,
                                           in1=high[s.u][:, part, :], op0=ALU.max, op1=ALU.subtract).then_inc(s_low, 1)
            paired(e, MT, rest)

        @block.tensor
        def _(e):
            e.wait_ge(s_bias, 1)
            e.wait_ge(s_sel, 3)
            turn(e, Step(0, 0))

            def step(s):
                if s.more:
                    turn(e, s.next())
                first(e, s)
                if not s.zero:
                    second(e, s.prev())
            paired(e, MT, step)
            second(e, Step(MT // 2, 0))


def combine(nc, c, out):
    misc = Arena(c.misc, 3100)
    ys = [[misc.take(D) for _ in range(TOP)] for _ in range(2)]
    o, first = ([misc.take(D) for _ in range(2)] for _ in range(2))
    at = [misc.take(TOP, I32) for _ in range(2)]
    S = lambda name: c.sem("combine_" + name)
    s_g, s_v, s_o = map(S, ("gpsimd", "vector", "o"))
    s_y, s_st = [S("y0"), S("y1")], [S("store0"), S("store1")]
    one = lambda a: a.rearrange("p (a d) -> p a d", a=1)
    with nc.Block() as block:
        @block.gpsimd
        def _(e):
            g = Chain(e, s_g)

            def gather(s):
                if not s.fresh:
                    e.wait_ge(s_o, s.i - 1)
                for k in range(TOP):
                    g.add(e.tensor_copy(at[s.u][:, k:k + 1], c.slot[k][:, bass.ds(s.i, 1)]))
                carry(e, g, c.spare)
                for k in range(TOP):
                    e.indirect_dma_start(out=ys[s.u][k], out_offset=None, in_=c.y_d,
                                         in_offset=bass.IndirectOffsetOnAxis(ap=at[s.u][:, k:k + 1], axis=0)).then_inc(s_y[s.u], 16)
            paired(e, NT, gather, g, 3)

        @block.vector
        def _(e):
            v = Chain(e, s_v)

            def add(s):
                e.wait_ge(s_y[s.u], 16 * TOP * (s.j + 1))
                v.link(e.scalar_tensor_tensor(out=one(first[s.u]), in0=one(ys[s.u][0]), scalar=c.prob[0][:, bass.ds(s.i, 1)],
                                              in1=c.acc3[:, bass.ds(s.i, 1), :], op0=ALU.mult, op1=ALU.add))
                if not s.fresh:
                    e.wait_ge(s_st[s.u], 16 * s.j)
                e.scalar_tensor_tensor(out=o[s.u], in0=ys[s.u][1], scalar=c.prob[1][:, bass.ds(s.i, 1)],
                                       in1=first[s.u], op0=ALU.mult, op1=ALU.add).then_inc(s_o, 1)
            paired(e, NT, add, v, 1)

        @block.sync
        def _(e):
            def store(s):
                e.wait_ge(s_o, s.i + 1)
                if s.more:
                    e.dma_start(out[bass.ds(s.i * P, P), :], o[s.u]).then_inc(s_st[s.u], 16)
                else:
                    e.dma_start(out[N - TAIL:N, :], o[s.u][0:TAIL, :]).then_inc(s_st[s.u], 16)
            paired(e, NT, store)
            e.wait_ge(s_st[0], 16 * (NT // 2 + 1))
            e.wait_ge(s_st[1], 16 * (NT // 2))


_INS = ["x", "src", "dst", "edge_weight", "gnn_wT", "gnn_b", "q_wT", "kv_wT", "proj_wT", "proj_b",
        "gate_wT", "gate_b", "w1T", "b1", "w2T", "b2"]


def kernel(**inputs):
    import numpy as _np
    import concourse.bacc as _bacc
    from concourse import mybir as _mybir
    from concourse.bass_utils import run_bass_kernel_spmd as _run

    a = {k.replace("L0_", ""): _np.asarray(v) for k, v in inputs.items()}
    rows = lambda w: w.reshape(DH, P, -1).transpose(1, 0, 2)
    lay = {"x": a["x"], "src": a["src"], "dst": a["dst"], "edge_weight": a["edge_weight"],
           "gnn_wT": rows(a["gnn_W"].T), "gnn_b": a["gnn_b"].reshape(1, D),
           "q_wT": rows(a["mix_Wq"].T), "kv_wT": rows(a["mix_Wkv"].T),
           "proj_wT": rows(a["mix_Wproj"].T), "proj_b": a["mix_bproj"].reshape(1, D),
           "gate_wT": rows(a["ffn_Wg"].T), "gate_b": a["ffn_bg"].reshape(1, NE),
           "w1T": a["ffn_W1"].transpose(2, 0, 1).reshape(DH, P, NE * H).transpose(1, 0, 2),
           "b1": a["ffn_b1"],
           "w2T": a["ffn_W2"].transpose(2, 0, 1).reshape(HB, P, NE * D).transpose(1, 0, 2),
           "b2": a["ffn_b2"]}
    nc = _bacc.Bacc("TRN2", target_bir_lowering=False, num_devices=1)
    arrays, args = {}, {}
    for name in _INS:
        arrays["in_" + name] = _np.ascontiguousarray(lay[name])
        args[name] = nc.dram_tensor("in_" + name, lay[name].shape, _mybir.dt.from_np(lay[name].dtype),
                                    kind="ExternalInput").ap()
    out = nc.dram_tensor("out0", (N, D), F32, kind="ExternalOutput").ap()
    build(nc, args, out, STAGE)
    return _run(nc, [arrays], core_ids=[0]).results[0]["out0"]


STAGE = 4
```

```python
import numpy as np
import concourse.bass as bass
from concourse import mybir
from contextlib import ExitStack

F32, F16, I32, U32, U16 = (mybir.dt.float32, mybir.dt.float16, mybir.dt.int32, mybir.dt.uint32, mybir.dt.uint16)
ALU = mybir.AluOpType
ACT = mybir.ActivationFunctionType
AX = mybir.AxisListType

P = 128
N, D = 6250, 256
NT = -(-N // P)
TAIL = N - (NT - 1) * P
NP = NT * P
E = 100000
EF = E // P
EC = EF + 1
ER = E - EF * P
ETM = (E + NT * (P - 1)) // P
UG, HG, QG = 12, 6, 6
ET = -(-ETM // (2 * UG)) * 2 * UG
W = 3
US = 17
assert EC % (2 * US) == 0
NE, H, TOP = 8, 1024, 2
MT = (TOP * N + NE * (P - 1)) // P
HB = H // P
DH = D // P
HEAD = 32
EPS = 1e-5
DEN_MIN = 1e-6
MISC = 3924
CH = DH * NE * H // 1024


class Arena:

    def __init__(self, t, cols):
        self.t, self.at, self.cols = t, 0, cols

    def take(self, n, dt=F32):
        words = n if dt in (F32, I32, U32) else -(-n // 2)
        words += words % 2
        a = self.t[:, self.at:self.at + words]
        self.at += words
        assert self.at <= self.cols, (self.at, self.cols)
        return (a if dt == F32 else a.bitcast(dt))[:, 0:n]


class Core:
    pass


def matrix(a, n, m):
    return a.rearrange("p (n m) -> p n m", n=n, m=m)


class Chain:

    def __init__(self, e, sem):
        self.e, self.sem, self.n, self.k = e, sem, 0, 0

    def enter(self, i, per):
        self.before = self.n + self.k
        self.n, self.k, self.per = self.before + i * per, 0, per

    def leave(self, trips):
        assert self.k == self.per, (self.k, self.per)
        self.n, self.k = self.before + trips * self.per, 0

    def add(self, ins):
        self.k += 1
        ins.then_inc(self.sem, 1)

    def sync(self):
        self.e.wait_ge(self.sem, self.n + self.k)

    def link(self, ins):
        self.add(ins)
        self.sync()


def build(nc, A, out, stage=9):
    ctx = ExitStack()
    with ctx:
        c = Core()
        c.sem = lambda name: ctx.enter_context(nc.semaphore(name))
        sb = lambda name, n, dt=F32: ctx.enter_context(nc.sbuf_tensor(name, [P, n], dt))
        c.acc = sb("acc", NT * D)
        c.big = sb("big", 4 * 8192)
        c.rec = sb("rec", ET * W, I32)
        c.pos = sb("pos", ET, I32)
        c.misc = sb("misc", MISC)
        k = Arena(sb("consts", 424), 424)
        c.ident = k.take(P)
        c.ident16 = k.take(P, F16)
        c.before = k.take(P, F16)
        c.column = k.take(P)
        c.idx = [k.take(UG, I32) for _ in range(2)]
        c.spare = k.take(8)
        c.valid = k.take(1)
        c.scale = k.take(2)
        c.descale = k.take(2)
        ps = ctx.enter_context(nc.psum_tensor("ps", [P, 8 * 512], F32))
        c.bank = [ps[:, 512 * i:512 * i + 512] for i in range(8)]
        c.wide = [ps[:, 1024 * i:1024 * i + 1024] for i in range(4)]
        wide16 = c.big[:, :].bitcast(F16)
        c.w1 = [wide16[:, part * 16384:(part + 1) * 16384] for part in range(2)]
        c.w2 = wide16[:, 32768:65536]
        c.w2_parts = c.w2.rearrange("p (n a d) -> p n a d", a=2, d=D)
        c.acc3 = matrix(c.acc[:, :], NT, D)
        dram = lambda name, shape, dt=F32: nc.dram_tensor(name, shape, dt).ap()
        c.rec_d = dram("rec_d", (P * ET, W), I32)
        c.blk_d = dram("blk_d", (1, ET), I32)
        c.z_d = dram("z_d", (NP, D))
        c.tok_d = dram("tok_d", (NP, 2 * D), F16)
        c.y_d = dram("y_d", (TOP * NP + MT * P, D))
        rank(nc, c, A)
        if stage >= 2:
            mix(nc, c, A)
        if stage >= 3:
            graph(nc, c)
        if stage >= 4:
            route(nc, c, A)
            experts(nc, c, A)
            combine(nc, c, A, out)
        else:
            dump(nc, c, out, stage)


def dump(nc, c, out, stage):
    s = c.sem("dump")
    with nc.Block() as block:
        @block.sync
        def _(e):
            if stage == 1:
                e.dma_start(out[0:512, :].rearrange("(p a) d -> p (a d)", p=P)[:, 0:782], c.pos[:, 0:782].bitcast(F32)).then_inc(s, 16)
                e.wait_ge(s, 16)
            else:
                e.dma_start(out[0:(NT - 1) * P, :].rearrange("(t p) d -> p t d", p=P), c.acc3[:, 0:NT - 1, :]).then_inc(s, 16)
                e.wait_ge(s, 16)
                e.dma_start(out[(NT - 1) * P:N, :], c.acc3[0:TAIL, NT - 1, :]).then_inc(s, 16)
                e.wait_ge(s, 32)


def rank(nc, c, A):
    big, acc = Arena(c.big, 32768), Arena(c.acc, NT * D)
    onehot = matrix(big.take(NT * EC, F16), NT, EC)
    pick1 = matrix(big.take(NT * P, F16), NT, P)
    pick256 = matrix(big.take(NT * P, F16), NT, P)
    band = big.take(5 * P, F16)
    blanks = matrix(acc.take(ET * W, I32), ET, W)
    src, dst, wgt, blk_i = (acc.take(EC, I32) for _ in range(4))
    blk16 = acc.take(EC, F16)
    ones, upto, base = (acc.take(EC) for _ in range(3))
    base_i, part_i = (acc.take(EC, I32) for _ in range(2))
    lo16, hi16 = (acc.take(EC, F16) for _ in range(2))
    place = big.take(EC)
    number = big.take(64)
    tile_no = big.take(ET)
    tiles_f, start128, end = (big.take(2) for _ in range(3))
    tiles_i = big.take(2, I32)
    started = big.take(ET, F16)
    few = big.take(2, F16)
    before_f = big.take(P)
    blk_row = big.take(ET, I32)
    rec = matrix(c.rec[:, 0:EC * W], EC, W)
    counts, starts, row = c.wide[0], c.bank[2], c.wide[3]
    s_load, s_out = (c.sem("rank_" + n) for n in ("load", "out"))
    s_preset, s_blank, s_k, s_hot, s_cnt, s_til, s_sta, s_end, s_row, s_base, s_pre, s_pos, s_rec, s_c, s_g, s_blkrow = (
        c.sem("rank_" + n) for n in ("preset", "blank", "consts", "hot", "counts", "tiles", "starts",
                                     "end", "row", "base", "prefix", "pos", "rec", "vector", "gpsimd", "blkrow"))
    cols = [(0, 512), (512, EC)]
    inputs = ((src, A["src"]), (dst, A["dst"]), (wgt, A["edge_weight"].bitcast(I32)))
    one = lambda a: a.rearrange("p (a t) -> p a t", a=1)
    def choose(e, b, u):
        e.wait_ge(s_pre, b + 1)
        e.copy_predicated(place, onehot[:, b, :].bitcast(U16), c.wide[u + 1][:, 0:EC]).then_inc(s_pos, 1)
        e.wait_ge(s_pos, b + 1)

    def places(e, b, u, free):
        if free:
            e.wait_ge(s_pos, b - 1)
        for x, y in cols:
            e.matmul(c.wide[u + 1][:, x:y], c.before, onehot[:, bass.ds(b, 1), x:y], start=True, stop=False)
            e.matmul(c.wide[u + 1][:, x:y], pick1[:, bass.ds(b, 1), :], lo16[:, x:y], start=False, stop=False)
            l = e.matmul(c.wide[u + 1][:, x:y], pick256[:, bass.ds(b, 1), :], hi16[:, x:y], start=False, stop=True)
        l.then_inc(s_pre, 1)

    with nc.Block() as block:
        @block.sync
        def _(e):
            for t, a in inputs:
                e.dma_start(t[:, 0:EF], a[0:EF * P].rearrange("(p t) -> p t", p=P)).then_inc(s_load, 16)
            e.wait_ge(s_preset, 3)
            for t, a in inputs:
                e.dma_start(t[0:ER, EF:EC], a[EF * P:E].rearrange("(p t) -> p t", t=1)).then_inc(s_load, 16)
            e.wait_ge(s_blank, 2)
            e.dma_start(c.rec_d.rearrange("(p t) w -> p (t w)", p=P), blanks.rearrange("p t w -> p (t w)")).then_inc(s_out, 16)
            e.wait_ge(s_blkrow, 1)
            e.dma_start(c.blk_d, blk_row[0:1, :]).then_inc(s_out, 16)
            e.wait_ge(s_out, 32)

        @block.gpsimd
        def _(e):
            g = Chain(e, s_g)
            iota = lambda t, n: g.add(e.iota(t, pattern=[[1, n]], base=0, channel_multiplier=0,
                                             allow_small_or_imprecise_dtypes=True))
            select = lambda t, op, base, pattern, by: e.affine_select(
                out=t, in_=t, compare_op=op, fill=0.0, base=base, pattern=pattern, channel_multiplier=by).then_inc(s_k, 1)
            iota(number, 64)
            iota(tile_no, ET)
            iota(c.column, P)
            g.add(e.memset(pick1, 1.0))
            g.add(e.memset(c.ident, 1.0))
            g.add(e.memset(before_f, 1.0))
            g.add(e.memset(few, 1.0))
            g.add(e.memset(band, 0.0))
            g.sync()
            e.memset(band[:, P - 1:P], 1.0).then_inc(s_k, 1)
            select(pick1, ALU.is_equal, 0, [[-1, NT], [0, P]], 1)
            select(c.ident, ALU.is_equal, 0, [[-1, P]], 1)
            select(before_f, ALU.is_gt, 0, [[1, P]], -1)
            select(few, ALU.is_gt, NT - 1, [[0, 2]], -1)
            e.wait_ge(s_load, 96)
            e.tensor_copy(rec[:, :, 0], dst).then_inc(s_rec, 1)
            e.tensor_copy(rec[:, :, 2], wgt).then_inc(s_rec, 1)

        @block.vector
        def _(e):
            v = Chain(e, s_c)
            e.memset(src[:, EF:EC], NP + P).then_inc(s_preset, 1)
            e.memset(dst[:, EF:EC], 0).then_inc(s_preset, 1)
            e.memset(wgt[:, EF:EC], 0).then_inc(s_preset, 1)
            e.memset(blanks, 0).then_inc(s_blank, 1)
            v.add(e.memset(place, 0.0))
            v.add(e.memset(ones, 1.0))
            e.wait_ge(s_blank, 1)
            e.memset(blanks.bitcast(F32)[:, :, 1], -1.0).then_inc(s_blank, 1)
            e.wait_ge(s_k, 5)
            e.tensor_copy(c.ident16, c.ident).then_inc(s_k, 1)
            e.tensor_copy(c.before, before_f).then_inc(s_k, 1)
            e.tensor_scalar(pick256, pick1, 256.0, None, ALU.mult).then_inc(s_k, 1)
            e.wait_ge(s_load, 96)
            v.link(e.tensor_scalar(blk_i, src, 7, None, ALU.logical_shift_right))
            v.link(e.tensor_copy(blk16, blk_i))
            with e.Fori(0, NT // 7) as i:
                for u in range(7):
                    b = i * 7 + u
                    e.tensor_scalar(onehot[:, bass.ds(b, 1), :], one(blk16), number[:, bass.ds(b, 1)], None,
                                    ALU.is_equal).then_inc(s_hot, 1)
            v.link(e.tensor_scalar(part_i, src, P - 1, None, ALU.bitwise_and))
            e.tensor_copy(rec.bitcast(F32)[:, :, 1], part_i).then_inc(s_rec, 1)
            e.wait_ge(s_cnt, 1)
            v.link(e.tensor_tensor_scan(upto, ones, counts[:, 0:EC], 0.0, ALU.mult, ALU.add))
            v.link(e.tensor_scalar(tiles_i[:, 0:1], upto[:, EC - 1:EC], P - 1.0, None, ALU.add))
            v.link(e.tensor_scalar(tiles_i[:, 1:2], tiles_i[:, 0:1], 7, None, ALU.logical_shift_right))
            e.tensor_copy(tiles_f[:, 0:1], tiles_i[:, 1:2]).then_inc(s_til, 1)
            e.wait_ge(s_til, 1)
            e.wait_ge(s_sta, 1)
            v.add(e.tensor_scalar(start128[:, 0:1], starts[:, 0:1], float(P), None, ALU.mult))
            v.link(e.tensor_tensor(end[:, 0:1], starts[:, 0:1], tiles_f[:, 0:1], ALU.add))
            e.tensor_scalar(started, tile_no, end[:, 0:1], None, ALU.is_ge).then_inc(s_end, 1)
            v.link(e.scalar_tensor_tensor(out=base, in0=upto, scalar=start128[:, 0:1], in1=counts[:, 0:EC],
                                          op0=ALU.add, op1=ALU.subtract))
            v.link(e.tensor_copy(base_i, base))
            v.link(e.tensor_scalar(part_i, base_i, 8, None, ALU.logical_shift_right))
            v.link(e.tensor_copy(hi16, part_i))
            v.link(e.tensor_scalar(part_i, base_i, 255, None, ALU.bitwise_and))
            e.tensor_copy(lo16, part_i).then_inc(s_base, 1)
            e.wait_ge(s_row, 1)
            e.tensor_scalar(blk_row[0:1, :], row[0:1, 0:ET], float(D), None, ALU.mult).then_inc(s_blkrow, 1)
            for b in range(NT):
                choose(e, b, b % 2)
            v.link(e.tensor_copy(base_i, place))
            v.add(e.tensor_scalar(part_i, base_i, 7, None, ALU.logical_shift_right))
            v.link(e.tensor_scalar(src, base_i, P - 1, None, ALU.bitwise_and))
            v.link(e.scalar_tensor_tensor(out=c.pos[:, 0:EC], in0=src, scalar=float(ET), in1=part_i,
                                          op0=ALU.mult, op1=ALU.add))

        @block.tensor
        def _(e):
            e.wait_ge(s_k, 8)
            for x, y in cols:
                e.matmul(counts[:, x:y], band[:, P:2 * P], band[:, P:P + y - x], start=True, stop=False)
            with e.Fori(0, NT // 7) as i:
                for u in range(7):
                    b = i * 7 + u
                    e.wait_ge(s_hot, b + 1)
                    for x, y in cols:
                        e.matmul(counts[:, x:y], band[:, bass.ds(P - 1 - b, P)], onehot[:, bass.ds(b, 1), x:y],
                                 start=False, stop=False)
            for x, y in cols:
                l = e.matmul(counts[:, x:y], band[:, P:2 * P], band[:, P:P + y - x], start=False, stop=True)
            l.then_inc(s_cnt, 1)
            e.wait_ge(s_til, 1)
            e.matmul(starts[:, 0:1], before_f, tiles_f[:, 0:1], start=True, stop=True).then_inc(s_sta, 1)
            e.wait_ge(s_end, 1)
            e.matmul(row[0:1, 0:512], few[:, 0:1], started[:, 0:512], start=True, stop=True)
            e.matmul(row[0:1, 512:ET], few[:, 0:1], started[:, 512:ET], start=True, stop=True).then_inc(s_row, 1)
            e.wait_ge(s_base, 1)
            places(e, 0, 0, False)
            places(e, 1, 1, False)
            with e.Fori(1, (NT - 1) // 2) as i:
                for u in range(2):
                    places(e, i * 2 + u, u, True)
            places(e, NT - 1, 0, True)


class Step:

    def __init__(self, j, u, more=True):
        self.j, self.u, self.more, self.i = j, u, more, j * 2 + u
        self.zero = isinstance(j, int) and j == u == 0
        self.fresh = isinstance(j, int) and j == 0
        self.first2 = self.fresh

    def next(self):
        return Step(self.j + self.u, 1 - self.u)

    def later(self, n):
        return Step(self.j + n // 2, self.u)

    def prev(self):
        return Step(self.j - 1 + self.u, 1 - self.u)


def paired(e, steps, body, chain=None, per=0):
    assert steps % 2
    body(Step(0, 0))
    body(Step(0, 1))
    with e.Fori(1, steps // 2) as j:
        if chain:
            chain.enter(j - 1, 2 * per)
        for u in range(2):
            body(Step(j, u))
    if chain:
        chain.leave(steps // 2 - 1)
    body(Step(steps // 2, 0, False))


def carry(e, g, spare):
    g.sync()
    g.add(e.tensor_tensor(spare[:, 4:6], spare[:, 0:2], spare[:, 2:4], ALU.add))


def stats(e, v, c, st, mean, var, s_var):
    with e.Fori(0, NT // 7) as i:
        v.enter(i, 7)
        for u in range(7):
            v.add(e.bn_stats(st[:, bass.ds(i * 7 + u, 1), :], c.acc3[:, bass.ds(i * 7 + u, 1), :]))
    v.leave(NT // 7)
    v.sync()
    v.add(e.tensor_tensor(mean, st[:, :, 1], st[:, :, 4], ALU.add))
    v.link(e.tensor_tensor(var, st[:, :, 1], st[:, :, 4], ALU.subtract))
    v.link(e.tensor_tensor(var, var, var, ALU.mult))
    v.add(e.tensor_scalar(var, var, 0.25, EPS, ALU.mult, ALU.add))
    v.link(e.tensor_tensor(st[:, :, 0], st[:, :, 2], st[:, :, 5], ALU.add))
    v.add(e.tensor_scalar(mean, mean, 0.5, None, ALU.mult))
    e.scalar_tensor_tensor(out=var, in0=st[:, :, 0], scalar=1.0 / D, in1=var, op0=ALU.mult, op1=ALU.add).then_inc(s_var, 1)


def mix(nc, c, A):
    big, misc = Arena(c.big, 32768), Arena(c.misc, MISC)
    qT = matrix(big.take(DH * NP), DH, NP)
    wq, wk, wp = (matrix(big.take(DH * D), DH, D) for _ in range(3))
    wvz = matrix(big.take(DH * 2 * D), DH, 2 * D)
    context, ksum = (matrix(big.take(DH * P), DH, P) for _ in range(2))
    heads = big.take(P)
    st = matrix(big.take(NT * 6), NT, 6)
    mean, var, std, rstd = (big.take(NT) for _ in range(4))
    xn = [big.take(D) for _ in range(2)]
    xT = [matrix(big.take(D), DH, P) for _ in range(2)]
    low, ex = big.take(2 * D), big.take(2 * D)
    kf = [big.take(D) for _ in range(2)]
    vo = [matrix(big.take(DH * (P + 1)), DH, P + 1) for _ in range(2)]
    zo = [big.take(D) for _ in range(2)]
    den = [big.take(D) for _ in range(2)]
    aT = [matrix(big.take(D), DH, P) for _ in range(2)]
    bias, ones, zeros = big.take(D), big.take(P), big.take(D + 4)
    valid = c.valid
    most = big.take(6)
    most2, clamp, s_f, both = (big.take(4) for _ in range(4))
    most2 = most2[:, 0:2]
    bits = big.take(2, I32)
    biases = big.take(H)
    assert big.at <= 24576
    big.at = 24576
    raw = big.take(8192)
    to = [misc.take(US, I32) for _ in range(2)]
    what = [misc.take(US * W, I32) for _ in range(2)]
    spare = c.spare
    part = [misc.take(1024) for _ in range(2)]
    S = lambda name: c.sem("mix_" + name)
    s_x, s_x0, s_w, s_raw, s_red, s_v, s_g, s_std = map(S, (
        "x", "x0", "weights", "raw", "reduced", "vector", "gpsimd", "std"))
    s_sc = [S("scatter0"), S("scatter1")]
    s_xn, s_tr, s_xt, s_qk, s_vz, s_low, s_ex, s_kf, s_vo, s_zo, s_ctx = map(S, (
        "xn", "tr", "xt", "qk", "vz", "low", "ex", "kf", "vo", "zo", "ctx"))
    s_zs = [S("zstore0"), S("zstore1")]
    s_bd, s_nd, s_at, s_pj, s_add = map(S, ("bd", "nd", "at", "pj", "add"))
    s_mt, s_mr, s_mb, s_scale = map(S, ("most_t", "most_r", "most_b", "scale"))
    s_k, s_ones, s_var, s_b1, s_b10, s_bmax, s_hi, s_lo = map(S, ("consts", "ones", "var", "b1", "b1_0", "most", "hi", "lo"))
    s_part = [S("part0"), S("part1")]
    qk_ps = [c.bank[0], c.bank[1]]
    vz_ps = [c.bank[2], c.bank[3]]
    tr_ps = [c.bank[4], c.bank[5]]
    ctx_ps = matrix(c.bank[6][:, 0:DH * (P + 1)], DH, P + 1)
    RAW = [("w1T", 0), ("w1T", 1), ("w2T", 0), ("w2T", 1)]
    flat = {k: A[k].rearrange("p a b -> p (a b)") for k in ("w1T", "w2T")}
    last = NT - 1

    def pieces(layer, n, k):
        if layer == 0:
            return c.w1[n][:, bass.ds(k * 1024, 1024)]
        return c.w2_parts[:, bass.ds(k * (1024 // D), 1024 // D), n, :]

    def shaped(layer, a):
        return a if layer == 0 else matrix(a, 1024 // D, D)

    def norm(e, s):
        if not s.fresh:
            e.wait_ge(s_tr, s.i - 1)
        e.tensor_scalar(xn[s.u], c.acc3[:, bass.ds(s.i, 1), :], mean[:, bass.ds(s.i, 1)], rstd[:, bass.ds(s.i, 1)],
                        ALU.subtract, ALU.mult).then_inc(s_xn, 1)

    def features(e, s):
        if s.more:
            norm(e, s.next())
        e.wait_ge(s_qk, s.i + 1)
        e.tensor_scalar(low, qk_ps[s.u], 0.0, None, ALU.min).then_inc(s_low, 1)
        if not s.fresh:
            e.wait_ge(s_ctx, s.i - 1)
        e.wait_ge(s_ex, s.i + 1)
        e.scalar_tensor_tensor(out=kf[s.u], in0=qk_ps[s.u][:, D:2 * D], scalar=0.0, in1=ex[:, D:2 * D],
                               op0=ALU.max, op1=ALU.add)
        e.scalar_tensor_tensor(out=qT[:, :, bass.ds(s.i * P, P)], in0=matrix(qk_ps[s.u][:, 0:D], DH, P), scalar=0.0,
                               in1=matrix(ex[:, 0:D], DH, P), op0=ALU.max, op1=ALU.add).then_inc(s_kf, 1)

    def add_to(e, s):
        e.wait_ge(s_pj, s.i + 1)
        e.tensor_tensor(c.acc3[:, bass.ds(s.i, 1), :], c.acc3[:, bass.ds(s.i, 1), :],
                        vz_ps[s.u][:, 0:D].rearrange("p (a d) -> p a d", a=1), ALU.add).then_inc(s_add, 1)

    def xt_copy(e, s):
        e.wait_ge(s_tr, s.i + 1)
        if not s.fresh:
            e.wait_ge(s_vz, s.i - 1)
        e.copy(xT[s.u], matrix(tr_ps[s.u][:, 0:D], DH, P)).then_inc(s_xt, 1)

    def copies(e, s):
        if s.more:
            xt_copy(e, s.next())
        e.wait_ge(s_low, s.i + 1)
        if not s.zero:
            e.wait_ge(s_kf, s.i)
        e.activation(ex, low, ACT.Exp).then_inc(s_ex, 1)
        e.wait_ge(s_vz, s.i + 1)
        if not s.fresh:
            e.wait_ge(s_ctx, s.i - 1)
        if not s.more:
            for h in range(DH):
                e.copy(vo[s.u][:, h, P:P + 1], valid)
        e.copy(vo[s.u][:, :, 0:P], matrix(vz_ps[s.u][:, 0:D], DH, P)).then_inc(s_vo, 1)
        if not s.fresh:
            e.wait_ge(s_zs[s.u], 16 * s.j)
        e.copy(zo[s.u], vz_ps[s.u][:, D:2 * D]).then_inc(s_zo, 1)

    def turn(e, s):
        e.wait_ge(s_xn, s.i + 1)
        if not s.fresh:
            e.wait_ge(s_xt, s.i - 1)
        for h in range(DH):
            l = e.transpose(tr_ps[s.u][:, h * P:h * P + P], xn[s.u][:, h * P:h * P + P], c.ident)
        l.then_inc(s_tr, 1)

    def project(e, s):
        if s.more:
            turn(e, s.next())
        e.wait_ge(s_xt, s.i + 1)
        if not s.fresh:
            e.wait_ge(s_kf, s.i - 1)
        for m in range(DH):
            for h in range(DH):
                e.matmul(qk_ps[s.u][:, m * P:m * P + P], wq[:, h, m * P:m * P + P], xT[s.u][:, h, :], start=h == 0, stop=h == 1)
        for h in range(DH):
            l = e.matmul(qk_ps[s.u][:, D:2 * D], xT[s.u][:, h, :], wk[:, h, :], start=h == 0, stop=h == 1)
        l.then_inc(s_qk, 1)
        if not s.fresh:
            e.wait_ge(s_zo, s.i - 1)
        for h in range(DH):
            l = e.matmul(vz_ps[s.u], xT[s.u][:, h, :], wvz[:, h, :], start=h == 0, stop=h == 1)
        l.then_inc(s_vz, 1)
        if not s.zero:
            context_sum(e, s.prev())

    def context_sum(e, s):
        e.wait_ge(s_kf, s.i + 1)
        e.wait_ge(s_vo, s.i + 1)
        for h in range(DH):
            l = e.matmul(ctx_ps[:, h, :], kf[s.u][:, h * P:h * P + P], vo[s.u][:, h, :], start=False, stop=False)
        l.then_inc(s_ctx, 1)

    def attend(e, s):
        if not s.fresh:
            e.wait_ge(s_at, s.i - 1)
        for h in range(DH):
            e.matmul(qk_ps[s.u][:, h * P:h * P + P], context[:, h, :], qT[:, h, bass.ds(s.i * P, P)], start=True, stop=True)
            l = e.matmul(qk_ps[s.u][:, D + h * P:D + h * P + P], ksum[:, h, :], qT[:, h, bass.ds(s.i * P, P)], start=True, stop=True)
        l.then_inc(s_nd, 1)

    def out_proj(e, s):
        if s.more:
            attend(e, s.next())
        e.wait_ge(s_at, s.i + 1)
        if not s.fresh:
            e.wait_ge(s_add, s.i - 1)
        for h in range(DH):
            e.matmul(vz_ps[s.u][:, 0:D], aT[s.u][:, h, :], wp[:, h, :], start=h == 0, stop=False)
        e.matmul(vz_ps[s.u][:, 0:D], ones[0:2, :], bias[0:2, :], start=False, stop=True).then_inc(s_pj, 1)

    with nc.Block() as block:
        @block.sync
        def _(e):
            e.wait_ge(s_x0, 1)
            e.dma_start(c.acc3[:, 0:last, :], A["x"][0:last * P, :].rearrange("(t p) d -> p t d", p=P)).then_inc(s_x, 16)
            e.dma_start(c.acc3[0:TAIL, last, :], A["x"][last * P:N, :]).then_inc(s_x, 16)
            e.dma_start(wq, A["q_wT"]).then_inc(s_w, 16)
            e.dma_start(wk, A["kv_wT"][:, :, 0:D]).then_inc(s_w, 16)
            e.dma_start(wvz[:, :, 0:D], A["kv_wT"][:, :, D:2 * D]).then_inc(s_w, 16)
            e.dma_start(wvz[:, :, D:2 * D], A["gnn_wT"]).then_inc(s_w, 16)
            e.dma_start(wp, A["proj_wT"]).then_inc(s_w, 16)
            e.dma_start(bias[0:1, :], A["proj_b"]).then_inc(s_w, 16)
            e.dma_start(bias[1:2, :], A["gnn_b"]).then_inc(s_w, 16)
            e.dma_start(raw, flat["w1T"][:, 0:8192]).then_inc(s_raw, 16)
            e.wait_ge(s_b10, 1)
            e.dma_start(biases[0:NE, :], A["b1"]).then_inc(s_b1, 16)
            e.wait_ge(s_red, 1)
            e.dma_start(raw, flat["w1T"][:, 8192:16384]).then_inc(s_raw, 16)

            def store(s):
                e.wait_ge(s_zo, s.i + 1)
                e.dma_start(c.z_d[bass.ds(s.i * P, P), :], zo[s.u]).then_inc(s_zs[s.u], 16)
            paired(e, NT, store)
            for r in (2, 3):
                e.wait_ge(s_red, r)
                e.dma_start(raw, flat["w2T"][:, (r - 2) * 8192:(r - 1) * 8192]).then_inc(s_raw, 16)
            for layer, name in enumerate(("w1T", "w2T")):
                def load(k, u):
                    e.dma_start(part[u], flat[name][:, bass.ds(k * 1024, 1024)]).then_inc(s_part[u], 16)
                if layer == 0:
                    load(0, 0)
                    load(1, 1)
                with e.Fori(1 - layer, CH // 2) as j:
                    for u in range(2):
                        e.wait_ge(s_lo, CH * layer + j * 2 + u - 1)
                        load(j * 2 + u, u)
            e.wait_ge(s_zs[0], 16 * (NT // 2 + 1))
            e.wait_ge(s_zs[1], 16 * (NT // 2))

        @block.gpsimd
        def _(e):
            g = Chain(e, s_g)
            g.add(e.memset(spare, 0.0))
            g.add(e.memset(valid, 1.0))
            g.sync()
            e.affine_select(out=valid, in_=valid, compare_op=ALU.is_gt, fill=0.0, base=TAIL,
                            pattern=[[0, 1]], channel_multiplier=-1).then_inc(s_k, 1)
            rec = matrix(c.rec[:, 0:EC * W], EC, W)

            def scatter(j, first, tail=False):
                for u in range(2):
                    if not first:
                        e.wait_ge(s_sc[u], 16 * US * j)
                    at = (j * 2 + u) * US
                    g.add(e.tensor_copy(to[u], c.pos[:, bass.ds(at, US)]))
                    g.add(e.tensor_copy(matrix(what[u], US, W), rec[:, bass.ds(at, US), :]))
                    carry(e, g, spare)
                    for n in range(US):
                        k = ER if tail and u == 1 and n == US - 1 else P
                        e.indirect_dma_start(out=c.rec_d, out_offset=bass.IndirectOffsetOnAxis(ap=to[u][0:k, n:n + 1], axis=0),
                                             in_=what[u][0:k, n * W:n * W + W], in_offset=None).then_inc(s_sc[u], 16)
            trips = EC // (2 * US)
            scatter(0, True)
            with e.Fori(1, trips - 1) as j:
                g.enter(j - 1, 6)
                scatter(j, False)
            g.leave(trips - 2)
            scatter(trips - 1, False, True)
            for u in range(2):
                e.wait_ge(s_sc[u], 16 * US * trips)

        @block.vector
        def _(e):
            v = Chain(e, s_v)
            e.memset(c.acc3[:, last, :], 0.0).then_inc(s_x0, 1)
            e.memset(zeros, 0.0).then_inc(s_ones, 1)
            e.memset(biases, 0.0).then_inc(s_b10, 1)
            v.link(e.memset(heads, 0.0))
            for a in range(0, P, HEAD):
                v.add(e.memset(heads[a:a + HEAD, a:a + HEAD], 1.0))
            for t in (ones, vo[0], vo[1]):
                e.memset(t, 1.0).then_inc(s_ones, 1)
            e.wait_ge(s_x, 32)
            stats(e, v, c, st, mean, var, s_var)
            e.wait_ge(s_std, 1)
            v.link(e.reciprocal(rstd, std))
            e.wait_ge(s_raw, 16)
            e.tensor_reduce(most[:, 0:1], raw, AX.X, ALU.max, apply_absolute_value=True).then_inc(s_red, 1)
            norm(e, Step(0, 0))
            paired(e, NT, lambda s: features(e, s))
            e.wait_ge(s_ctx, NT + 1)
            for h in range(DH):
                v.add(e.tensor_tensor(context[:, h, :], ctx_ps[:, h, 0:P], heads, ALU.mult))
                l = e.tensor_scalar(ksum[:, h, :], heads, ctx_ps[:, h, P:P + 1], None, ALU.mult)
            l.then_inc(s_bd, 1)
            e.wait_ge(s_raw, 32)
            e.tensor_reduce(most[:, 1:2], raw, AX.X, ALU.max, apply_absolute_value=True).then_inc(s_red, 1)

            def attention(s):
                e.wait_ge(s_nd, s.i + 1)
                if not s.fresh:
                    e.wait_ge(s_pj, s.i - 1)
                v.link(e.tensor_scalar(den[s.u], qk_ps[s.u][:, D:2 * D], DEN_MIN, None, ALU.max))
                v.link(e.reciprocal(den[s.u], den[s.u]))
                e.tensor_tensor(aT[s.u], matrix(qk_ps[s.u][:, 0:D], DH, P), matrix(den[s.u], DH, P), ALU.mult).then_inc(s_at, 1)
                if not s.zero:
                    add_to(e, s.prev())
            paired(e, NT, attention, v, 2)
            add_to(e, Step(NT // 2, 0))
            for r in (2, 3):
                e.wait_ge(s_raw, 16 * (r + 1))
                e.tensor_reduce(most[:, r:r + 1], raw, AX.X, ALU.max, apply_absolute_value=True).then_inc(s_red, 1)
            e.wait_ge(s_b1, 16)
            v.link(e.tensor_reduce(most[:, 4:5], biases, AX.X, ALU.max, apply_absolute_value=True))
            e.wait_ge(s_red, 4)
            v.link(e.tensor_tensor(most2, most[:, 0:4:2], most[:, 1:4:2], ALU.max))
            e.tensor_tensor(most2[:, 0:1], most2[:, 0:1], most[:, 4:5], ALU.max).then_inc(s_bmax, 1)
            e.wait_ge(s_mt, 1)
            v.link(e.tensor_reduce(clamp[0:2, 0:1], c.bank[7][0:2, 0:P], AX.X, ALU.max))
            v.link(e.tensor_scalar(clamp[0:2, 0:1], clamp[0:2, 0:1], 2.0 ** -60, 2.0 ** 60, ALU.max, ALU.min))
            v.link(e.tensor_scalar(bits[0:2, 0:1], clamp[0:2, 0:1].bitcast(I32), 0x7F800000, None, ALU.bitwise_and))
            v.add(e.tensor_scalar(s_f[0:2, 0:1].bitcast(I32), bits[0:2, 0:1], -1.0, 257.0 * 2 ** 23, ALU.mult, ALU.add))
            v.link(e.tensor_scalar(s_f[0:2, 1:2].bitcast(I32), bits[0:2, 0:1], 3.0 * 2 ** 23, None, ALU.subtract))
            v.add(e.tensor_scalar(both[0:2, 0:2], c.ident[0:2, 0:2], s_f[0:2, 0:1], None, ALU.mult))
            e.tensor_scalar(both[0:2, 2:4], c.ident[0:2, 0:2], s_f[0:2, 1:2], None, ALU.mult).then_inc(s_mr, 1)
            e.wait_ge(s_mb, 1)
            v.link(e.tensor_copy(c.scale, c.bank[7][:, 256:258]))
            v.link(e.tensor_copy(c.descale, c.bank[7][:, 258:260]))
            v.add(e.tensor_tensor(c.descale[:, 1:2], c.descale[:, 0:1], c.descale[:, 1:2], ALU.mult))
            v.sync()
            e.nop().then_inc(s_scale, 1)

            def low_part(layer, j, u):
                k = j * 2 + u
                e.wait_ge(s_hi, CH * layer + k + 1)
                e.scalar_tensor_tensor(out=pieces(layer, 1, k), in0=shaped(layer, part[u]), scalar=c.scale[:, layer:layer + 1],
                                       in1=pieces(layer, 0, k), op0=ALU.mult, op1=ALU.subtract).then_inc(s_lo, 1)
            for layer in range(2):
                with e.Fori(0, CH // 2) as j:
                    for u in range(2):
                        low_part(layer, j, u)

        @block.scalar
        def _(e):
            e.wait_ge(s_var, 1)
            e.activation(std, var, ACT.Sqrt).then_inc(s_std, 1)
            xt_copy(e, Step(0, 0))
            e.wait_ge(s_k, 1)
            e.wait_ge(s_ones, 4)
            paired(e, NT, lambda s: copies(e, s))
            e.wait_ge(s_scale, 1)
            for layer in range(2):
                with e.Fori(0, CH // 2) as j:
                    for u in range(2):
                        k = j * 2 + u
                        e.wait_ge(s_part[u], 16 * (CH // 2 * layer + j + 1))
                        e.activation(pieces(layer, 0, k), shaped(layer, part[u]), ACT.Copy,
                                     scale=c.scale[:, layer:layer + 1]).then_inc(s_hi, 1)

        @block.tensor
        def _(e):
            e.wait_ge(s_w, 16 * 7)
            e.wait_ge(s_ones, 4)
            e.matmul(ctx_ps, zeros[:, 0:P], matrix(zeros[:, 0:DH * (P + 1)], DH, P + 1), start=True, stop=False)
            turn(e, Step(0, 0))
            paired(e, NT, lambda s: project(e, s))
            context_sum(e, Step(NT // 2, 0))
            e.matmul(ctx_ps, zeros[:, 0:P], matrix(zeros[:, 0:DH * (P + 1)], DH, P + 1), start=False, stop=True).then_inc(s_ctx, 1)
            e.wait_ge(s_bd, 1)
            e.wait_ge(s_zo, NT)
            attend(e, Step(0, 0))
            paired(e, NT, lambda s: out_proj(e, s))
            e.wait_ge(s_bmax, 1)
            e.transpose(c.bank[7][0:2, 0:P], most2, c.ident).then_inc(s_mt, 1)
            e.wait_ge(s_mr, 1)
            e.matmul(c.bank[7][:, 256:260], ones[0:2, :], both[0:2, :], start=True, stop=True).then_inc(s_mb, 1)


def graph(nc, c):
    misc = Arena(c.misc, MISC)
    rows = [misc.take(D) for _ in range(UG)]
    hot = [misc.take(P) for _ in range(HG)]
    near = [matrix(misc.take(UG * 2), UG, 2) for _ in range(2)]
    rec, rec_f = matrix(c.rec[:, :], ET, W), matrix(c.rec[:, :].bitcast(F32), ET, W)
    turns, LEAD = ET // UG, HG // 2
    S = lambda name: c.sem("graph_" + name)
    s_rec, s_near, s_idx, s_blk, s_g = map(S, ("rec", "near", "idx", "blk", "gpsimd"))
    s_row, s_mm, s_add = ([S(f"{name}{k}") for k in range(UG)] for name in ("row", "mm", "add"))
    s_hot = S("hot")
    idx, spare = c.idx, c.spare
    with nc.Block() as block:
        @block.sync
        def _(e):
            e.dma_start(c.rec[:, :], c.rec_d.rearrange("(p t) w -> p (t w)", p=P)).then_inc(s_rec, 16)
            e.dma_start(c.pos[0:1, :], c.blk_d).then_inc(s_blk, 16)

        def fetch(e, q, u):
            part = slice(u * UG, (u + 1) * UG) if isinstance(q, int) else bass.ds(q * UG, UG)
            e.copy(idx[u], rec[:, part, 0]).then_inc(s_idx, 1)
            e.copy(near[u], rec_f[:, part, 1:3]).then_inc(s_near, 1)

        @block.scalar
        def _(e):
            e.wait_ge(s_rec, 16)
            fetch(e, 0, 0)
            fetch(e, 1, 1)
            with e.Fori(1, turns // 2) as j:
                for u in range(2):
                    q = j * 2 + u
                    e.wait_ge(s_mm[UG - 1], q - 1)
                    fetch(e, q, u)

        def gather(e, g, q, u):
            for k in range(UG):
                if k % QG == 0:
                    if k == 0:
                        e.wait_ge(s_idx, q + 1)
                    if not (isinstance(q, int) and q == 0):
                        e.wait_ge(s_mm[k + QG - 1], q)
                    carry(e, g, spare)
                e.indirect_dma_start(out=rows[k], out_offset=None, in_=c.z_d,
                                     in_offset=bass.IndirectOffsetOnAxis(ap=idx[u][:, k:k + 1], axis=0)).then_inc(s_row[k], 16)

        @block.gpsimd
        def _(e):
            g = Chain(e, s_g)
            gather(e, g, 0, 0)
            gather(e, g, 1, 1)
            with e.Fori(1, turns // 2) as j:
                g.enter(j - 1, 2 * UG // QG)
                for u in range(2):
                    gather(e, g, j * 2 + u, u)
            g.leave(turns // 2 - 1)

        def one_hot(e, u, k):
            e.tensor_scalar(hot[k % HG], c.column, near[u][:, k, 0:1], near[u][:, k, 1:2],
                            ALU.is_equal, ALU.mult).then_inc(s_hot, 1)

        @block.vector
        def _(e):
            e.wait_ge(s_near, 1)
            e.wait_ge(s_blk, 16)
            for k in range(LEAD):
                one_hot(e, 0, k)

            def turn(q, u, more=True):
                _, starts = nc.values_load_multi_w_load_instructions(
                    c.pos[0:1, bass.ds(q * UG, UG)], engines=[mybir.EngineType.DVE], min_val=0, max_val=(NT - 1) * D)
                for k in range(UG):
                    n = k + LEAD
                    if n == UG and more:
                        e.wait_ge(s_near, q + 2)
                    if n < UG:
                        one_hot(e, u, n)
                    elif more:
                        one_hot(e, 1 - u, n - UG)
                    rows_of = c.acc[:, bass.ds(starts[k], D)]
                    e.wait_ge(s_mm[k], q + 1)
                    if k:
                        e.wait_ge(s_add[k - 1], q + 1)
                    elif not (isinstance(q, int) and q == 0):
                        e.wait_ge(s_add[UG - 1], q)
                    e.tensor_tensor(rows_of, rows_of, c.bank[k % HG][:, 0:D], ALU.add).then_inc(s_add[k], 1)
            turn(0, 0)
            turn(1, 1)
            with e.Fori(1, turns // 2 - 1) as j:
                turn(j * 2, 0)
                turn(j * 2 + 1, 1)
            turn(turns - 2, 0)
            turn(turns - 1, 1, False)

        @block.tensor
        def _(e):
            with e.Fori(0, turns) as q:
                for k in range(UG):
                    e.wait_ge(s_hot, q * UG + k + 1)
                    e.wait_ge(s_row[k], 16 * (q + 1))
                    e.matmul(c.bank[k % HG][:, 0:D], hot[k % HG], rows[k], start=True, stop=True).then_inc(s_mm[k], 1)


def route(nc, c, A):
    misc, more, pos = Arena(c.misc, MISC), Arena(c.rec, ET * W), Arena(c.pos, ET)
    more.t = c.rec[:, :].bitcast(F32)
    pos.t = c.pos[:, :].bitcast(F32)
    c.prob = [pos.take(NT) for _ in range(TOP)]
    c.slot = [pos.take(NT, I32) for _ in range(TOP)]
    c.experts = matrix(pos.take((MT + 1) * 2, I32), (MT + 1) // 2, 4)
    c.token = pos.take(MT, I32)
    c.dest = pos.take(MT, I32)
    c.share = matrix(more.take(NT * NE), NT, NE)
    st = matrix(more.take(NT * 6), NT, 6)
    mean, var, std, rstd = (more.take(NT) for _ in range(4))
    scores = matrix(more.take(NT * NE), NT, NE)
    shared = more.at
    wg = matrix(more.take(DH * NE), DH, NE)
    bg, ones = more.take(NE), more.take(P)
    xn = [misc.take(D) for _ in range(2)]
    xT = [matrix(misc.take(D), DH, P) for _ in range(2)]
    tok = [misc.take(2 * D, F16) for _ in range(2)]
    S = lambda name: c.sem("route_" + name)
    s_w, s_v, s_var, s_std, s_ones, s_xn, s_tr, s_xt, s_gate, s_hi, s_lo = map(S, (
        "weights", "vector", "var", "std", "ones", "xn", "tr", "xt", "gate", "hi", "lo"))
    s_score = S("score")
    s_st = [S("store0"), S("store1")]

    def score(e, s):
        e.wait_ge(s_gate, s.i + 1)
        e.copy(scores[:, bass.ds(s.i, 1), :], g_ps[s.u][:, 0:NE].rearrange("p (a t) -> p a t", a=1)).then_inc(s_score, 1)

    tr_ps, g_ps, bg_ps = [c.bank[4], c.bank[5]], [c.bank[0], c.bank[1]], c.bank[2][:, 0:NE]

    def norm(e, s):
        if not s.fresh:
            e.wait_ge(s_tr, s.i - 1)
            e.wait_ge(s_lo, s.i - 1)
        e.tensor_scalar(xn[s.u], c.acc3[:, bass.ds(s.i, 1), :], mean[:, bass.ds(s.i, 1)], rstd[:, bass.ds(s.i, 1)],
                        ALU.subtract, ALU.mult).then_inc(s_xn, 1)

    def turn(e, s):
        e.wait_ge(s_xn, s.i + 1)
        if not s.fresh:
            e.wait_ge(s_xt, s.i - 1)
        for h in range(DH):
            l = e.transpose(tr_ps[s.u][:, h * P:h * P + P], xn[s.u][:, h * P:h * P + P], c.ident)
        l.then_inc(s_tr, 1)

    def gate(e, s):
        if s.more:
            turn(e, s.next())
        e.wait_ge(s_xt, s.i + 1)
        if not s.fresh:
            e.wait_ge(s_score, s.i - 1)
        for h in range(DH):
            l = e.matmul(g_ps[s.u][:, 0:NE], xT[s.u][:, h, :], wg[:, h, :], start=h == 0, stop=h == DH - 1)
        l.then_inc(s_gate, 1)

    with nc.Block() as block:
        @block.sync
        def _(e):
            e.dma_start(wg, A["gate_wT"]).then_inc(s_w, 16)
            e.dma_start(bg[0:1, :], A["gate_b"]).then_inc(s_w, 16)

            def store(s):
                e.wait_ge(s_lo, s.i + 1)
                e.dma_start(c.tok_d[bass.ds(s.i * P, P), :], tok[s.u]).then_inc(s_st[s.u], 16)
            paired(e, NT, store)
            e.wait_ge(s_st[0], 16 * (NT // 2 + 1))
            e.wait_ge(s_st[1], 16 * (NT // 2))

        @block.vector
        def _(e):
            v = Chain(e, s_v)
            e.memset(ones, 1.0).then_inc(s_ones, 1)
            stats(e, v, c, st, mean, var, s_var)
            e.wait_ge(s_std, 1)
            v.link(e.reciprocal(rstd, std))
            norm(e, Step(0, 0))

            def split(s):
                if s.more:
                    norm(e, s.next())
                e.wait_ge(s_hi, s.i + 1)
                e.tensor_tensor(tok[s.u][:, D:2 * D], xn[s.u], tok[s.u][:, 0:D], ALU.subtract).then_inc(s_lo, 1)
            paired(e, NT, split)

        @block.scalar
        def _(e):
            e.wait_ge(s_var, 1)
            e.activation(std, var, ACT.Sqrt).then_inc(s_std, 1)

            def copies(s):
                e.wait_ge(s_xn, s.i + 1)
                if not s.fresh:
                    e.wait_ge(s_st[s.u], 16 * s.j)
                e.copy(tok[s.u][:, 0:D], xn[s.u]).then_inc(s_hi, 1)
                e.wait_ge(s_tr, s.i + 1)
                if not s.fresh:
                    e.wait_ge(s_gate, s.i - 1)
                e.copy(xT[s.u], matrix(tr_ps[s.u][:, 0:D], DH, P)).then_inc(s_xt, 1)
                if not s.zero:
                    score(e, s.prev())
            paired(e, NT, copies)
            score(e, Step(NT // 2, 0))

        @block.tensor
        def _(e):
            e.wait_ge(s_w, 32)
            e.wait_ge(s_ones, 1)
            e.matmul(bg_ps, ones[0:1, :], bg[0:1, :], start=True, stop=True)
            turn(e, Step(0, 0))
            paired(e, NT, lambda s: gate(e, s))

    misc.at = 0
    more.at = shared
    share = c.share
    hot = [matrix(more.take(NT * NE), NT, NE) for _ in range(TOP)]
    mask16 = matrix(more.take(NE * NT, F16), NE, NT)
    ones16 = more.take(P, F16)
    slots, after = matrix(misc.take(NE * NT), NE, NT), matrix(misc.take(NE * NT), NE, NT)
    by_token = matrix(misc.take(NT * NE), NT, NE)
    ones_row = misc.take(NE * NT)
    slot_f = [misc.take(NT) for _ in range(TOP)]
    last_e, past, tiles, ends, shift = (misc.take(NE) for _ in range(5))
    tiles_i = misc.take(2 * NE, I32)
    begun = matrix(misc.take(MT * (NE - 1)), MT, NE - 1)
    order = misc.take(MT)
    gap, ex, total = (misc.take(NT) for _ in range(3))
    best = [misc.take(NT) for _ in range(TOP)]
    rank_of = more.take(NE)
    lead = more.take(NT)
    above, sums = matrix(c.bank[0][:, 0:NE * NT], NE, NT), matrix(c.bank[1][:, 0:NE * NT], NE, NT)
    flat = lambda a: a.rearrange("p a b -> p (a b)")
    turned = lambda a: a.rearrange("p a b -> p b a")
    col = lambda a: a.rearrange("p (t a) -> p t a", a=1)
    s_c, s_mask, s_cnt, s_gap, s_ex = map(S, ("chain2", "mask", "counts", "gap", "ex"))
    with nc.Block() as block:
        @block.vector
        def _(e):
            v = Chain(e, s_c)
            v.add(e.memset(ones16, 1.0))
            v.add(e.memset(ones_row, 1.0))
            v.add(e.memset(past, 0.0))
            v.link(e.tensor_scalar(rank_of, c.column[:, 0:NE], -1.0, float(NE), ALU.mult, ALU.add))
            wide = [P, NT, NE]
            v.link(e.tensor_tensor(scores, scores, bg_ps.rearrange("p (a e) -> p a e", a=1).to_broadcast(wide), ALU.add))
            for k in range(TOP):
                v.link(e.tensor_reduce(best[k], scores, AX.X, ALU.max))
                v.link(e.tensor_tensor(hot[k], scores, col(best[k]).to_broadcast(wide), ALU.is_equal))
                v.link(e.tensor_tensor(by_token, hot[k], rank_of.rearrange("p (a e) -> p a e", a=1).to_broadcast(wide), ALU.mult))
                v.link(e.tensor_reduce(lead, by_token, AX.X, ALU.max))
                v.link(e.tensor_tensor(hot[k], by_token, col(lead).to_broadcast(wide), ALU.is_equal))
                if k == 0:
                    v.link(e.scalar_tensor_tensor(out=scores, in0=hot[0], scalar=-3e38, in1=scores, op0=ALU.mult, op1=ALU.add))
            e.tensor_tensor(gap, best[1], best[0], ALU.subtract).then_inc(s_gap, 1)
            for k in range(TOP):
                v.add(e.tensor_scalar(hot[k][:, NT - 1, :], hot[k][:, NT - 1, :], c.valid, None, ALU.mult))
            v.sync()
            e.tensor_tensor(turned(mask16), hot[0], hot[1], ALU.add).then_inc(s_mask, 1)
            e.wait_ge(s_ex, 1)
            v.link(e.tensor_scalar(total, ex, 1.0, None, ALU.add))
            v.link(e.reciprocal(c.prob[0], total))
            v.link(e.tensor_tensor(c.prob[1], ex, c.prob[0], ALU.mult))
            v.add(e.tensor_tensor(share, hot[0], col(c.prob[0]).to_broadcast([P, NT, NE]), ALU.mult))
            v.link(e.tensor_tensor(by_token, hot[1], col(c.prob[1]).to_broadcast([P, NT, NE]), ALU.mult))
            v.link(e.tensor_tensor(share, share, by_token, ALU.add))
            e.wait_ge(s_cnt, 1)
            v.link(e.tensor_tensor_scan(flat(after), ones_row, flat(sums), 0.0, ALU.mult, ALU.add))
            v.add(e.tensor_copy(last_e, after[:, :, NT - 1]))
            v.link(e.tensor_copy(past[:, 1:NE], after[:, 0:NE - 1, NT - 1]))
            v.add(e.tensor_tensor(slots, after, sums, ALU.subtract))
            v.link(e.tensor_tensor(tiles, last_e, past, ALU.subtract))
            v.link(e.tensor_tensor(slots, slots, above, ALU.add))
            v.link(e.tensor_scalar(tiles_i[:, 0:NE], tiles, P - 1.0, None, ALU.add))
            v.link(e.tensor_scalar(tiles_i[:, NE:2 * NE], tiles_i[:, 0:NE], 7, None, ALU.logical_shift_right))
            v.link(e.tensor_copy(tiles, tiles_i[:, NE:2 * NE]))
            v.link(e.tensor_tensor_scan(ends, ones_row[:, 0:NE], tiles, 0.0, ALU.mult, ALU.add))
            v.link(e.tensor_tensor(shift, ends, tiles, ALU.subtract))
            v.link(e.scalar_tensor_tensor(out=shift, in0=shift, scalar=float(P), in1=past, op0=ALU.mult, op1=ALU.subtract))
            v.link(e.tensor_tensor(slots, slots, col(shift).to_broadcast([P, NE, NT]), ALU.add))
            for k in range(TOP):
                v.link(e.tensor_tensor(by_token, hot[k], turned(slots), ALU.mult))
                v.link(e.tensor_reduce(slot_f[k], by_token, AX.X, ALU.add))
                v.link(e.tensor_copy(c.slot[k], slot_f[k]))
            v.link(e.tensor_tensor(begun, col(c.column[:, 0:MT]).to_broadcast([P, MT, NE - 1]),
                                   ends[:, 0:NE - 1].rearrange("p (a e) -> p a e", a=1).to_broadcast([P, MT, NE - 1]), ALU.is_ge))
            v.link(e.tensor_reduce(order, begun, AX.X, ALU.add))
            v.link(e.memset(c.experts, 0))
            v.add(e.tensor_copy(c.experts[:, 1:, 0], order[:, 1:MT - 1:2]))
            v.add(e.tensor_copy(c.experts[:, :, 1], order[:, 0:MT:2]))
            v.add(e.tensor_copy(c.experts[:, 0:MT // 2, 2], order[:, 1:MT:2]))

        @block.scalar
        def _(e):
            e.wait_ge(s_gap, 1)
            e.activation(ex, gap, ACT.Exp).then_inc(s_ex, 1)

        @block.tensor
        def _(e):
            e.wait_ge(s_mask, 1)
            e.wait_ge(s_c, 1)
            e.matmul(flat(above), c.before, flat(mask16), start=True, stop=True)
            e.matmul(flat(sums), ones16, flat(mask16), start=True, stop=True).then_inc(s_cnt, 1)

    misc.at, more.at = 0, shared
    number = [misc.take(NT) for _ in range(TOP)]
    nowhere = more.take(MT)
    empty, row_of = more.take(MT), more.take(MT)
    row_f, tile_f = ([matrix(misc.take(NT), NT // 7, 7) for _ in range(TOP)] for _ in range(2))
    part = misc.take(NT, I32)
    hot_row = [matrix(misc.take(7 * P), 7, P) for _ in range(2)]
    hot_tile = [matrix(misc.take(7 * MT), 7, MT) for _ in range(2)]
    who = c.bank[2][:, 0:MT]
    s_n, s_c3, s_rows = map(S, ("number", "chain3", "rows"))
    s_used = [S("used0"), S("used1")]
    with nc.Block() as block:
        @block.gpsimd
        def _(e):
            for k in range(TOP):
                e.iota(number[k], pattern=[[TOP * P, NT]], base=k + 1, channel_multiplier=TOP,
                       allow_small_or_imprecise_dtypes=True).then_inc(s_n, 1)
            e.iota(nowhere, pattern=[[P, MT]], base=TOP * NP, channel_multiplier=1,
                   allow_small_or_imprecise_dtypes=True).then_inc(s_n, 1)

        @block.vector
        def _(e):
            v = Chain(e, s_c3)
            e.wait_ge(s_n, TOP + 1)
            for k in range(TOP):
                v.add(e.tensor_tensor(number[k][:, NT - 1:NT], number[k][:, NT - 1:NT], c.valid, ALU.mult))
                v.link(e.tensor_scalar(part, c.slot[k], P - 1, None, ALU.bitwise_and))
                v.link(e.tensor_copy(flat(row_f[k]), part))
                v.link(e.tensor_scalar(part, c.slot[k], 7, None, ALU.logical_shift_right))
                v.link(e.tensor_copy(flat(tile_f[k]), part))

            def hots(g, first=False):
                some = lambda a: a[:, bass.ds(g, 1), :].rearrange("p a (t b) -> p (a t) b", b=1)
                for k in range(TOP):
                    if not first:
                        e.wait_ge(s_used[k], g)
                    v.add(e.tensor_tensor(hot_row[k], c.column.rearrange("p (a t) -> p a t", a=1).to_broadcast([P, 7, P]),
                                          some(row_f[k]).to_broadcast([P, 7, P]), ALU.is_equal))
                    v.link(e.tensor_tensor(hot_tile[k], c.column[:, 0:MT].rearrange("p (a t) -> p a t", a=1).to_broadcast([P, 7, MT]),
                                           some(tile_f[k]).to_broadcast([P, 7, MT]), ALU.is_equal))
                    e.tensor_tensor(hot_tile[k], hot_tile[k], some(matrix(number[k], NT // 7, 7)).to_broadcast([P, 7, MT]), ALU.mult).then_inc(s_rows, 1)
            hots(0, True)
            with e.Fori(1, NT // 7) as g:
                v.enter(g - 1, 2 * TOP)
                hots(g)
            v.leave(NT // 7 - 1)
            for k in range(TOP):
                e.wait_ge(s_used[k], NT // 7)
            v.add(e.tensor_scalar(empty, who, 0.0, None, ALU.is_equal))
            v.sync()
            v.add(e.tensor_tensor(nowhere, empty, nowhere, ALU.mult))
            v.link(e.scalar_tensor_tensor(out=row_of, in0=who, scalar=-1.0, in1=empty, op0=ALU.add, op1=ALU.add))
            v.link(e.tensor_copy(c.dest, row_of))
            v.add(e.tensor_scalar(c.token, c.dest, TOP // 2, None, ALU.logical_shift_right))
            v.link(e.tensor_tensor(row_of, row_of, nowhere, ALU.add))
            v.link(e.tensor_copy(c.dest, row_of))

        @block.tensor
        def _(e):
            def sums(g, start=False, stop=False):
                for k in range(TOP):
                    e.wait_ge(s_rows, g * TOP + k + 1)
                    for n in range(7):
                        l = e.matmul(who, hot_row[k][:, n, :], hot_tile[k][:, n, :], start=start and k == n == 0,
                                     stop=stop and k == TOP - 1 and n == 6)
                    l.then_inc(s_used[k], 1)
            sums(0, start=True)
            with e.Fori(1, NT // 7 - 1) as g:
                sums(g)
            sums(NT // 7 - 1, stop=True)


def experts(nc, c, A):
    misc, more = Arena(c.misc, MISC), Arena(c.rec, ET * W)
    more.t = c.rec[:, :].bitcast(F32)
    xs = [misc.take(2 * D, F16) for _ in range(2)]
    xT = [matrix(misc.take(2 * D, F16), 2 * DH, P) for _ in range(2)]
    y, y2 = ([misc.take(D) for _ in range(2)] for _ in range(2))
    bias = misc.take(H, F16)
    select = misc.take(NE * P, F16)
    more.at = NT * NE
    at_high = more.at
    high, low = ([matrix(more.take(H, F16), HB, P) for _ in range(2)] for _ in range(2))
    bias_f = more.t[:, at_high:at_high + H]
    S = lambda name: c.sem("experts_" + name)
    s_y2 = S("y2")
    s_b, s_b0, s_bh, s_bias, s_sel, s_tr, s_xt, s_h, s_high, s_low, s_y, s_out = map(S, (
        "b1", "b1_0", "b1_high", "bias", "select", "tr", "xt", "h", "high", "low", "y", "out"))
    s_g = S("gpsimd")
    at, to = ([misc.take(1, I32) for _ in range(2)] for _ in range(2))
    AHEAD = 4
    s_xs, s_ys = [S("xs0"), S("xs1")], [S("ystore0"), S("ystore1")]
    tr_ps = [matrix(c.bank[u][:, 0:D].bitcast(F16), 2 * DH, P) for u in range(2)]
    h_ps = [matrix(c.wide[1 + u], HB, P) for u in range(2)]
    y_ps = [c.bank[6], c.bank[7]]
    half = HB // 2
    w1h, w1l = c.w1
    BEHIND = ((), (), (0,), (1,), (2,), (3, 4), (5,), (6, 7))

    def turn(e, s):
        e.wait_ge(s_xs[s.u], 16 * (s.j + 1))
        if not s.fresh:
            e.wait_ge(s_xt, s.i - 1)
        for n in range(2 * DH):
            l = e.transpose(tr_ps[s.u][:, n, :], xs[s.u][:, n * P:n * P + P], c.ident16)
        l.then_inc(s_tr, 1)

    def first(e, s, x, m):
        if m == 0:
            e.wait_ge(s_xt, s.i + 1)
        if not s.fresh and m % half == 0:
            e.wait_ge(s_low, 2 * s.i - 3 + m // half)
        o = h_ps[s.u][:, m, :]
        e.matmul(o, bias[:, m * P:m * P + P], select[:, bass.ds(x * P, P)], start=True, stop=False)
        for h in range(DH):
            at = bass.ds(x * H + (h * NE * H + m * P), P)
            e.matmul(o, w1h[:, at], xT[s.u][:, h, :], start=False, stop=False)
            e.matmul(o, w1h[:, at], xT[s.u][:, DH + h, :], start=False, stop=False)
            l = e.matmul(o, w1l[:, at], xT[s.u][:, h, :], start=False, stop=h == DH - 1)
        if m % half == half - 1:
            l.then_inc(s_h, 1)

    def second(e, s, x, m):
        if m % half == 0:
            e.wait_ge(s_low, 2 * s.i + 1 + m // half)
        if m == 0 and not s.fresh:
            e.wait_ge(s_y, s.i - 1)
        at = x * (2 * D) + m * NE * 2 * D
        if m == HB - 1:
            e.matmul(y_ps[s.u][:, 0:D], low[s.u][:, m, :], c.w2[:, bass.ds(at, D)], start=False, stop=False)
        l = e.matmul(y_ps[s.u], high[s.u][:, m, :], c.w2[:, bass.ds(at, 2 * D)], start=m == 0, stop=m == HB - 1)
        if m < HB - 1:
            e.matmul(y_ps[s.u][:, 0:D], low[s.u][:, m, :], c.w2[:, bass.ds(at, D)], start=False, stop=False)
        else:
            l.then_inc(s_out, 1)

    def relu(e, s):
        for n in range(2):
            e.wait_ge(s_h, 2 * s.i + 1 + n)
            if not s.fresh and n == 0:
                e.wait_ge(s_out, s.i - 1)
            part = slice(n * half, (n + 1) * half)
            e.activation(high[s.u][:, part, :], h_ps[s.u][:, part, :], ACT.Relu).then_inc(s_high, 1)

    def result(e, s):
        e.wait_ge(s_out, s.i + 1)
        if not s.fresh:
            e.wait_ge(s_ys[s.u], 16 * s.j)
        e.activation(y2[s.u], y_ps[s.u][:, D:2 * D], ACT.Copy, scale=c.descale[:, 1:2]).then_inc(s_y2, 1)

    def total(e, s):
        e.wait_ge(s_y2, s.i + 1)
        e.scalar_tensor_tensor(out=y[s.u], in0=y_ps[s.u][:, 0:D], scalar=c.descale[:, 1:2], in1=y2[s.u],
                               op0=ALU.mult, op1=ALU.add).then_inc(s_y, 1)

    with nc.Block() as block:
        @block.sync
        def _(e):
            e.wait_ge(s_b0, 1)
            e.dma_start(bias_f[0:NE, :], A["b1"]).then_inc(s_b, 16)
            e.dma_start(bias_f[32:32 + NE, :], A["b1"]).then_inc(s_b, 16)

        @block.gpsimd
        def _(e):
            e.memset(select, 0.0).then_inc(s_sel, 1)
            e.wait_ge(s_sel, 1)
            for n, base in enumerate((0, -32)):
                e.affine_select(out=matrix(select, NE, P), in_=matrix(select, NE, P), compare_op=ALU.not_equal, fill=1.0,
                                base=base, pattern=[[-1, NE], [0, P]], channel_multiplier=1).then_inc(s_sel, 1)
                e.wait_ge(s_sel, n + 2)

            g = Chain(e, s_g)

            def gather(s):
                if not s.fresh:
                    e.wait_ge(s_tr, s.i - 1)
                column = bass.ds(s.i, 1) if not isinstance(s.i, int) else slice(s.i, s.i + 1)
                g.add(e.tensor_copy(at[s.u], c.token[:, column]))
                carry(e, g, c.spare)
                e.indirect_dma_start(out=xs[s.u], out_offset=None, in_=c.tok_d,
                                     in_offset=bass.IndirectOffsetOnAxis(ap=at[s.u][:, 0:1], axis=0)).then_inc(s_xs[s.u], 16)

            def scatter(s):
                e.wait_ge(s_y, s.i + 1)
                if not s.fresh:
                    e.wait_ge(s_ys[s.u], 16 * s.j)
                g.add(e.tensor_copy(to[s.u], c.dest[:, bass.ds(s.i, 1)]))
                carry(e, g, c.spare)
                e.indirect_dma_start(out=c.y_d, out_offset=bass.IndirectOffsetOnAxis(ap=to[s.u][:, 0:1], axis=0),
                                     in_=y[s.u], in_offset=None).then_inc(s_ys[s.u], 16)

            def both(s):
                scatter(s)
                gather(s.later(AHEAD))
            for i in range(AHEAD):
                gather(Step(i // 2, i % 2))
            paired(e, MT - AHEAD, both, g, 4)
            for i in range(MT - AHEAD, MT):
                scatter(Step(i // 2, i % 2))
            e.wait_ge(s_ys[0], 16 * (MT // 2 + 1))
            e.wait_ge(s_ys[1], 16 * (MT // 2))

        @block.scalar
        def _(e):
            e.wait_ge(s_b, 32)
            e.wait_ge(s_b0, 2)
            e.activation(bias[0:NE, :], bias_f[0:NE, :], ACT.Copy, scale=c.scale[0:NE, 0:1]).then_inc(s_bh, 1)
            e.activation(bias[32:32 + NE, :], bias_f[32:32 + NE, :], ACT.Copy, scale=c.scale[32:32 + NE, 0:1]).then_inc(s_bh, 1)

            def step(s):
                e.wait_ge(s_tr, s.i + 1)
                if not s.fresh:
                    e.wait_ge(s_h, 2 * s.i - 2)
                e.copy(xT[s.u], tr_ps[s.u]).then_inc(s_xt, 1)
                if not s.zero:
                    relu(e, s.prev())
                    if not s.first2:
                        result(e, s.prev().prev())
            paired(e, MT, step)
            relu(e, Step(MT // 2, 0))
            result(e, Step(MT // 2 - 1, 1))
            result(e, Step(MT // 2, 0))

        @block.vector
        def _(e):
            e.memset(bias_f, 0.0).then_inc(s_b0, 1)
            e.memset(bias, 0.0).then_inc(s_b0, 1)
            e.wait_ge(s_bh, 2)
            e.scalar_tensor_tensor(out=bias[32:32 + NE, :], in0=bias_f[32:32 + NE, :], scalar=c.scale[32:32 + NE, 0:1],
                                   in1=bias[32:32 + NE, :], op0=ALU.mult, op1=ALU.subtract).then_inc(s_bias, 1)

            def rest(s):
                for n in range(2):
                    e.wait_ge(s_high, 2 * s.i + 1 + n)
                    if not s.fresh and n == 0:
                        e.wait_ge(s_out, s.i - 1)
                    part = slice(n * half, (n + 1) * half)
                    e.scalar_tensor_tensor(out=low[s.u][:, part, :], in0=h_ps[s.u][:, part, :], scalar=0.0,
                                           in1=high[s.u][:, part, :], op0=ALU.max, op1=ALU.subtract).then_inc(s_low, 1)
                if not s.zero:
                    total(e, s.prev())
            paired(e, MT, rest)
            total(e, Step(MT // 2, 0))

        @block.tensor
        def _(e):
            e.wait_ge(s_bias, 1)
            e.wait_ge(s_sel, 3)
            turn(e, Step(0, 0))

            known = {}

            def step(s):
                if s.u == 0:
                    _, x = nc.values_load_multi_w_load_instructions(
                        c.experts[0:1, bass.ds(s.j, 1), 0:3], engines=[mybir.EngineType.PE], min_val=0, max_val=NE - 1)
                    known[-1], known[0], known[1] = x
                if s.more:
                    turn(e, s.next())
                for m in range(HB):
                    first(e, s, known[s.u], m)
                    if not s.zero:
                        for n in BEHIND[m]:
                            second(e, s.prev(), known[s.u - 1], n)
            paired(e, MT, step)
            for m in range(HB):
                second(e, Step(MT // 2, 0), known[0], m)


def combine(nc, c, A, out):
    G = 7
    steps = NT // G
    big, misc = Arena(c.big, 4 * 8192), Arena(c.misc, MISC)
    ys = [big.take(G * TOP * D).rearrange("p (t k d) -> p t k d", t=G, k=TOP) for _ in range(2)]
    b2 = matrix(big.take(G * D), G, D)
    cb = [misc.take(P) for _ in range(2)]
    cbT = [misc.take(P) for _ in range(2)]
    pairs = -(-G // 2)
    S = lambda name: c.sem("combine_" + name)
    s_b2, s_z, s_cb, s_ct, s_cbT, s_b, s_v, s_o, s_st = map(S, (
        "b2", "zero", "cb", "ct", "cbT", "b", "vector", "o", "store"))
    s_y = [S("y0"), S("y1")]
    b_ps = [matrix(c.bank[m], 2, D) for m in range(pairs)]
    ct_ps = [c.bank[pairs], c.bank[pairs + 1]]
    tiles = lambda s, n, k: bass.ds(s.i * G + n, k)
    with nc.Block() as block:
        @block.sync
        def _(e):
            def load(s):
                if not s.fresh:
                    e.wait_ge(s_o, pairs * (s.i - 1))
                full = G if s.more else G - 1
                for n, size, to in ((s.i * G * P, full * P, ys[s.u][:, 0:full]), (N - TAIL, TAIL, ys[s.u][0:TAIL, G - 1:G])):
                    if size:
                        e.dma_start(to.rearrange("p t k d -> p t (k d)"),
                                    c.y_d[bass.ds(TOP * n, TOP * size), :].rearrange(
                                        "(t p k) d -> p t (k d)", p=min(P, size), k=TOP)).then_inc(s_y[s.u], 16)
                    if s.more:
                        break
            paired(e, steps, load)

        @block.scalar
        def _(e):
            def shares(s):
                if not s.fresh:
                    e.wait_ge(s_ct, s.i - 1)
                e.copy(matrix(cb[s.u][:, 0:G * NE], G, NE), c.share[:, tiles(s, 0, G), :]).then_inc(s_cb, 1)
                if not s.fresh:
                    e.wait_ge(s_b, pairs * (s.i - 1))
                e.wait_ge(s_ct, s.i + 1)
                e.copy(cbT[s.u], ct_ps[s.u][:, 0:P]).then_inc(s_cbT, 1)

            e.wait_ge(s_z, 3)
            for t in range(G):
                e.dma_start(b2[t * NE:t * NE + NE, t, :], A["b2"]).then_inc(s_b2, 16)
            paired(e, steps, shares)

        @block.gpsimd
        def _(e):
            with e.Fori(0, steps - 1) as i:
                e.wait_ge(s_o, pairs * (i + 1))
                e.dma_start(out[bass.ds(i * (G * P), G * P), :].rearrange("(t p) d -> p t d", p=P),
                            c.acc3[:, bass.ds(i * G, G), :]).then_inc(s_st, 16)
            e.wait_ge(s_o, pairs * steps)
            e.dma_start(out[N - TAIL - (G - 1) * P:N - TAIL, :].rearrange("(t p) d -> p t d", p=P),
                        c.acc3[:, NT - G:NT - 1, :]).then_inc(s_st, 16)
            e.dma_start(out[N - TAIL:N, :], c.acc3[0:TAIL, NT - 1, :]).then_inc(s_st, 16)
            e.wait_ge(s_st, 16 * (steps + 1))

        @block.vector
        def _(e):
            v = Chain(e, s_v)
            for t in (cb[0], cb[1], b2):
                e.memset(t, 0.0).then_inc(s_z, 1)

            def add(s):
                e.wait_ge(s_y[s.u], 16 * (s.j + (1 if s.more else 2)))
                for k in range(TOP):
                    for n in range(G):
                        t = tiles(s, n, 1)
                        a = c.acc3[:, t, :]
                        l = e.scalar_tensor_tensor(out=a, in0=ys[s.u][:, n:n + 1, k, :], scalar=c.prob[k][:, t], in1=a,
                                                   op0=ALU.mult, op1=ALU.add)
                        v.add(l)
                    v.sync()
                for m in range(pairs):
                    e.wait_ge(s_b, pairs * s.i + m + 1)
                    k = min(2, G - 2 * m)
                    a = c.acc3[:, tiles(s, 2 * m, k), :]
                    e.tensor_tensor(a, b_ps[m][:, 0:k, :], a, ALU.add).then_inc(s_o, 1)
            paired(e, steps, add, v, TOP * G)

        @block.tensor
        def _(e):
            e.wait_ge(s_b2, 16 * G)

            def bias(s):
                e.wait_ge(s_cb, s.i + 1)
                if not s.fresh:
                    e.wait_ge(s_cbT, s.i - 1)
                e.transpose(ct_ps[s.u][:, 0:P], cb[s.u], c.ident).then_inc(s_ct, 1)
                e.wait_ge(s_cbT, s.i + 1)
                for n in range(G):
                    if n % 2 == 0 and not s.zero:
                        e.wait_ge(s_o, pairs * (s.i - 1) + n // 2 + 1)
                    l = e.matmul(b_ps[n // 2][:, n % 2, :], cbT[s.u], b2[:, n, :], start=True, stop=True)
                    if n % 2 or n == G - 1:
                        l.then_inc(s_b, 1)
            paired(e, steps, bias)


_INS = ["x", "src", "dst", "edge_weight", "gnn_wT", "gnn_b", "q_wT", "kv_wT", "proj_wT", "proj_b",
        "gate_wT", "gate_b", "w1T", "b1", "w2T", "b2"]


def kernel(**inputs):
    import numpy as _np
    import concourse.bacc as _bacc
    from concourse import mybir as _mybir
    from concourse.bass_utils import run_bass_kernel_spmd as _run

    a = {k.replace("L0_", ""): _np.asarray(v) for k, v in inputs.items()}
    rows = lambda w: w.reshape(DH, P, -1).transpose(1, 0, 2)
    lay = {"x": a["x"], "src": a["src"], "dst": a["dst"], "edge_weight": a["edge_weight"],
           "gnn_wT": rows(a["gnn_W"].T), "gnn_b": a["gnn_b"].reshape(1, D),
           "q_wT": rows(a["mix_Wq"].T), "kv_wT": rows(a["mix_Wkv"].T),
           "proj_wT": rows(a["mix_Wproj"].T), "proj_b": a["mix_bproj"].reshape(1, D),
           "gate_wT": rows(a["ffn_Wg"].T), "gate_b": a["ffn_bg"].reshape(1, NE),
           "w1T": a["ffn_W1"].transpose(2, 0, 1).reshape(DH, P, NE * H).transpose(1, 0, 2),
           "b1": a["ffn_b1"],
           "w2T": a["ffn_W2"].transpose(2, 0, 1).reshape(HB, P, NE * D).transpose(1, 0, 2),
           "b2": a["ffn_b2"]}
    nc = _bacc.Bacc("TRN2", target_bir_lowering=False, num_devices=1)
    arrays, args = {}, {}
    for name in _INS:
        arrays["in_" + name] = _np.ascontiguousarray(lay[name])
        args[name] = nc.dram_tensor("in_" + name, lay[name].shape, _mybir.dt.from_np(lay[name].dtype),
                                    kind="ExternalInput").ap()
    out = nc.dram_tensor("out0", (N, D), F32, kind="ExternalOutput").ap()
    build(nc, args, out, STAGE)
    return _run(nc, [arrays], core_ids=[0]).results[0]["out0"]


STAGE = 4
```

```python
import numpy as np
import concourse.bass as bass
from concourse import mybir
from contextlib import ExitStack

F32, F16, I32, U32, U16 = (mybir.dt.float32, mybir.dt.float16, mybir.dt.int32, mybir.dt.uint32, mybir.dt.uint16)
ALU = mybir.AluOpType
ACT = mybir.ActivationFunctionType
AX = mybir.AxisListType

P = 128
N, D = 6250, 256
NT = -(-N // P)
TAIL = N - (NT - 1) * P
NP = NT * P
E = 100000
EF = E // P
EC = EF + 1
ER = E - EF * P
ETM = (E + NT * (P - 1)) // P
UG, HG, QG = 12, 6, 6
ET = -(-ETM // (2 * UG)) * 2 * UG
W = 3
US = 17
assert EC % (2 * US) == 0
EARLY = 4 * US
NE, H, TOP = 8, 1024, 2
MT = (TOP * N + NE * (P - 1)) // P
HB = H // P
DH = D // P
HEAD = 32
EPS = 1e-5
DEN_MIN = 1e-6
MISC = 3924
CH = DH * NE * H // 1024


class Arena:

    def __init__(self, t, cols):
        self.t, self.at, self.cols = t, 0, cols

    def take(self, n, dt=F32):
        words = n if dt in (F32, I32, U32) else -(-n // 2)
        words += words % 2
        a = self.t[:, self.at:self.at + words]
        self.at += words
        assert self.at <= self.cols, (self.at, self.cols)
        return (a if dt == F32 else a.bitcast(dt))[:, 0:n]


class Core:
    pass


def part_of(at, n):
    return slice(at, at + n) if isinstance(at, int) else bass.ds(at, n)


def matrix(a, n, m):
    return a.rearrange("p (n m) -> p n m", n=n, m=m)


class Chain:

    def __init__(self, e, sem):
        self.e, self.sem, self.n, self.k = e, sem, 0, 0

    def enter(self, i, per):
        self.before = self.n + self.k
        self.n, self.k, self.per = self.before + i * per, 0, per

    def leave(self, trips):
        assert self.k == self.per, (self.k, self.per)
        self.n, self.k = self.before + trips * self.per, 0

    def add(self, ins):
        self.k += 1
        ins.then_inc(self.sem, 1)

    def sync(self):
        self.e.wait_ge(self.sem, self.n + self.k)

    def link(self, ins):
        self.add(ins)
        self.sync()


def build(nc, A, out):
    ctx = ExitStack()
    with ctx:
        c = Core()
        c.sem = lambda name: ctx.enter_context(nc.semaphore(name))
        sb = lambda name, n, dt=F32: ctx.enter_context(nc.sbuf_tensor(name, [P, n], dt))
        c.acc = sb("acc", NT * D)
        c.big = sb("big", 4 * 8192)
        c.rec = sb("rec", ET * W, I32)
        c.pos = sb("pos", ET, I32)
        c.misc = sb("misc", MISC)
        edge = Arena(c.misc, MISC)
        c.to = [edge.take(US, I32) for _ in range(2)]
        c.what = [edge.take(US * W, I32) for _ in range(2)]
        c.misc_free = edge.at
        k = Arena(sb("consts", 424), 424)
        c.ident = k.take(P)
        c.ident16 = k.take(P, F16)
        c.before = k.take(P, F16)
        c.column = k.take(P)
        c.idx = [k.take(UG, I32) for _ in range(2)]
        c.spare = k.take(8)
        c.valid = k.take(1)
        c.scale = k.take(2)
        c.descale = k.take(2)
        ps = ctx.enter_context(nc.psum_tensor("ps", [P, 8 * 512], F32))
        c.bank = [ps[:, 512 * i:512 * i + 512] for i in range(8)]
        c.wide = [ps[:, 1024 * i:1024 * i + 1024] for i in range(4)]
        wide16 = c.big[:, :].bitcast(F16)
        c.w1 = [wide16[:, part * 16384:(part + 1) * 16384] for part in range(2)]
        c.w2 = wide16[:, 32768:65536]
        c.w2_parts = c.w2.rearrange("p (n a d) -> p n a d", a=2, d=D)
        c.acc3 = matrix(c.acc[:, :], NT, D)
        dram = lambda name, shape, dt=F32: nc.dram_tensor(name, shape, dt).ap()
        c.rec_d = dram("rec_d", (P * ET, W), I32)
        c.blk_d = dram("blk_d", (1, ET), I32)
        c.z_d = dram("z_d", (NP, D))
        c.tok_d = dram("tok_d", (NP, 2 * D), F16)
        c.y_d = dram("y_d", (TOP * NP + MT * P, D))
        rank(nc, c, A)
        mix(nc, c, A)
        graph(nc, c)
        route(nc, c, A)
        experts(nc, c, A)
        combine(nc, c, A, out)


def rank(nc, c, A):
    big, acc = Arena(c.big, 32768), Arena(c.acc, NT * D)
    onehot = matrix(big.take(NT * EC, F16), NT, EC)
    pick1 = matrix(big.take(NT * P, F16), NT, P)
    pick256 = matrix(big.take(NT * P, F16), NT, P)
    band = big.take(5 * P, F16)
    blanks = matrix(acc.take(ET * W, I32), ET, W)
    src, dst, wgt, blk_i = (acc.take(EC, I32) for _ in range(4))
    blk16 = acc.take(EC, F16)
    ones, upto, base = (acc.take(EC) for _ in range(3))
    base_i, part_i = (acc.take(EC, I32) for _ in range(2))
    lo16, hi16 = (acc.take(EC, F16) for _ in range(2))
    place = big.take(EC)
    number = big.take(64)
    tile_no = big.take(ET)
    tiles_f, start128, end = (big.take(2) for _ in range(3))
    tiles_i = big.take(2, I32)
    started = big.take(ET, F16)
    few = big.take(2, F16)
    before_f = big.take(P)
    blk_row = big.take(ET, I32)
    rec = matrix(c.rec[:, 0:EC * W], EC, W)
    counts, starts, row = c.wide[0], c.bank[2], c.wide[3]
    early = matrix(big.take(NT * EARLY), NT, EARLY)
    c.s_sc = [c.sem("scatter0"), c.sem("scatter1")]
    c.s_scatter = c.sem("scatter")
    s_load, s_out = (c.sem("rank_" + n) for n in ("load", "out"))
    s_preset, s_blank, s_k, s_hot, s_cnt, s_til, s_sta, s_end, s_row, s_base, s_pre, s_pos, s_rec, s_c, s_g, s_blkrow = (
        c.sem("rank_" + n) for n in ("preset", "blank", "consts", "hot", "counts", "tiles", "starts",
                                     "end", "row", "base", "prefix", "pos", "rec", "vector", "gpsimd", "blkrow"))
    cols, late = [(0, 512), (512, EC)], [(EARLY, 512), (512, EC)]
    inputs = ((src, A["src"]), (dst, A["dst"]), (wgt, A["edge_weight"].bitcast(I32)))
    one = lambda a: a.rearrange("p (a t) -> p a t", a=1)
    def choose(e, b, u):
        e.wait_ge(s_pre, b + 1)
        e.copy_predicated(place[:, EARLY:EC], onehot[:, b, EARLY:EC].bitcast(U16),
                          c.wide[u + 1][:, EARLY:EC]).then_inc(s_pos, 1)
        e.wait_ge(s_pos, b + 1)

    def places(e, b, u, free):
        if free:
            e.wait_ge(s_pos, b - 1)
        for x, y in late:
            e.matmul(c.wide[u + 1][:, x:y], c.before, onehot[:, bass.ds(b, 1), x:y], start=True, stop=False)
            e.matmul(c.wide[u + 1][:, x:y], pick1[:, bass.ds(b, 1), :], lo16[:, x:y], start=False, stop=False)
            l = e.matmul(c.wide[u + 1][:, x:y], pick256[:, bass.ds(b, 1), :], hi16[:, x:y], start=False, stop=True)
        l.then_inc(s_pre, 1)

    def early_places(e, g):
        o = matrix(c.bank[3 + g % 3][:, 0:7 * EARLY], 7, EARLY)
        if g >= 3:
            e.wait_ge(s_early, g - 2)
        e.matmul(o, c.before, onehot[:, 7 * g:7 * g + 7, 0:EARLY], start=True, stop=False)
        for n in range(7):
            e.matmul(o[:, n, :], pick1[:, 7 * g + n, :], lo16[:, 0:EARLY], start=False, stop=False)
            l = e.matmul(o[:, n, :], pick256[:, 7 * g + n, :], hi16[:, 0:EARLY], start=False, stop=n == 6)
        l.then_inc(s_first, 1)

    def slots(e, v, x, y):
        v.link(e.tensor_copy(base_i[:, x:y], place[:, x:y]))
        v.add(e.tensor_scalar(part_i[:, x:y], base_i[:, x:y], 7, None, ALU.logical_shift_right))
        v.link(e.tensor_scalar(src[:, x:y], base_i[:, x:y], P - 1, None, ALU.bitwise_and))
        v.link(e.scalar_tensor_tensor(out=c.pos[:, x:y], in0=src[:, x:y], scalar=float(ET), in1=part_i[:, x:y],
                                      op0=ALU.mult, op1=ALU.add))

    s_first, s_early = c.sem("rank_first"), c.sem("rank_early")
    with nc.Block() as block:
        @block.sync
        def _(e):
            for t, a in inputs:
                e.dma_start(t[:, 0:EF], a[0:EF * P].rearrange("(p t) -> p t", p=P)).then_inc(s_load, 16)
            e.wait_ge(s_preset, 3)
            for t, a in inputs:
                e.dma_start(t[0:ER, EF:EC], a[EF * P:E].rearrange("(p t) -> p t", t=1)).then_inc(s_load, 16)
            e.wait_ge(s_blank, 2)
            e.dma_start(c.rec_d.rearrange("(p t) w -> p (t w)", p=P), blanks.rearrange("p t w -> p (t w)")).then_inc(s_out, 16)
            e.wait_ge(s_blkrow, 1)
            e.dma_start(c.blk_d, blk_row[0:1, :]).then_inc(s_out, 16)
            e.wait_ge(s_out, 32)

        @block.gpsimd
        def _(e):
            g = Chain(e, s_g)
            iota = lambda t, n: g.add(e.iota(t, pattern=[[1, n]], base=0, channel_multiplier=0,
                                             allow_small_or_imprecise_dtypes=True))
            select = lambda t, op, base, pattern, by: e.affine_select(
                out=t, in_=t, compare_op=op, fill=0.0, base=base, pattern=pattern, channel_multiplier=by).then_inc(s_k, 1)
            iota(number, 64)
            iota(tile_no, ET)
            iota(c.column, P)
            g.add(e.memset(pick1, 1.0))
            g.add(e.memset(c.ident, 1.0))
            g.add(e.memset(before_f, 1.0))
            g.add(e.memset(few, 1.0))
            g.add(e.memset(band, 0.0))
            g.sync()
            e.memset(band[:, P - 1:P], 1.0).then_inc(s_k, 1)
            select(pick1, ALU.is_equal, 0, [[-1, NT], [0, P]], 1)
            select(c.ident, ALU.is_equal, 0, [[-1, P]], 1)
            select(before_f, ALU.is_gt, 0, [[1, P]], -1)
            select(few, ALU.is_gt, NT - 1, [[0, 2]], -1)
            e.wait_ge(s_load, 96)
            e.tensor_copy(rec[:, :, 0], dst).then_inc(s_rec, 1)
            e.tensor_copy(rec[:, :, 2], wgt).then_inc(s_rec, 1)

        @block.vector
        def _(e):
            v = Chain(e, s_c)
            e.memset(src[:, EF:EC], NP + P).then_inc(s_preset, 1)
            e.memset(dst[:, EF:EC], 0).then_inc(s_preset, 1)
            e.memset(wgt[:, EF:EC], 0).then_inc(s_preset, 1)
            e.memset(blanks, 0).then_inc(s_blank, 1)
            v.add(e.memset(place, 0.0))
            v.add(e.memset(ones, 1.0))
            e.wait_ge(s_blank, 1)
            e.memset(blanks.bitcast(F32)[:, :, 1], -1.0).then_inc(s_blank, 1)
            e.wait_ge(s_g, 3)
            e.wait_ge(s_load, 96)
            v.link(e.tensor_scalar(blk_i, src, 7, None, ALU.logical_shift_right))
            v.link(e.tensor_copy(blk16, blk_i))
            with e.Fori(0, NT // 7) as i:
                for u in range(7):
                    b = i * 7 + u
                    e.tensor_scalar(onehot[:, bass.ds(b, 1), :], one(blk16), number[:, bass.ds(b, 1)], None,
                                    ALU.is_equal).then_inc(s_hot, 1)
            e.wait_ge(s_k, 5)
            e.tensor_copy(c.ident16, c.ident).then_inc(s_k, 1)
            e.tensor_copy(c.before, before_f).then_inc(s_k, 1)
            e.tensor_scalar(pick256, pick1, 256.0, None, ALU.mult).then_inc(s_k, 1)
            v.link(e.tensor_scalar(part_i, src, P - 1, None, ALU.bitwise_and))
            e.tensor_copy(rec.bitcast(F32)[:, :, 1], part_i).then_inc(s_rec, 1)
            e.wait_ge(s_cnt, 1)
            v.link(e.tensor_tensor_scan(upto, ones, counts[:, 0:EC], 0.0, ALU.mult, ALU.add))
            v.link(e.tensor_scalar(tiles_i[:, 0:1], upto[:, EC - 1:EC], P - 1.0, None, ALU.add))
            v.link(e.tensor_scalar(tiles_i[:, 1:2], tiles_i[:, 0:1], 7, None, ALU.logical_shift_right))
            e.tensor_copy(tiles_f[:, 0:1], tiles_i[:, 1:2]).then_inc(s_til, 1)
            e.wait_ge(s_til, 1)
            e.wait_ge(s_sta, 1)
            v.add(e.tensor_scalar(start128[:, 0:1], starts[:, 0:1], float(P), None, ALU.mult))
            v.link(e.tensor_tensor(end[:, 0:1], starts[:, 0:1], tiles_f[:, 0:1], ALU.add))
            e.tensor_scalar(started, tile_no, end[:, 0:1], None, ALU.is_ge).then_inc(s_end, 1)
            v.link(e.scalar_tensor_tensor(out=base, in0=upto, scalar=start128[:, 0:1], in1=counts[:, 0:EC],
                                          op0=ALU.add, op1=ALU.subtract))
            v.link(e.tensor_copy(base_i, base))
            v.link(e.tensor_scalar(part_i, base_i, 8, None, ALU.logical_shift_right))
            v.link(e.tensor_copy(hi16, part_i))
            v.link(e.tensor_scalar(part_i, base_i, 255, None, ALU.bitwise_and))
            e.tensor_copy(lo16, part_i).then_inc(s_base, 1)
            e.wait_ge(s_row, 1)
            e.tensor_scalar(blk_row[0:1, :], row[0:1, 0:ET], float(D), None, ALU.mult).then_inc(s_blkrow, 1)
            for g in range(NT // 7):
                e.wait_ge(s_first, g + 1)
                e.tensor_tensor(early[:, 7 * g:7 * g + 7, :], matrix(c.bank[3 + g % 3][:, 0:7 * EARLY], 7, EARLY),
                                onehot[:, 7 * g:7 * g + 7, 0:EARLY], ALU.mult).then_inc(s_early, 1)
            e.wait_ge(s_early, NT // 7)
            v.link(e.tensor_reduce(place[:, 0:EARLY], early.rearrange("p b t -> p t b"), AX.X, ALU.add))
            slots(e, v, 0, EARLY)
            c.ranked = v.n + v.k

        @block.tensor
        def _(e):
            e.wait_ge(s_k, 5)
            for x, y in cols:
                e.matmul(counts[:, x:y], band[:, P:2 * P], band[:, P:P + y - x], start=True, stop=False)
            with e.Fori(0, NT // 7) as i:
                for u in range(7):
                    b = i * 7 + u
                    e.wait_ge(s_hot, b + 1)
                    for x, y in cols:
                        e.matmul(counts[:, x:y], band[:, bass.ds(P - 1 - b, P)], onehot[:, bass.ds(b, 1), x:y],
                                 start=False, stop=False)
            for x, y in cols:
                l = e.matmul(counts[:, x:y], band[:, P:2 * P], band[:, P:P + y - x], start=False, stop=True)
            l.then_inc(s_cnt, 1)
            e.wait_ge(s_til, 1)
            e.matmul(starts[:, 0:1], before_f, tiles_f[:, 0:1], start=True, stop=True).then_inc(s_sta, 1)
            e.wait_ge(s_end, 1)
            e.matmul(row[0:1, 0:512], few[:, 0:1], started[:, 0:512], start=True, stop=True)
            e.matmul(row[0:1, 512:ET], few[:, 0:1], started[:, 512:ET], start=True, stop=True).then_inc(s_row, 1)
            e.wait_ge(s_k, 8)
            e.wait_ge(s_base, 1)
            for g in range(NT // 7):
                early_places(e, g)

    with nc.Block() as block:
        @block.gpsimd
        def _(e):
            g = Chain(e, c.s_scatter)
            g.link(e.memset(c.spare, 0.0))
            for j in range(EARLY // (2 * US)):
                scatter(e, g, c, j, first=j == 0)
            c.scattered = g.n + g.k

        @block.vector
        def _(e):
            v = Chain(e, s_c)
            v.n = c.ranked
            for b in range(NT):
                choose(e, b, b % 2)
            slots(e, v, EARLY, EC)

        @block.tensor
        def _(e):
            places(e, 0, 0, False)
            places(e, 1, 1, False)
            with e.Fori(1, (NT - 1) // 2) as i:
                for u in range(2):
                    places(e, i * 2 + u, u, True)
            places(e, NT - 1, 0, True)


class Step:

    def __init__(self, j, u, more=True):
        self.j, self.u, self.more, self.i = j, u, more, j * 2 + u
        self.zero = isinstance(j, int) and j == u == 0
        self.fresh = isinstance(j, int) and j == 0

    def next(self):
        return Step(self.j + self.u, 1 - self.u)

    def later(self, n):
        return Step(self.j + n // 2, self.u, self.more)

    def prev(self):
        return Step(self.j - 1 + self.u, 1 - self.u)


def paired(e, steps, body, chain=None, per=0):
    assert steps % 2
    body(Step(0, 0))
    body(Step(0, 1))
    with e.Fori(1, steps // 2) as j:
        if chain:
            chain.enter(j - 1, 2 * per)
        for u in range(2):
            body(Step(j, u))
    if chain:
        chain.leave(steps // 2 - 1)
    body(Step(steps // 2, 0, False))


def carry(e, g, spare):
    g.sync()
    g.add(e.tensor_tensor(spare[:, 4:6], spare[:, 0:2], spare[:, 2:4], ALU.add))


def scatter(e, g, c, j, first=False, tail=False):
    rec = matrix(c.rec[:, 0:EC * W], EC, W)
    for u in range(2):
        if not first:
            e.wait_ge(c.s_sc[u], 16 * US * j)
        at = (j * 2 + u) * US
        columns = part_of(at, US)
        g.add(e.tensor_copy(c.to[u], c.pos[:, columns]))
        g.add(e.tensor_copy(matrix(c.what[u], US, W), rec[:, columns, :]))
        carry(e, g, c.spare)
        for n in range(US):
            k = ER if tail and u == 1 and n == US - 1 else P
            e.indirect_dma_start(out=c.rec_d, out_offset=bass.IndirectOffsetOnAxis(ap=c.to[u][0:k, n:n + 1], axis=0),
                                 in_=c.what[u][0:k, n * W:n * W + W], in_offset=None).then_inc(c.s_sc[u], 16)


def stats(e, v, c, st, mean, var, s_var):
    with e.Fori(0, NT // 7) as i:
        v.enter(i, 7)
        for u in range(7):
            v.add(e.bn_stats(st[:, bass.ds(i * 7 + u, 1), :], c.acc3[:, bass.ds(i * 7 + u, 1), :]))
    v.leave(NT // 7)
    v.sync()
    v.add(e.tensor_tensor(mean, st[:, :, 1], st[:, :, 4], ALU.add))
    v.link(e.tensor_tensor(var, st[:, :, 1], st[:, :, 4], ALU.subtract))
    v.link(e.tensor_tensor(var, var, var, ALU.mult))
    v.add(e.tensor_scalar(var, var, 0.25, EPS, ALU.mult, ALU.add))
    v.link(e.tensor_tensor(st[:, :, 0], st[:, :, 2], st[:, :, 5], ALU.add))
    v.add(e.tensor_scalar(mean, mean, 0.5, None, ALU.mult))
    e.scalar_tensor_tensor(out=var, in0=st[:, :, 0], scalar=1.0 / D, in1=var, op0=ALU.mult, op1=ALU.add).then_inc(s_var, 1)


def mix(nc, c, A):
    big, misc = Arena(c.big, 32768), Arena(c.misc, MISC)
    qT = matrix(big.take(DH * NP), DH, NP)
    wq, wk, wp = (matrix(big.take(DH * D), DH, D) for _ in range(3))
    wvz = matrix(big.take(DH * 2 * D), DH, 2 * D)
    context, ksum = (matrix(big.take(DH * P), DH, P) for _ in range(2))
    heads = big.take(P)
    st = matrix(big.take(NT * 6), NT, 6)
    mean, var, std, rstd = (big.take(NT) for _ in range(4))
    xn = [big.take(D) for _ in range(2)]
    xT = [matrix(big.take(D), DH, P) for _ in range(2)]
    low, ex = big.take(2 * D), big.take(2 * D)
    kf = [big.take(D) for _ in range(2)]
    vo = [matrix(big.take(DH * (P + 1)), DH, P + 1) for _ in range(2)]
    zo = [big.take(D) for _ in range(2)]
    den = [big.take(D) for _ in range(2)]
    aT = [matrix(big.take(D), DH, P) for _ in range(2)]
    bias, ones, zeros = big.take(D), big.take(P), big.take(D + 4)
    valid = c.valid
    most = big.take(6)
    most2, clamp, s_f, both = (big.take(4) for _ in range(4))
    most2 = most2[:, 0:2]
    bits = big.take(2, I32)
    biases = big.take(NE * HB)
    assert big.at <= 24576
    big.at = 24576
    raw = big.take(8192)
    misc.at = c.misc_free
    part = [misc.take(1024) for _ in range(2)]
    S = lambda name: c.sem("mix_" + name)
    s_x, s_x0, s_w, s_raw, s_red, s_v, s_std = map(S, (
        "x", "x0", "weights", "raw", "reduced", "vector", "std"))
    s_xn, s_tr, s_xt, s_qk, s_vz, s_low, s_ex, s_kf, s_vo, s_zo, s_ctx = map(S, (
        "xn", "tr", "xt", "qk", "vz", "low", "ex", "kf", "vo", "zo", "ctx"))
    s_zs = [S("zstore0"), S("zstore1")]
    s_bd, s_nd, s_at, s_pj, s_add = map(S, ("bd", "nd", "at", "pj", "add"))
    s_mt, s_mr, s_mb, s_scale = map(S, ("most_t", "most_r", "most_b", "scale"))
    s_k, s_ones, s_var, s_b1, s_bmax, s_hi, s_lo = map(S, ("consts", "ones", "var", "b1", "most", "hi", "lo"))
    s_part = [S("part0"), S("part1")]
    qk_ps = [c.bank[0], c.bank[1]]
    vz_ps = [c.bank[2], c.bank[3]]
    tr_ps = [c.bank[4], c.bank[5]]
    ctx_ps = matrix(c.bank[6][:, 0:DH * (P + 1)], DH, P + 1)
    flat = {k: A[k].rearrange("p a b -> p (a b)") for k in ("w1T", "w2T")}
    last = NT - 1

    def pieces(layer, n, k):
        if layer == 0:
            return c.w1[n][:, bass.ds(k * 1024, 1024)]
        return c.w2_parts[:, bass.ds(k * (1024 // D), 1024 // D), n, :]

    def shaped(layer, a):
        return a if layer == 0 else matrix(a, 1024 // D, D)

    def norm(e, s):
        if not s.fresh:
            e.wait_ge(s_tr, s.i - 1)
        e.tensor_scalar(xn[s.u], c.acc3[:, bass.ds(s.i, 1), :], mean[:, bass.ds(s.i, 1)], rstd[:, bass.ds(s.i, 1)],
                        ALU.subtract, ALU.mult).then_inc(s_xn, 1)

    def features(e, s):
        if s.more:
            norm(e, s.next())
        e.wait_ge(s_qk, s.i + 1)
        e.tensor_scalar(low, qk_ps[s.u], 0.0, None, ALU.min).then_inc(s_low, 1)
        if not s.fresh:
            e.wait_ge(s_ctx, s.i - 1)
        e.wait_ge(s_ex, s.i + 1)
        e.scalar_tensor_tensor(out=kf[s.u], in0=qk_ps[s.u][:, D:2 * D], scalar=0.0, in1=ex[:, D:2 * D],
                               op0=ALU.max, op1=ALU.add)
        e.scalar_tensor_tensor(out=qT[:, :, bass.ds(s.i * P, P)], in0=matrix(qk_ps[s.u][:, 0:D], DH, P), scalar=0.0,
                               in1=matrix(ex[:, 0:D], DH, P), op0=ALU.max, op1=ALU.add).then_inc(s_kf, 1)

    def add_to(e, s):
        e.wait_ge(s_pj, s.i + 1)
        e.tensor_tensor(c.acc3[:, bass.ds(s.i, 1), :], c.acc3[:, bass.ds(s.i, 1), :],
                        vz_ps[s.u][:, 0:D].rearrange("p (a d) -> p a d", a=1), ALU.add).then_inc(s_add, 1)

    def xt_copy(e, s):
        e.wait_ge(s_tr, s.i + 1)
        if not s.fresh:
            e.wait_ge(s_vz, s.i - 1)
        e.copy(xT[s.u], matrix(tr_ps[s.u][:, 0:D], DH, P)).then_inc(s_xt, 1)

    def copies(e, s):
        if s.more:
            xt_copy(e, s.next())
        e.wait_ge(s_low, s.i + 1)
        if not s.zero:
            e.wait_ge(s_kf, s.i)
        e.activation(ex, low, ACT.Exp).then_inc(s_ex, 1)
        e.wait_ge(s_vz, s.i + 1)
        if not s.fresh:
            e.wait_ge(s_ctx, s.i - 1)
        if not s.more:
            for h in range(DH):
                e.copy(vo[s.u][:, h, P:P + 1], valid)
        e.copy(vo[s.u][:, :, 0:P], matrix(vz_ps[s.u][:, 0:D], DH, P)).then_inc(s_vo, 1)
        if not s.fresh:
            e.wait_ge(s_zs[s.u], 16 * s.j)
        e.copy(zo[s.u], vz_ps[s.u][:, D:2 * D]).then_inc(s_zo, 1)

    def turn(e, s):
        e.wait_ge(s_xn, s.i + 1)
        if not s.fresh:
            e.wait_ge(s_xt, s.i - 1)
        for h in range(DH):
            l = e.transpose(tr_ps[s.u][:, h * P:h * P + P], xn[s.u][:, h * P:h * P + P], c.ident)
        l.then_inc(s_tr, 1)

    def project(e, s):
        if s.more:
            turn(e, s.next())
        e.wait_ge(s_xt, s.i + 1)
        if not s.fresh:
            e.wait_ge(s_kf, s.i - 1)
        for m in range(DH):
            for h in range(DH):
                e.matmul(qk_ps[s.u][:, m * P:m * P + P], wq[:, h, m * P:m * P + P], xT[s.u][:, h, :], start=h == 0, stop=h == 1)
        for h in range(DH):
            l = e.matmul(qk_ps[s.u][:, D:2 * D], xT[s.u][:, h, :], wk[:, h, :], start=h == 0, stop=h == 1)
        l.then_inc(s_qk, 1)
        if not s.fresh:
            e.wait_ge(s_zo, s.i - 1)
        for h in range(DH):
            l = e.matmul(vz_ps[s.u], xT[s.u][:, h, :], wvz[:, h, :], start=h == 0, stop=h == 1)
        l.then_inc(s_vz, 1)
        if not s.zero:
            context_sum(e, s.prev())

    def context_sum(e, s):
        e.wait_ge(s_kf, s.i + 1)
        e.wait_ge(s_vo, s.i + 1)
        for h in range(DH):
            l = e.matmul(ctx_ps[:, h, :], kf[s.u][:, h * P:h * P + P], vo[s.u][:, h, :], start=False, stop=False)
        l.then_inc(s_ctx, 1)

    def attend(e, s):
        if not s.fresh:
            e.wait_ge(s_at, s.i - 1)
        for h in range(DH):
            e.matmul(qk_ps[s.u][:, h * P:h * P + P], context[:, h, :], qT[:, h, bass.ds(s.i * P, P)], start=True, stop=True)
            l = e.matmul(qk_ps[s.u][:, D + h * P:D + h * P + P], ksum[:, h, :], qT[:, h, bass.ds(s.i * P, P)], start=True, stop=True)
        l.then_inc(s_nd, 1)

    def out_proj(e, s):
        if s.more:
            attend(e, s.next())
        e.wait_ge(s_at, s.i + 1)
        if not s.fresh:
            e.wait_ge(s_add, s.i - 1)
        for h in range(DH):
            e.matmul(vz_ps[s.u][:, 0:D], aT[s.u][:, h, :], wp[:, h, :], start=h == 0, stop=False)
        e.matmul(vz_ps[s.u][:, 0:D], ones[0:2, :], bias[0:2, :], start=False, stop=True).then_inc(s_pj, 1)

    with nc.Block() as block:
        @block.sync
        def _(e):
            e.wait_ge(s_x0, 1)
            e.dma_start(c.acc3[:, 0:last, :], A["x"][0:last * P, :].rearrange("(t p) d -> p t d", p=P)).then_inc(s_x, 16)
            e.dma_start(c.acc3[0:TAIL, last, :], A["x"][last * P:N, :]).then_inc(s_x, 16)
            e.dma_start(wq, A["q_wT"]).then_inc(s_w, 16)
            e.dma_start(wk, A["kv_wT"][:, :, 0:D]).then_inc(s_w, 16)
            e.dma_start(wvz[:, :, 0:D], A["kv_wT"][:, :, D:2 * D]).then_inc(s_w, 16)
            e.dma_start(wvz[:, :, D:2 * D], A["gnn_wT"]).then_inc(s_w, 16)
            e.dma_start(wp, A["proj_wT"]).then_inc(s_w, 16)
            e.dma_start(bias[0:1, :], A["proj_b"]).then_inc(s_w, 16)
            e.dma_start(bias[1:2, :], A["gnn_b"]).then_inc(s_w, 16)
            e.dma_start(raw, flat["w1T"][:, 0:8192]).then_inc(s_raw, 16)
            e.dma_start(biases, A["b1T"]).then_inc(s_b1, 16)
            e.wait_ge(s_red, 1)
            e.dma_start(raw, flat["w1T"][:, 8192:16384]).then_inc(s_raw, 16)

            def store(s):
                e.wait_ge(s_zo, s.i + 1)
                e.dma_start(c.z_d[bass.ds(s.i * P, P), :], zo[s.u]).then_inc(s_zs[s.u], 16)
            paired(e, NT, store)
            for r in (2, 3):
                e.wait_ge(s_red, r)
                e.dma_start(raw, flat["w2T"][:, (r - 2) * 8192:(r - 1) * 8192]).then_inc(s_raw, 16)
            for layer, name in enumerate(("w1T", "w2T")):
                def load(k, u):
                    e.dma_start(part[u], flat[name][:, bass.ds(k * 1024, 1024)]).then_inc(s_part[u], 16)
                if layer == 0:
                    load(0, 0)
                    load(1, 1)
                with e.Fori(1 - layer, CH // 2) as j:
                    for u in range(2):
                        e.wait_ge(s_lo, CH * layer + j * 2 + u - 1)
                        load(j * 2 + u, u)
            e.wait_ge(s_zs[0], 16 * (NT // 2 + 1))
            e.wait_ge(s_zs[1], 16 * (NT // 2))

        @block.gpsimd
        def _(e):
            g = Chain(e, c.s_scatter)
            g.n = c.scattered
            g.link(e.memset(valid, 1.0))
            e.affine_select(out=valid, in_=valid, compare_op=ALU.is_gt, fill=0.0, base=TAIL,
                            pattern=[[0, 1]], channel_multiplier=-1).then_inc(s_k, 1)
            trips = EC // (2 * US)
            with e.Fori(EARLY // (2 * US), trips - 1) as j:
                g.enter(j - EARLY // (2 * US), 6)
                scatter(e, g, c, j)
            g.leave(trips - 1 - EARLY // (2 * US))
            scatter(e, g, c, trips - 1, tail=True)
            for u in range(2):
                e.wait_ge(c.s_sc[u], 16 * US * trips)

        @block.vector
        def _(e):
            v = Chain(e, s_v)
            e.memset(c.acc3[:, last, :], 0.0).then_inc(s_x0, 1)
            e.memset(zeros, 0.0).then_inc(s_ones, 1)
            v.link(e.memset(heads, 0.0))
            for a in range(0, P, HEAD):
                v.add(e.memset(heads[a:a + HEAD, a:a + HEAD], 1.0))
            for t in (ones, vo[0], vo[1]):
                e.memset(t, 1.0).then_inc(s_ones, 1)
            e.wait_ge(s_x, 32)
            stats(e, v, c, st, mean, var, s_var)
            e.wait_ge(s_std, 1)
            v.link(e.reciprocal(rstd, std))
            e.wait_ge(s_raw, 16)
            e.tensor_reduce(most[:, 0:1], raw, AX.X, ALU.max, apply_absolute_value=True).then_inc(s_red, 1)
            norm(e, Step(0, 0))
            paired(e, NT, lambda s: features(e, s))
            e.wait_ge(s_ctx, NT + 1)
            for h in range(DH):
                v.add(e.tensor_tensor(context[:, h, :], ctx_ps[:, h, 0:P], heads, ALU.mult))
                l = e.tensor_scalar(ksum[:, h, :], heads, ctx_ps[:, h, P:P + 1], None, ALU.mult)
            l.then_inc(s_bd, 1)
            e.wait_ge(s_raw, 32)
            e.tensor_reduce(most[:, 1:2], raw, AX.X, ALU.max, apply_absolute_value=True).then_inc(s_red, 1)

            def attention(s):
                e.wait_ge(s_nd, s.i + 1)
                if not s.fresh:
                    e.wait_ge(s_pj, s.i - 1)
                v.link(e.tensor_scalar(den[s.u], qk_ps[s.u][:, D:2 * D], DEN_MIN, None, ALU.max))
                v.link(e.reciprocal(den[s.u], den[s.u]))
                e.tensor_tensor(aT[s.u], matrix(qk_ps[s.u][:, 0:D], DH, P), matrix(den[s.u], DH, P), ALU.mult).then_inc(s_at, 1)
                if not s.zero:
                    add_to(e, s.prev())
            paired(e, NT, attention, v, 2)
            add_to(e, Step(NT // 2, 0))
            for r in (2, 3):
                e.wait_ge(s_raw, 16 * (r + 1))
                e.tensor_reduce(most[:, r:r + 1], raw, AX.X, ALU.max, apply_absolute_value=True).then_inc(s_red, 1)
            e.wait_ge(s_b1, 16)
            v.link(e.tensor_reduce(most[:, 4:5], biases, AX.X, ALU.max, apply_absolute_value=True))
            e.wait_ge(s_red, 4)
            v.link(e.tensor_tensor(most2, most[:, 0:4:2], most[:, 1:4:2], ALU.max))
            e.tensor_tensor(most2[:, 0:1], most2[:, 0:1], most[:, 4:5], ALU.max).then_inc(s_bmax, 1)
            e.wait_ge(s_mt, 1)
            v.link(e.tensor_reduce(clamp[0:2, 0:1], c.bank[7][0:2, 0:P], AX.X, ALU.max))
            v.link(e.tensor_scalar(clamp[0:2, 0:1], clamp[0:2, 0:1], 2.0 ** -60, 2.0 ** 60, ALU.max, ALU.min))
            v.link(e.tensor_scalar(bits[0:2, 0:1], clamp[0:2, 0:1].bitcast(I32), 0x7F800000, None, ALU.bitwise_and))
            v.add(e.tensor_scalar(s_f[0:2, 0:1].bitcast(I32), bits[0:2, 0:1], -1.0, 257.0 * 2 ** 23, ALU.mult, ALU.add))
            v.link(e.tensor_scalar(s_f[0:2, 1:2].bitcast(I32), bits[0:2, 0:1], 3.0 * 2 ** 23, None, ALU.subtract))
            v.add(e.tensor_scalar(both[0:2, 0:2], c.ident[0:2, 0:2], s_f[0:2, 0:1], None, ALU.mult))
            e.tensor_scalar(both[0:2, 2:4], c.ident[0:2, 0:2], s_f[0:2, 1:2], None, ALU.mult).then_inc(s_mr, 1)
            e.wait_ge(s_mb, 1)
            v.link(e.tensor_copy(c.scale, c.bank[7][:, 256:258]))
            v.link(e.tensor_copy(c.descale, c.bank[7][:, 258:260]))
            v.add(e.tensor_tensor(c.descale[:, 1:2], c.descale[:, 0:1], c.descale[:, 1:2], ALU.mult))
            v.sync()
            e.nop().then_inc(s_scale, 1)

            def low_part(layer, j, u):
                k = j * 2 + u
                e.wait_ge(s_hi, CH * layer + k + 1)
                e.scalar_tensor_tensor(out=pieces(layer, 1, k), in0=shaped(layer, part[u]), scalar=c.scale[:, layer:layer + 1],
                                       in1=pieces(layer, 0, k), op0=ALU.mult, op1=ALU.subtract).then_inc(s_lo, 1)
            for layer in range(2):
                with e.Fori(0, CH // 2) as j:
                    for u in range(2):
                        low_part(layer, j, u)

        @block.scalar
        def _(e):
            e.wait_ge(s_var, 1)
            e.activation(std, var, ACT.Sqrt).then_inc(s_std, 1)
            xt_copy(e, Step(0, 0))
            e.wait_ge(s_k, 1)
            e.wait_ge(s_ones, 4)
            paired(e, NT, lambda s: copies(e, s))
            e.wait_ge(s_scale, 1)
            for layer in range(2):
                with e.Fori(0, CH // 2) as j:
                    for u in range(2):
                        k = j * 2 + u
                        e.wait_ge(s_part[u], 16 * (CH // 2 * layer + j + 1))
                        e.activation(pieces(layer, 0, k), shaped(layer, part[u]), ACT.Copy,
                                     scale=c.scale[:, layer:layer + 1]).then_inc(s_hi, 1)

        @block.tensor
        def _(e):
            e.wait_ge(s_w, 16 * 7)
            e.wait_ge(s_ones, 4)
            e.matmul(ctx_ps, zeros[:, 0:P], matrix(zeros[:, 0:DH * (P + 1)], DH, P + 1), start=True, stop=False)
            turn(e, Step(0, 0))
            paired(e, NT, lambda s: project(e, s))
            context_sum(e, Step(NT // 2, 0))
            e.matmul(ctx_ps, zeros[:, 0:P], matrix(zeros[:, 0:DH * (P + 1)], DH, P + 1), start=False, stop=True).then_inc(s_ctx, 1)
            e.wait_ge(s_bd, 1)
            e.wait_ge(s_zo, NT)
            attend(e, Step(0, 0))
            paired(e, NT, lambda s: out_proj(e, s))
            e.wait_ge(s_bmax, 1)
            e.transpose(c.bank[7][0:2, 0:P], most2, c.ident).then_inc(s_mt, 1)
            e.wait_ge(s_mr, 1)
            e.matmul(c.bank[7][:, 256:260], ones[0:2, :], both[0:2, :], start=True, stop=True).then_inc(s_mb, 1)


def graph(nc, c):
    misc = Arena(c.misc, MISC)
    rows = [misc.take(D) for _ in range(UG)]
    hot = [misc.take(P) for _ in range(HG)]
    near = [matrix(misc.take(UG * 2), UG, 2) for _ in range(2)]
    rec, rec_f = matrix(c.rec[:, :], ET, W), matrix(c.rec[:, :].bitcast(F32), ET, W)
    turns, LEAD = ET // UG, HG // 2
    S = lambda name: c.sem("graph_" + name)
    s_rec, s_near, s_idx, s_blk, s_g = map(S, ("rec", "near", "idx", "blk", "gpsimd"))
    s_row, s_mm, s_add = ([S(f"{name}{k}") for k in range(UG)] for name in ("row", "mm", "add"))
    s_hot = S("hot")
    idx, spare = c.idx, c.spare
    with nc.Block() as block:
        @block.sync
        def _(e):
            e.dma_start(c.rec[:, :], c.rec_d.rearrange("(p t) w -> p (t w)", p=P)).then_inc(s_rec, 16)
            e.dma_start(c.pos[0:1, :], c.blk_d).then_inc(s_blk, 16)

        def fetch(e, q, u):
            part = part_of(q * UG, UG)
            e.copy(idx[u], rec[:, part, 0]).then_inc(s_idx, 1)
            e.copy(near[u], rec_f[:, part, 1:3]).then_inc(s_near, 1)

        @block.scalar
        def _(e):
            e.wait_ge(s_rec, 16)
            fetch(e, 0, 0)
            fetch(e, 1, 1)
            with e.Fori(1, turns // 2) as j:
                for u in range(2):
                    q = j * 2 + u
                    e.wait_ge(s_mm[UG - 1], q - 1)
                    fetch(e, q, u)

        def gather(e, g, q, u):
            for k in range(UG):
                if k % QG == 0:
                    if k == 0:
                        e.wait_ge(s_idx, q + 1)
                    if not (isinstance(q, int) and q == 0):
                        e.wait_ge(s_mm[k + QG - 1], q)
                    carry(e, g, spare)
                e.indirect_dma_start(out=rows[k], out_offset=None, in_=c.z_d,
                                     in_offset=bass.IndirectOffsetOnAxis(ap=idx[u][:, k:k + 1], axis=0)).then_inc(s_row[k], 16)

        @block.gpsimd
        def _(e):
            g = Chain(e, s_g)
            gather(e, g, 0, 0)
            gather(e, g, 1, 1)
            with e.Fori(1, turns // 2) as j:
                g.enter(j - 1, 2 * UG // QG)
                for u in range(2):
                    gather(e, g, j * 2 + u, u)
            g.leave(turns // 2 - 1)

        def one_hot(e, u, k):
            e.tensor_scalar(hot[k % HG], c.column, near[u][:, k, 0:1], near[u][:, k, 1:2],
                            ALU.is_equal, ALU.mult).then_inc(s_hot, 1)

        @block.vector
        def _(e):
            e.wait_ge(s_near, 1)
            e.wait_ge(s_blk, 16)
            for k in range(LEAD):
                one_hot(e, 0, k)

            def turn(q, u, more=True):
                _, starts = nc.values_load_multi_w_load_instructions(
                    c.pos[0:1, bass.ds(q * UG, UG)], engines=[mybir.EngineType.DVE], min_val=0, max_val=(NT - 1) * D)
                for k in range(UG):
                    n = k + LEAD
                    if n == UG and more:
                        e.wait_ge(s_near, q + 2)
                    if n < UG:
                        one_hot(e, u, n)
                    elif more:
                        one_hot(e, 1 - u, n - UG)
                    rows_of = c.acc[:, bass.ds(starts[k], D)]
                    e.wait_ge(s_mm[k], q + 1)
                    if k:
                        e.wait_ge(s_add[k - 1], q + 1)
                    elif not (isinstance(q, int) and q == 0):
                        e.wait_ge(s_add[UG - 1], q)
                    e.tensor_tensor(rows_of, rows_of, c.bank[k % HG][:, 0:D], ALU.add).then_inc(s_add[k], 1)
            turn(0, 0)
            turn(1, 1)
            with e.Fori(1, turns // 2 - 1) as j:
                turn(j * 2, 0)
                turn(j * 2 + 1, 1)
            turn(turns - 2, 0)
            turn(turns - 1, 1, False)

        @block.tensor
        def _(e):
            with e.Fori(0, turns) as q:
                for k in range(UG):
                    e.wait_ge(s_hot, q * UG + k + 1)
                    e.wait_ge(s_row[k], 16 * (q + 1))
                    e.matmul(c.bank[k % HG][:, 0:D], hot[k % HG], rows[k], start=True, stop=True).then_inc(s_mm[k], 1)


def route(nc, c, A):
    misc, more, pos = Arena(c.misc, MISC), Arena(c.rec, ET * W), Arena(c.pos, ET)
    more.t = c.rec[:, :].bitcast(F32)
    pos.t = c.pos[:, :].bitcast(F32)
    c.prob = [pos.take(NT) for _ in range(TOP)]
    c.slot = [pos.take(NT, I32) for _ in range(TOP)]
    c.experts = matrix(pos.take(MT // 4 * 8, I32), MT // 4, 8)
    c.expert = pos.take(MT, I32)
    c.token = pos.take(MT, I32)
    c.dest = pos.take(MT, I32)
    c.share = matrix(more.take(NT * NE), NT, NE)
    st = matrix(more.take(NT * 6), NT, 6)
    mean, var, std, rstd = (more.take(NT) for _ in range(4))
    scores = matrix(more.take(NT * NE), NT, NE)
    shared = more.at
    wg = matrix(more.take(DH * NE), DH, NE)
    bg, ones = more.take(NE), more.take(P)
    xn = [misc.take(D) for _ in range(2)]
    xT = [matrix(misc.take(D), DH, P) for _ in range(2)]
    tok = [misc.take(2 * D, F16) for _ in range(2)]
    S = lambda name: c.sem("route_" + name)
    s_w, s_v, s_var, s_std, s_ones, s_xn, s_tr, s_xt, s_gate, s_hi, s_lo = map(S, (
        "weights", "vector", "var", "std", "ones", "xn", "tr", "xt", "gate", "hi", "lo"))
    s_score = S("score")
    s_st = [S("store0"), S("store1")]

    def score(e, s):
        e.wait_ge(s_gate, s.i + 1)
        e.copy(scores[:, bass.ds(s.i, 1), :], g_ps[s.u][:, 0:NE].rearrange("p (a t) -> p a t", a=1)).then_inc(s_score, 1)

    tr_ps, g_ps, bg_ps = [c.bank[4], c.bank[5]], [c.bank[0], c.bank[1]], c.bank[2][:, 0:NE]

    def norm(e, s):
        if not s.fresh:
            e.wait_ge(s_tr, s.i - 1)
            e.wait_ge(s_lo, s.i - 1)
        e.tensor_scalar(xn[s.u], c.acc3[:, bass.ds(s.i, 1), :], mean[:, bass.ds(s.i, 1)], rstd[:, bass.ds(s.i, 1)],
                        ALU.subtract, ALU.mult).then_inc(s_xn, 1)

    def turn(e, s):
        e.wait_ge(s_xn, s.i + 1)
        if not s.fresh:
            e.wait_ge(s_xt, s.i - 1)
        for h in range(DH):
            l = e.transpose(tr_ps[s.u][:, h * P:h * P + P], xn[s.u][:, h * P:h * P + P], c.ident)
        l.then_inc(s_tr, 1)

    def gate(e, s):
        if s.more:
            turn(e, s.next())
        e.wait_ge(s_xt, s.i + 1)
        if not s.fresh:
            e.wait_ge(s_score, s.i - 1)
        for h in range(DH):
            l = e.matmul(g_ps[s.u][:, 0:NE], xT[s.u][:, h, :], wg[:, h, :], start=h == 0, stop=h == DH - 1)
        l.then_inc(s_gate, 1)

    with nc.Block() as block:
        @block.sync
        def _(e):
            e.dma_start(wg, A["gate_wT"]).then_inc(s_w, 16)
            e.dma_start(bg[0:1, :], A["gate_b"]).then_inc(s_w, 16)

            def store(s):
                e.wait_ge(s_lo, s.i + 1)
                e.dma_start(c.tok_d[bass.ds(s.i * P, P), :], tok[s.u]).then_inc(s_st[s.u], 16)
            paired(e, NT, store)
            e.wait_ge(s_st[0], 16 * (NT // 2 + 1))
            e.wait_ge(s_st[1], 16 * (NT // 2))

        @block.vector
        def _(e):
            v = Chain(e, s_v)
            e.memset(ones, 1.0).then_inc(s_ones, 1)
            stats(e, v, c, st, mean, var, s_var)
            e.wait_ge(s_std, 1)
            v.link(e.reciprocal(rstd, std))
            norm(e, Step(0, 0))

            def split(s):
                if s.more:
                    norm(e, s.next())
                e.wait_ge(s_hi, s.i + 1)
                e.tensor_tensor(tok[s.u][:, D:2 * D], xn[s.u], tok[s.u][:, 0:D], ALU.subtract).then_inc(s_lo, 1)
            paired(e, NT, split)

        @block.scalar
        def _(e):
            e.wait_ge(s_var, 1)
            e.activation(std, var, ACT.Sqrt).then_inc(s_std, 1)

            def copies(s):
                e.wait_ge(s_xn, s.i + 1)
                if not s.fresh:
                    e.wait_ge(s_st[s.u], 16 * s.j)
                e.copy(tok[s.u][:, 0:D], xn[s.u]).then_inc(s_hi, 1)
                e.wait_ge(s_tr, s.i + 1)
                if not s.fresh:
                    e.wait_ge(s_gate, s.i - 1)
                e.copy(xT[s.u], matrix(tr_ps[s.u][:, 0:D], DH, P)).then_inc(s_xt, 1)
                if not s.zero:
                    score(e, s.prev())
            paired(e, NT, copies)
            score(e, Step(NT // 2, 0))

        @block.tensor
        def _(e):
            e.wait_ge(s_w, 32)
            e.wait_ge(s_ones, 1)
            e.matmul(bg_ps, ones[0:1, :], bg[0:1, :], start=True, stop=True)
            turn(e, Step(0, 0))
            paired(e, NT, lambda s: gate(e, s))

    misc.at = 0
    more.at = shared
    share = c.share
    hot = [matrix(more.take(NT * NE), NT, NE) for _ in range(TOP)]
    mask16 = matrix(more.take(NE * NT, F16), NE, NT)
    ones16 = more.take(P, F16)
    slots, after = matrix(misc.take(NE * NT), NE, NT), matrix(misc.take(NE * NT), NE, NT)
    by_token = matrix(misc.take(NT * NE), NT, NE)
    ones_row = misc.take(NE * NT)
    slot_f = [misc.take(NT) for _ in range(TOP)]
    last_e, past, tiles, ends, shift = (misc.take(NE) for _ in range(5))
    tiles_i = misc.take(2 * NE, I32)
    begun = matrix(misc.take(MT * (NE - 1)), MT, NE - 1)
    order = misc.take(MT)
    gap, ex, total = (misc.take(NT) for _ in range(3))
    best = [misc.take(NT) for _ in range(TOP)]
    rank_of = more.take(NE)
    lead = more.take(NT)
    above, sums = matrix(c.bank[0][:, 0:NE * NT], NE, NT), matrix(c.bank[1][:, 0:NE * NT], NE, NT)
    flat = lambda a: a.rearrange("p a b -> p (a b)")
    turned = lambda a: a.rearrange("p a b -> p b a")
    col = lambda a: a.rearrange("p (t a) -> p t a", a=1)
    s_c, s_mask, s_cnt, s_gap, s_ex = map(S, ("chain2", "mask", "counts", "gap", "ex"))
    with nc.Block() as block:
        @block.vector
        def _(e):
            v = Chain(e, s_c)
            v.add(e.memset(ones16, 1.0))
            v.add(e.memset(ones_row, 1.0))
            v.add(e.memset(past, 0.0))
            v.link(e.tensor_scalar(rank_of, c.column[:, 0:NE], -1.0, float(NE), ALU.mult, ALU.add))
            wide = [P, NT, NE]
            v.link(e.tensor_tensor(scores, scores, bg_ps.rearrange("p (a e) -> p a e", a=1).to_broadcast(wide), ALU.add))
            for k in range(TOP):
                v.link(e.tensor_reduce(best[k], scores, AX.X, ALU.max))
                v.link(e.tensor_tensor(hot[k], scores, col(best[k]).to_broadcast(wide), ALU.is_equal))
                v.link(e.tensor_tensor(by_token, hot[k], rank_of.rearrange("p (a e) -> p a e", a=1).to_broadcast(wide), ALU.mult))
                v.link(e.tensor_reduce(lead, by_token, AX.X, ALU.max))
                v.link(e.tensor_tensor(hot[k], by_token, col(lead).to_broadcast(wide), ALU.is_equal))
                if k == 0:
                    v.link(e.scalar_tensor_tensor(out=scores, in0=hot[0], scalar=-3e38, in1=scores, op0=ALU.mult, op1=ALU.add))
            e.tensor_tensor(gap, best[1], best[0], ALU.subtract).then_inc(s_gap, 1)
            for k in range(TOP):
                v.add(e.tensor_scalar(hot[k][:, NT - 1, :], hot[k][:, NT - 1, :], c.valid, None, ALU.mult))
            v.sync()
            e.tensor_tensor(turned(mask16), hot[0], hot[1], ALU.add).then_inc(s_mask, 1)
            e.wait_ge(s_ex, 1)
            v.link(e.tensor_scalar(total, ex, 1.0, None, ALU.add))
            v.link(e.reciprocal(c.prob[0], total))
            v.link(e.tensor_tensor(c.prob[1], ex, c.prob[0], ALU.mult))
            v.add(e.tensor_tensor(share, hot[0], col(c.prob[0]).to_broadcast([P, NT, NE]), ALU.mult))
            v.link(e.tensor_tensor(by_token, hot[1], col(c.prob[1]).to_broadcast([P, NT, NE]), ALU.mult))
            v.link(e.tensor_tensor(share, share, by_token, ALU.add))
            e.wait_ge(s_cnt, 1)
            v.link(e.tensor_tensor_scan(flat(after), ones_row, flat(sums), 0.0, ALU.mult, ALU.add))
            v.add(e.tensor_copy(last_e, after[:, :, NT - 1]))
            v.link(e.tensor_copy(past[:, 1:NE], after[:, 0:NE - 1, NT - 1]))
            v.add(e.tensor_tensor(slots, after, sums, ALU.subtract))
            v.link(e.tensor_tensor(tiles, last_e, past, ALU.subtract))
            v.link(e.tensor_tensor(slots, slots, above, ALU.add))
            v.link(e.tensor_scalar(tiles_i[:, 0:NE], tiles, P - 1.0, None, ALU.add))
            v.link(e.tensor_scalar(tiles_i[:, NE:2 * NE], tiles_i[:, 0:NE], 7, None, ALU.logical_shift_right))
            v.link(e.tensor_copy(tiles, tiles_i[:, NE:2 * NE]))
            v.link(e.tensor_tensor_scan(ends, ones_row[:, 0:NE], tiles, 0.0, ALU.mult, ALU.add))
            v.link(e.tensor_tensor(shift, ends, tiles, ALU.subtract))
            v.link(e.scalar_tensor_tensor(out=shift, in0=shift, scalar=float(P), in1=past, op0=ALU.mult, op1=ALU.subtract))
            v.link(e.tensor_tensor(slots, slots, col(shift).to_broadcast([P, NE, NT]), ALU.add))
            for k in range(TOP):
                v.link(e.tensor_tensor(by_token, hot[k], turned(slots), ALU.mult))
                v.link(e.tensor_reduce(slot_f[k], by_token, AX.X, ALU.add))
                v.link(e.tensor_copy(c.slot[k], slot_f[k]))
            v.link(e.tensor_tensor(begun, col(c.column[:, 0:MT]).to_broadcast([P, MT, NE - 1]),
                                   ends[:, 0:NE - 1].rearrange("p (a e) -> p a e", a=1).to_broadcast([P, MT, NE - 1]), ALU.is_ge))
            v.link(e.tensor_reduce(order, begun, AX.X, ALU.add))
            v.link(e.memset(c.experts, 0))
            for n in range(5):
                v.add(e.tensor_copy(c.experts[:, :, n], order[:, n:n + MT - 4:4]))
            v.add(e.tensor_copy(c.expert, order))
            c.routed = v.n + v.k

        @block.scalar
        def _(e):
            e.wait_ge(s_gap, 1)
            e.activation(ex, gap, ACT.Exp).then_inc(s_ex, 1)

        @block.tensor
        def _(e):
            e.wait_ge(s_mask, 1)
            e.wait_ge(s_c, 1)
            e.matmul(flat(above), c.before, flat(mask16), start=True, stop=True)
            e.matmul(flat(sums), ones16, flat(mask16), start=True, stop=True).then_inc(s_cnt, 1)

    misc.at, more.at = 0, shared
    number = [misc.take(NT) for _ in range(TOP)]
    nowhere = more.take(MT)
    empty, row_of = more.take(MT), more.take(MT)
    row_f, tile_f = ([matrix(misc.take(NT), NT // 7, 7) for _ in range(TOP)] for _ in range(2))
    part = misc.take(NT, I32)
    hot_row = [matrix(misc.take(7 * P), 7, P) for _ in range(2)]
    hot_tile = [matrix(misc.take(7 * MT), 7, MT) for _ in range(2)]
    who = c.bank[2][:, 0:MT]
    some = lambda a, g: a[:, part_of(g, 1), :].rearrange("p a (t b) -> p (a t) b", b=1)
    s_n, s_rows, s_tiles = map(S, ("number", "rows", "tiles"))
    s_used = [S("used0"), S("used1")]
    s_number = S("numbered")
    with nc.Block() as block:
        @block.gpsimd
        def _(e):
            for k in range(TOP):
                e.iota(number[k], pattern=[[TOP * P, NT]], base=k + 1, channel_multiplier=TOP,
                       allow_small_or_imprecise_dtypes=True).then_inc(s_n, 1)
            e.iota(nowhere, pattern=[[P, MT]], base=TOP * NP, channel_multiplier=1,
                   allow_small_or_imprecise_dtypes=True).then_inc(s_n, 1)

            def numbers(g):
                for k in range(TOP):
                    e.wait_ge(s_tiles, g * TOP + k + 1)
                    e.tensor_tensor(hot_tile[k], hot_tile[k], some(matrix(number[k], NT // 7, 7), g).to_broadcast([P, 7, MT]),
                                    ALU.mult).then_inc(s_number, 1)
            for g in range(NT // 7):
                numbers(g)

        @block.vector
        def _(e):
            v = Chain(e, s_c)
            v.n = c.routed
            e.wait_ge(s_n, TOP + 1)
            for k in range(TOP):
                v.add(e.tensor_tensor(number[k][:, NT - 1:NT], number[k][:, NT - 1:NT], c.valid, ALU.mult))
                v.link(e.tensor_scalar(part, c.slot[k], P - 1, None, ALU.bitwise_and))
                v.link(e.tensor_copy(flat(row_f[k]), part))
                v.link(e.tensor_scalar(part, c.slot[k], 7, None, ALU.logical_shift_right))
                v.link(e.tensor_copy(flat(tile_f[k]), part))

            def hots(g, first=False):
                for k in range(TOP):
                    if not first:
                        e.wait_ge(s_used[k], g)
                    e.tensor_tensor(hot_tile[k], c.column[:, 0:MT].rearrange("p (a t) -> p a t", a=1).to_broadcast([P, 7, MT]),
                                    some(tile_f[k], g).to_broadcast([P, 7, MT]), ALU.is_equal).then_inc(s_tiles, 1)
                    e.tensor_tensor(hot_row[k], c.column.rearrange("p (a t) -> p a t", a=1).to_broadcast([P, 7, P]),
                                    some(row_f[k], g).to_broadcast([P, 7, P]), ALU.is_equal).then_inc(s_rows, 1)
            hots(0, True)
            with e.Fori(1, NT // 7) as g:
                hots(g)
            for k in range(TOP):
                e.wait_ge(s_used[k], NT // 7)
            v.add(e.tensor_scalar(empty, who, 0.0, None, ALU.is_equal))
            v.sync()
            v.add(e.tensor_tensor(nowhere, empty, nowhere, ALU.mult))
            v.link(e.scalar_tensor_tensor(out=row_of, in0=who, scalar=-1.0, in1=empty, op0=ALU.add, op1=ALU.add))
            v.link(e.tensor_copy(c.dest, row_of))
            v.add(e.tensor_scalar(c.token, c.dest, TOP // 2, None, ALU.logical_shift_right))
            v.link(e.tensor_tensor(row_of, row_of, nowhere, ALU.add))
            v.link(e.tensor_copy(c.dest, row_of))

        @block.tensor
        def _(e):
            def sums(g, start=False, stop=False):
                for k in range(TOP):
                    e.wait_ge(s_rows, g * TOP + k + 1)
                    e.wait_ge(s_number, g * TOP + k + 1)
                    for n in range(7):
                        l = e.matmul(who, hot_row[k][:, n, :], hot_tile[k][:, n, :], start=start and k == n == 0,
                                     stop=stop and k == TOP - 1 and n == 6)
                    l.then_inc(s_used[k], 1)
            sums(0, start=True)
            with e.Fori(1, NT // 7 - 1) as g:
                sums(g)
            sums(NT // 7 - 1, stop=True)


def experts(nc, c, A):
    misc, more = Arena(c.misc, MISC), Arena(c.rec, ET * W)
    more.t = c.rec[:, :].bitcast(F32)
    xs = [misc.take(2 * D, F16) for _ in range(2)]
    xT = [matrix(misc.take(2 * D, F16), 2 * DH, P) for _ in range(2)]
    y, y2 = ([misc.take(D) for _ in range(2)] for _ in range(2))
    b1 = misc.take(NE * HB)
    b1x = [misc.take(HB) for _ in range(2)]
    hidden = matrix(misc.take(H), HB, P)
    more.at = NT * NE
    high, low = ([matrix(more.take(H, F16), HB, P) for _ in range(2)] for _ in range(2))
    S = lambda name: c.sem("experts_" + name)
    s_b, s_bias, s_bx, s_tr, s_xt, s_h, s_relu, s_high, s_low, s_out, s_y2, s_y, s_g = map(S, (
        "b1", "bias", "b1_x", "tr", "xt", "h", "relu", "high", "low", "out", "y2", "y", "gpsimd"))
    at, to = ([misc.take(1, I32) for _ in range(2)] for _ in range(2))
    AHEAD = 6
    s_xs, s_ys = [S("xs0"), S("xs1")], [S("ystore0"), S("ystore1")]
    tr_ps = [matrix(c.bank[u][:, 0:D].bitcast(F16), 2 * DH, P) for u in range(2)]
    h_ps = [matrix(c.wide[1 + u], HB, P) for u in range(2)]
    y_ps = [c.bank[6], c.bank[7]]
    half = HB // 2
    w1h, w1l = c.w1
    BEHIND = ((), (), (0,), (1,), (2,), (3, 4), (5,), (6, 7))

    def turn(e, s):
        e.wait_ge(s_xs[s.u], 16 * (s.j + 1))
        if not s.fresh:
            e.wait_ge(s_xt, s.i - 1)
        for n in range(2 * DH):
            l = e.transpose(tr_ps[s.u][:, n, :], xs[s.u][:, n * P:n * P + P], c.ident16)
        l.then_inc(s_tr, 1)

    def first(e, s, x, m):
        if m == 0:
            e.wait_ge(s_xt, s.i + 1)
        if not s.fresh and m % half == 0:
            e.wait_ge(s_relu, 2 * s.i - 3 + m // half)
        o = h_ps[s.u][:, m, :]
        for h in range(DH):
            at = bass.ds(x * H + (h * NE * H + m * P), P)
            e.matmul(o, w1h[:, at], xT[s.u][:, h, :], start=h == 0, stop=False)
            e.matmul(o, w1h[:, at], xT[s.u][:, DH + h, :], start=False, stop=False)
            l = e.matmul(o, w1l[:, at], xT[s.u][:, h, :], start=False, stop=h == DH - 1)
        if m % half == half - 1:
            l.then_inc(s_h, 1)

    def second(e, s, x, m):
        if m % half == 0:
            e.wait_ge(s_low, 2 * s.i + 1 + m // half)
        if m == 0 and not s.fresh:
            e.wait_ge(s_y, s.i - 1)
        at = x * (2 * D) + m * NE * 2 * D
        if m == HB - 1:
            e.matmul(y_ps[s.u][:, 0:D], low[s.u][:, m, :], c.w2[:, bass.ds(at, D)], start=False, stop=False)
        l = e.matmul(y_ps[s.u], high[s.u][:, m, :], c.w2[:, bass.ds(at, 2 * D)], start=m == 0, stop=m == HB - 1)
        if m < HB - 1:
            e.matmul(y_ps[s.u][:, 0:D], low[s.u][:, m, :], c.w2[:, bass.ds(at, D)], start=False, stop=False)
        else:
            l.then_inc(s_out, 1)

    def relu(e, s, x):
        e.copy(b1x[s.u], b1[:, bass.ds(x * HB, HB)]).then_inc(s_bx, 1)
        e.wait_ge(s_bx, s.i + 1)
        for n in range(2):
            e.wait_ge(s_h, 2 * s.i + 1 + n)
            if not s.zero:
                e.wait_ge(s_low, 2 * s.i - 1 + n)
            for m in range(n * half, (n + 1) * half):
                l = e.activation(hidden[:, m, :], h_ps[s.u][:, m, :], ACT.Relu, bias=b1x[s.u][:, m:m + 1])
            l.then_inc(s_relu, 1)

    def result(e, s):
        e.wait_ge(s_out, s.i + 1)
        if not s.fresh:
            e.wait_ge(s_ys[s.u], 16 * s.j)
        e.activation(y2[s.u], y_ps[s.u][:, D:2 * D], ACT.Copy, scale=c.descale[:, 1:2]).then_inc(s_y2, 1)

    def total(e, s):
        e.wait_ge(s_y2, s.i + 1)
        e.scalar_tensor_tensor(out=y[s.u], in0=y_ps[s.u][:, 0:D], scalar=c.descale[:, 1:2], in1=y2[s.u],
                               op0=ALU.mult, op1=ALU.add).then_inc(s_y, 1)

    with nc.Block() as block:
        @block.sync
        def _(e):
            e.dma_start(b1, A["b1T"]).then_inc(s_b, 16)

        @block.gpsimd
        def _(e):
            g = Chain(e, s_g)

            def gather(s):
                if not s.fresh:
                    e.wait_ge(s_tr, s.i - 1)
                g.add(e.tensor_copy(at[s.u], c.token[:, part_of(s.i, 1)]))
                carry(e, g, c.spare)
                e.indirect_dma_start(out=xs[s.u], out_offset=None, in_=c.tok_d,
                                     in_offset=bass.IndirectOffsetOnAxis(ap=at[s.u][:, 0:1], axis=0)).then_inc(s_xs[s.u], 16)

            def scatter(s):
                e.wait_ge(s_y, s.i + 1)
                if not s.fresh:
                    e.wait_ge(s_ys[s.u], 16 * s.j)
                g.add(e.tensor_copy(to[s.u], c.dest[:, bass.ds(s.i, 1)]))
                carry(e, g, c.spare)
                e.indirect_dma_start(out=c.y_d, out_offset=bass.IndirectOffsetOnAxis(ap=to[s.u][:, 0:1], axis=0),
                                     in_=y[s.u], in_offset=None).then_inc(s_ys[s.u], 16)

            def both(s):
                scatter(s)
                gather(s.later(AHEAD))
            for i in range(AHEAD):
                gather(Step(i // 2, i % 2))
            paired(e, MT - AHEAD, both, g, 4)
            for i in range(MT - AHEAD, MT):
                scatter(Step(i // 2, i % 2))
            e.wait_ge(s_ys[0], 16 * (MT // 2 + 1))
            e.wait_ge(s_ys[1], 16 * (MT // 2))

        @block.scalar
        def _(e):
            e.wait_ge(s_b, 16)
            e.activation(b1, b1, ACT.Copy, scale=c.scale[:, 0:1]).then_inc(s_bias, 1)
            e.wait_ge(s_bias, 1)
            known = {}

            def step(s):
                if s.u == 0:
                    some = slice(0, 1) if s.zero else part_of(s.i - 1, 2)
                    _, x = nc.values_load_multi_w_load_instructions(
                        c.expert[0:1, some], engines=[mybir.EngineType.Activation], min_val=0, max_val=NE - 1)
                    known[0], known[1] = x[0], x[-1]
                e.wait_ge(s_tr, s.i + 1)
                if not s.fresh:
                    e.wait_ge(s_h, 2 * s.i - 2)
                e.copy(xT[s.u], tr_ps[s.u]).then_inc(s_xt, 1)
                if not s.zero:
                    relu(e, s.prev(), known[s.u])
                    if not s.fresh:
                        result(e, s.prev().prev())
            paired(e, MT, step)
            relu(e, Step(MT // 2, 0), known[1])
            result(e, Step(MT // 2 - 1, 1))
            result(e, Step(MT // 2, 0))

        @block.vector
        def _(e):
            def rest(s):
                for n in range(2):
                    e.wait_ge(s_relu, 2 * s.i + 1 + n)
                    if not s.fresh and n == 0:
                        e.wait_ge(s_out, s.i - 1)
                    part = slice(n * half, (n + 1) * half)
                    e.tensor_copy(high[s.u][:, part, :], hidden[:, part, :]).then_inc(s_high, 1)
                    e.wait_ge(s_high, 2 * s.i + 1 + n)
                    e.tensor_tensor(low[s.u][:, part, :], hidden[:, part, :], high[s.u][:, part, :], ALU.subtract).then_inc(s_low, 1)
                if not s.zero:
                    total(e, s.prev())
            paired(e, MT, rest)
            total(e, Step(MT // 2, 0))

        @block.tensor
        def _(e):
            def step(s, x, before):
                if s.more:
                    turn(e, s.next())
                for m in range(HB):
                    first(e, s, x, m)
                    if not s.zero:
                        for n in BEHIND[m]:
                            second(e, s.prev(), before, n)

            def four(q, more=True):
                _, x = nc.values_load_multi_w_load_instructions(
                    c.experts[0:1, part_of(q, 1), 0:5], engines=[mybir.EngineType.PE], min_val=0, max_val=NE - 1)
                if isinstance(q, int) and q == 0:
                    turn(e, Step(0, 0))
                    step(Step(0, 0), x[0], None)
                for n in range(1, 5):
                    step(Step(q * 2 + n // 2, n % 2, more or n < 4), x[n], x[n - 1])
                return x[4]
            fours = MT // 4
            four(0)
            with e.Fori(1, fours - 1) as q:
                four(q)
            x = four(fours - 1, False)
            for m in range(HB):
                second(e, Step(MT // 2, 0), x, m)


def combine(nc, c, A, out):
    G = 7
    steps = NT // G
    big, misc = Arena(c.big, 4 * 8192), Arena(c.misc, MISC)
    ys = [big.take(G * TOP * D).rearrange("p (t k d) -> p t k d", t=G, k=TOP) for _ in range(2)]
    b2 = matrix(big.take(G * D), G, D)
    cb = [misc.take(P) for _ in range(2)]
    cbT = [misc.take(P) for _ in range(2)]
    pairs = -(-G // 2)
    S = lambda name: c.sem("combine_" + name)
    s_b2, s_z, s_cb, s_ct, s_cbT, s_b, s_v, s_o, s_st = map(S, (
        "b2", "zero", "cb", "ct", "cbT", "b", "vector", "o", "store"))
    s_y = [S("y0"), S("y1")]
    b_ps = [matrix(c.bank[m], 2, D) for m in range(pairs)]
    ct_ps = [c.bank[pairs], c.bank[pairs + 1]]
    s_g = S("gpsimd")
    MINE = 5
    tiles = lambda s, n, k: part_of(s.i * G + n, k)
    with nc.Block() as block:
        @block.sync
        def _(e):
            def load(s):
                full = G if s.more else G - 1
                e.dma_start(ys[s.u][:, 0:full].rearrange("p t k d -> p t (k d)"),
                            c.y_d[bass.ds(s.i * (TOP * G * P), TOP * full * P), :].rearrange(
                                "(t p k) d -> p t (k d)", p=P, k=TOP)).then_inc(s_y[s.u], 16)
                if not s.more:
                    e.dma_start(ys[s.u][0:TAIL, G - 1:G].rearrange("p t k d -> p t (k d)"),
                                c.y_d[TOP * (N - TAIL):TOP * N, :].rearrange(
                                    "(t p k) d -> p t (k d)", t=1, k=TOP)).then_inc(s_y[s.u], 16)

            def store(s):
                e.wait_ge(s_o, pairs * (s.i + 1))
                e.dma_start(out[bass.ds(s.i * (G * P), G * P), :].rearrange("(t p) d -> p t d", p=P),
                            c.acc3[:, tiles(s, 0, G), :]).then_inc(s_st, 16)

            def both(s):
                store(s)
                load(s.later(2))
            load(Step(0, 0))
            load(Step(0, 1))
            paired(e, steps - 2, both)
            store(Step(steps // 2 - 1, 1))
            e.wait_ge(s_o, pairs * steps)
            e.dma_start(out[N - TAIL - (G - 1) * P:N - TAIL, :].rearrange("(t p) d -> p t d", p=P),
                        c.acc3[:, NT - G:NT - 1, :]).then_inc(s_st, 16)
            e.dma_start(out[N - TAIL:N, :], c.acc3[0:TAIL, NT - 1, :]).then_inc(s_st, 16)
            e.wait_ge(s_st, 16 * (steps + 1))

        @block.scalar
        def _(e):
            def shares(s):
                if not s.fresh:
                    e.wait_ge(s_ct, s.i - 1)
                e.copy(matrix(cb[s.u][:, 0:G * NE], G, NE), c.share[:, tiles(s, 0, G), :]).then_inc(s_cb, 1)
                if not s.fresh:
                    e.wait_ge(s_b, pairs * (s.i - 1))
                e.wait_ge(s_ct, s.i + 1)
                e.copy(cbT[s.u], ct_ps[s.u][:, 0:P]).then_inc(s_cbT, 1)

            e.wait_ge(s_z, 3)
            for t in range(G):
                e.dma_start(b2[t * NE:t * NE + NE, t, :], A["b2"]).then_inc(s_b2, 16)
            paired(e, steps, shares)

        @block.gpsimd
        def _(e):
            g = Chain(e, s_g)

            def add(s):
                e.wait_ge(s_y[s.u], 16 * (s.j + (1 if s.more else 2)))
                k = G - MINE
                a = c.acc3[:, tiles(s, MINE, k), :]
                for n in range(TOP):
                    y = ys[s.u][:, MINE:G, n, :]
                    p = c.prob[n][:, tiles(s, MINE, k)].rearrange("p (t a) -> p t a", a=1)
                    g.link(e.tensor_tensor(y, y, p.to_broadcast([P, k, D]), ALU.mult))
                    g.link(e.tensor_tensor(a, a, y, ALU.add))
            for i in range(steps):
                add(Step(i // 2, i % 2, i < steps - 1))

        @block.vector
        def _(e):
            v = Chain(e, s_v)
            for t in (cb[0], cb[1], b2):
                e.memset(t, 0.0).then_inc(s_z, 1)

            def add(s):
                e.wait_ge(s_y[s.u], 16 * (s.j + (1 if s.more else 2)))
                for k in range(TOP):
                    for n in range(MINE):
                        t = tiles(s, n, 1)
                        a = c.acc3[:, t, :]
                        v.add(e.scalar_tensor_tensor(out=a, in0=ys[s.u][:, n:n + 1, k, :], scalar=c.prob[k][:, t], in1=a,
                                                     op0=ALU.mult, op1=ALU.add))
                    v.sync()
                for m in range(pairs):
                    if m == MINE // 2:
                        e.wait_ge(s_g, 2 * TOP * (s.i + 1))
                    e.wait_ge(s_b, pairs * s.i + m + 1)
                    k = min(2, G - 2 * m)
                    a = c.acc3[:, tiles(s, 2 * m, k), :]
                    e.tensor_tensor(a, b_ps[m][:, 0:k, :], a, ALU.add).then_inc(s_o, 1)
            paired(e, steps, add, v, TOP * MINE)

        @block.tensor
        def _(e):
            e.wait_ge(s_b2, 16 * G)

            def bias(s):
                e.wait_ge(s_cb, s.i + 1)
                if not s.fresh:
                    e.wait_ge(s_cbT, s.i - 1)
                e.transpose(ct_ps[s.u][:, 0:P], cb[s.u], c.ident).then_inc(s_ct, 1)
                e.wait_ge(s_cbT, s.i + 1)
                for n in range(G):
                    if n % 2 == 0 and not s.zero:
                        e.wait_ge(s_o, pairs * (s.i - 1) + n // 2 + 1)
                    l = e.matmul(b_ps[n // 2][:, n % 2, :], cbT[s.u], b2[:, n, :], start=True, stop=True)
                    if n % 2 or n == G - 1:
                        l.then_inc(s_b, 1)
            paired(e, steps, bias)


_INS = ["x", "src", "dst", "edge_weight", "gnn_wT", "gnn_b", "q_wT", "kv_wT", "proj_wT", "proj_b",
        "gate_wT", "gate_b", "w1T", "b1T", "w2T", "b2"]


def kernel(**inputs):
    import numpy as _np
    import concourse.bacc as _bacc
    from concourse import mybir as _mybir
    from concourse.bass_utils import run_bass_kernel_spmd as _run

    a = {k.replace("L0_", ""): _np.asarray(v) for k, v in inputs.items()}
    rows = lambda w: w.reshape(DH, P, -1).transpose(1, 0, 2)
    lay = {"x": a["x"], "src": a["src"], "dst": a["dst"], "edge_weight": a["edge_weight"],
           "gnn_wT": rows(a["gnn_W"].T), "gnn_b": a["gnn_b"].reshape(1, D),
           "q_wT": rows(a["mix_Wq"].T), "kv_wT": rows(a["mix_Wkv"].T),
           "proj_wT": rows(a["mix_Wproj"].T), "proj_b": a["mix_bproj"].reshape(1, D),
           "gate_wT": rows(a["ffn_Wg"].T), "gate_b": a["ffn_bg"].reshape(1, NE),
           "w1T": a["ffn_W1"].transpose(2, 0, 1).reshape(DH, P, NE * H).transpose(1, 0, 2),
           "b1T": a["ffn_b1"].reshape(NE * HB, P).T,
           "w2T": a["ffn_W2"].transpose(2, 0, 1).reshape(HB, P, NE * D).transpose(1, 0, 2),
           "b2": a["ffn_b2"]}
    nc = _bacc.Bacc("TRN2", target_bir_lowering=False, num_devices=1)
    arrays, args = {}, {}
    for name in _INS:
        arrays["in_" + name] = _np.ascontiguousarray(lay[name])
        args[name] = nc.dram_tensor("in_" + name, lay[name].shape, _mybir.dt.from_np(lay[name].dtype),
                                    kind="ExternalInput").ap()
    out = nc.dram_tensor("out0", (N, D), F32, kind="ExternalOutput").ap()
    build(nc, args, out)
    return _run(nc, [arrays], core_ids=[0]).results[0]["out0"]
```
